# Optimizing a Trainium2 kernel written in Bass

```python
import numpy as np
import jax
import jax.numpy as jnp

def _softmax(x, axis=-1):
    return jax.nn.softmax(x, axis=axis)

def _gelu(x):
    return jax.nn.gelu(x, approximate=True)

def _silu(x):
    return jax.nn.silu(x)

def _sigmoid(x):
    return jax.nn.sigmoid(x)

def _layernorm(x, axis=-1, eps=1e-05):
    m = jnp.mean(x, axis=axis, keepdims=True)
    v = jnp.var(x, axis=axis, keepdims=True)
    return (x - m) / jnp.sqrt(v + eps)

def _scatter_add(tgt, idx, src, axis=0):
    return tgt.at[idx].add(src)

def _segment_sum(src, seg, n):
    return jax.ops.segment_sum(src, seg, n)
kernel_name = 'mk_perceiver_d1_seqx_r4_68ec63'

def setup_inputs(seed: int=0):
    np.random.seed(seed)
    _w = jnp.asarray

    def _rec_inputs():
        import jax
        import jax.numpy as jnp
        _rk = jax.random.key(seed)
        x = -0.0002928 + 1 * jax.random.normal(jax.random.fold_in(_rk, 1), (32, 32, 256), jnp.float32)
        _lenS = 32 - jax.random.randint(jax.random.fold_in(_rk, 7), (32,), 0, max(1, 32 // 4) + 1, jnp.int32)
        _lenS2 = 257 - jax.random.randint(jax.random.fold_in(_rk, 8), (32,), 0, max(1, 257 // 4) + 1, jnp.int32)
        _ctx_1024P = jax.random.normal(jax.random.fold_in(_rk, 11), (32, 16, 256), jnp.float32)
        _ctx_1024c = jax.random.dirichlet(jax.random.fold_in(_rk, 511), 0.3 * jnp.ones((16,), jnp.float32), (32, 257))
        _ctx_1024t = jnp.einsum('bsk,bkd->bsd', _ctx_1024c, _ctx_1024P)
        _ctx_1024t = _ctx_1024t * jax.lax.rsqrt(jnp.mean(jnp.square(_ctx_1024t)) + 1e-12) * 0.953939
        ctx_1024 = -1.39393e-06 + 0.999914 * (_ctx_1024t + 0.3 * jax.random.normal(jax.random.fold_in(_rk, 611), (32, 257, 256), jnp.float32))
        _validS = jnp.arange(32)[None, :] < _lenS[:, None]
        _validS2 = jnp.arange(257)[None, :] < _lenS2[:, None]
        _causal = jnp.tril(jnp.ones((32, 32), dtype=bool))
        mask_Bx1x1xS2_if1 = jnp.where(jnp.ones((32, 1, 1, 257), dtype=bool), 1, 0).astype(jnp.int32)
        return (x, ctx_1024, mask_Bx1x1xS2_if1)
    x, ctx_1024, mask_Bx1x1xS2_if1 = _rec_inputs()

    def _L0_xattn_setup():
        import jax, jax.numpy as jnp
        import numpy as np
        N_HEADS = 16
        D_MODEL = 256
        D_K = D_MODEL // N_HEADS
        B, S = (2, 512)
        key = jax.random.key(seed)
        ks = jax.random.split(key, 12)
        sc = 1.0 / np.sqrt(D_MODEL)
        inp = {'query': jax.random.normal(ks[0], (B, S, D_MODEL), jnp.float32), 'key': jax.random.normal(ks[1], (B, S, D_MODEL), jnp.float32), 'value': jax.random.normal(ks[2], (B, S, D_MODEL), jnp.float32), 'mask': jnp.ones((B, 1, 1, S), jnp.int32), 'Wq': jax.random.normal(ks[3], (D_MODEL, D_MODEL), jnp.float32) * sc, 'bq': jnp.zeros((D_MODEL,), jnp.float32), 'Wk': jax.random.normal(ks[4], (D_MODEL, D_MODEL), jnp.float32) * sc, 'bk': jnp.zeros((D_MODEL,), jnp.float32), 'Wv': jax.random.normal(ks[5], (D_MODEL, D_MODEL), jnp.float32) * sc, 'bv': jnp.zeros((D_MODEL,), jnp.float32), 'Wo': jax.random.normal(ks[6], (D_MODEL, D_MODEL), jnp.float32) * sc, 'bo': jnp.zeros((D_MODEL,), jnp.float32)}
        return inp
    _L0_xattn_all = _L0_xattn_setup()
    _L0_xattn_in = {k: v for k, v in _L0_xattn_all.items() if k in ('Wq', 'bq', 'Wk', 'bk', 'Wv', 'bv', 'Wo', 'bo')}
    del _L0_xattn_all

    def _L0_attn_setup():
        import jax, jax.numpy as jnp
        import numpy as np
        B, N, D = (4, 512, 256)
        H = 16
        HD = D // H
        SCALE = 1.0 / HD
        NEG = -10000.0
        THETA = 10000.0

        def _rope(t):
            d, n = (t.shape[-1], t.shape[-2])
            inv_freq = 1.0 / THETA ** (jnp.arange(0, d, 2, dtype=jnp.float32) / d)
            ang = jnp.arange(n, dtype=jnp.float32)[:, None] * inv_freq[None, :]
            cos = jnp.repeat(jnp.cos(ang), 2, axis=-1)
            sin = jnp.repeat(jnp.sin(ang), 2, axis=-1)
            x1, x2 = (t[..., ::2], t[..., 1::2])
            rot = jnp.stack([-x2, x1], axis=-1).reshape(t.shape)
            return t * cos + rot * sin
        key = jax.random.key(seed)
        ks = jax.random.split(key, 6)
        s = (1.0 / D) ** 0.5
        return {'x': jax.random.normal(ks[0], (B, N, D), jnp.float32), 'Wq': jax.random.normal(ks[1], (D, D), jnp.float32) * s, 'Wk': jax.random.normal(ks[2], (D, D), jnp.float32) * s, 'Wv': jax.random.normal(ks[3], (D, D), jnp.float32) * s, 'Wo': jax.random.normal(ks[4], (D, D), jnp.float32) * s, 'bo': jnp.zeros((D,), jnp.float32)}
    _L0_attn_all = _L0_attn_setup()
    _L0_attn_in = {k: v for k, v in _L0_attn_all.items() if k in ('Wq', 'Wk', 'Wv', 'Wo', 'bo')}
    del _L0_attn_all

    def _L0_ffn_setup():
        import jax, jax.numpy as jnp
        import numpy as np
        NUM_EXPERTS = 8
        EXPERT_CAPACITY = 2.0
        key = jax.random.key(seed)
        k1, k2, k3, k4 = jax.random.split(key, 4)
        B, T, C, H, E = (4, 1024, 256, 1024, NUM_EXPERTS)
        x = jax.random.normal(k1, (B, T, C), jnp.float32)
        gate_w = jax.random.normal(k2, (C, E), jnp.float32) * 0.02
        w1 = jax.random.normal(k3, (E, C, H), jnp.float32) * 0.02
        w2 = jax.random.normal(k4, (E, H, C), jnp.float32) * 0.02
        return {'x': x, 'gate_w': gate_w, 'w1': w1, 'w2': w2}
    _L0_ffn_all = _L0_ffn_setup()
    _L0_ffn_in = {k: v for k, v in _L0_ffn_all.items() if k in ('gate_w', 'w1', 'w2')}
    del _L0_ffn_all
    return {'x': x, 'ctx_1024': ctx_1024, 'mask_Bx1x1xS2_if1': mask_Bx1x1xS2_if1, 'L0_xattn_Wq': _L0_xattn_in['Wq'], 'L0_xattn_bq': _L0_xattn_in['bq'], 'L0_xattn_Wk': _L0_xattn_in['Wk'], 'L0_xattn_bk': _L0_xattn_in['bk'], 'L0_xattn_Wv': _L0_xattn_in['Wv'], 'L0_xattn_bv': _L0_xattn_in['bv'], 'L0_xattn_Wo': _L0_xattn_in['Wo'], 'L0_xattn_bo': _L0_xattn_in['bo'], 'L0_attn_Wq': _L0_attn_in['Wq'], 'L0_attn_Wk': _L0_attn_in['Wk'], 'L0_attn_Wv': _L0_attn_in['Wv'], 'L0_attn_Wo': _L0_attn_in['Wo'], 'L0_attn_bo': _L0_attn_in['bo'], 'L0_ffn_gate_w': _L0_ffn_in['gate_w'], 'L0_ffn_w1': _L0_ffn_in['w1'], 'L0_ffn_w2': _L0_ffn_in['w2']}

def reference(x, ctx_1024, mask_Bx1x1xS2_if1, L0_xattn_Wq, L0_xattn_bq, L0_xattn_Wk, L0_xattn_bk, L0_xattn_Wv, L0_xattn_bv, L0_xattn_Wo, L0_xattn_bo, L0_attn_Wq, L0_attn_Wk, L0_attn_Wv, L0_attn_Wo, L0_attn_bo, L0_ffn_gate_w, L0_ffn_w1, L0_ffn_w2):
    import jax
    import jax.numpy as jnp

    def _L0_xattn_ref(query, key, value, mask, Wq, bq, Wk, bk, Wv, bv, Wo, bo):
        import jax, jax.numpy as jnp
        import numpy as np
        N_HEADS = 16
        D_MODEL = 256
        D_K = D_MODEL // N_HEADS
        B, S = (2, 512)
        q = query @ Wq.T + bq
        k = key @ Wk.T + bk
        v = value @ Wv.T + bv

        def split_heads(x):
            b, s, _ = x.shape
            return x.reshape(b, s, N_HEADS, D_K).transpose(0, 2, 1, 3)
        q, k, v = (split_heads(q), split_heads(k), split_heads(v))
        att = jnp.einsum('bhqd,bhkd->bhqk', q, k) / jnp.sqrt(jnp.float32(D_K))
        att = jnp.where(mask == 0, -jnp.inf, att)
        scores = jax.nn.softmax(att, axis=-1)
        out = jnp.einsum('bhqk,bhkd->bhqd', scores, v)
        b = out.shape[0]
        out = out.transpose(0, 2, 1, 3).reshape(b, -1, N_HEADS * D_K)
        return out @ Wo.T + bo

    def _L0_attn_ref(x, Wq, Wk, Wv, Wo, bo):
        import jax, jax.numpy as jnp
        import numpy as np
        B, N, D = (4, 512, 256)
        H = 16
        HD = D // H
        SCALE = 1.0 / HD
        NEG = -10000.0
        THETA = 10000.0

        def _rope(t):
            d, n = (t.shape[-1], t.shape[-2])
            inv_freq = 1.0 / THETA ** (jnp.arange(0, d, 2, dtype=jnp.float32) / d)
            ang = jnp.arange(n, dtype=jnp.float32)[:, None] * inv_freq[None, :]
            cos = jnp.repeat(jnp.cos(ang), 2, axis=-1)
            sin = jnp.repeat(jnp.sin(ang), 2, axis=-1)
            x1, x2 = (t[..., ::2], t[..., 1::2])
            rot = jnp.stack([-x2, x1], axis=-1).reshape(t.shape)
            return t * cos + rot * sin
        b, n, _ = x.shape
        q = (x @ Wq.T).reshape(b, n, H, HD).transpose(0, 2, 1, 3)
        k = (x @ Wk.T).reshape(b, n, H, HD).transpose(0, 2, 1, 3)
        v = (x @ Wv.T).reshape(b, n, H, HD).transpose(0, 2, 1, 3)
        q = _rope(q)
        k = _rope(k)
        i = jnp.arange(n)
        add_mask = jnp.where(i[:, None] >= i[None, :], 0.0, NEG).astype(x.dtype)
        scores = jnp.einsum('bhqd,bhkd->bhqk', q, k) * SCALE + add_mask
        attn = jax.nn.softmax(scores, axis=-1)
        out = jnp.einsum('bhqk,bhkd->bhqd', attn, v)
        out = out.transpose(0, 2, 1, 3).reshape(b, n, H * HD)
        return out @ Wo.T + bo

    def _L0_ffn_ref(x, gate_w, w1, w2):
        import jax, jax.numpy as jnp
        import numpy as np
        NUM_EXPERTS = 8
        EXPERT_CAPACITY = 2.0
        B, T, C = x.shape
        E = gate_w.shape[1]
        cap = int(EXPERT_CAPACITY * T / E)
        scores = jnp.einsum('BTC,CE->BTE', x, gate_w)
        probs = jax.nn.softmax(scores, axis=-1)
        probs_et = jnp.transpose(probs, (0, 2, 1))
        top_p, top_idx = jax.lax.top_k(probs_et, cap)
        xin = jnp.take_along_axis(x[:, None, :, :], top_idx[..., None], axis=2)
        h = jax.nn.gelu(jnp.einsum('BElC,ECH->BElH', xin, w1), approximate=False)
        y = jnp.einsum('BElH,EHC->BElC', h, w2)
        y = y * top_p[..., None]
        b_idx = jnp.arange(B)[:, None, None]
        out = jnp.zeros((B, T, C), x.dtype).at[b_idx, top_idx].add(y)
        return out
    x = x + _L0_xattn_ref(_layernorm(x, axis=-1), ctx_1024, ctx_1024, mask_Bx1x1xS2_if1, L0_xattn_Wq, L0_xattn_bq, L0_xattn_Wk, L0_xattn_bk, L0_xattn_Wv, L0_xattn_bv, L0_xattn_Wo, L0_xattn_bo)
    x = x + _L0_attn_ref(_layernorm(x, axis=-1), L0_attn_Wq, L0_attn_Wk, L0_attn_Wv, L0_attn_Wo, L0_attn_bo)
    x = x + _L0_ffn_ref(_layernorm(x, axis=-1), L0_ffn_gate_w, L0_ffn_w1, L0_ffn_w2)
    return x

_drawn_inputs = setup_inputs


def setup_inputs(seed=0):
    import zlib

    import numpy as np

    out = dict(_drawn_inputs(seed))
    spreads = {'L0_xattn_bq': (0.0, 0.349),
     'L0_xattn_bk': (0.0, 0.8),
     'L0_xattn_bv': (0.0, 0.1),
     'L0_xattn_bo': (0.0, 0.1),
     'L0_attn_bo': (0.0, 0.1)}
    factors = {'L0_ffn_gate_w': 3.151, 'L0_ffn_w1': 2.782, 'L0_ffn_w2': 2.729}
    for name, (base, spread) in spreads.items():
        noise = np.random.default_rng([zlib.crc32(name.encode()), seed]).standard_normal(out[name].shape)
        drawn = base * np.exp(spread * noise) if base else spread * noise
        out[name] = jnp.asarray(drawn.astype(out[name].dtype))
    for name, factor in factors.items():
        out[name] = (out[name] * factor).astype(out[name].dtype)
    return out
```

```python
from contextlib import ExitStack

import concourse.bass as bass
from concourse import mybir
import numpy as np

ALU = mybir.AluOpType
ACT = mybir.ActivationFunctionType
F32 = mybir.dt.float32
BF16 = mybir.dt.bfloat16
I32 = mybir.dt.int32
X = mybir.AxisListType.X

B, S, D = 32, 32, 256
KEYS = 257
H, DK = 16, 16
E, CAP, HID = 8, 8, 1024
EPS = 1e-5
P = 128
BT = P // S
TILES = B // BT
C = D // P
G = 4
HG = H // G
KB = BT * KEYS
KT = (KEYS - 1) // P
PIECES = [(0, 344), (344, 342), (686, 342)]
HC = HID // P
NEG = -10000.0

CONSTS = [("ident", P), ("headmask", 8), ("diag", P), ("expand", HG * DK), ("rep", S), ("cos", DK), ("sin", DK),
          ("causal", S), ("batch_ones", P), ("code", BT * CAP), ("before", S), ("after", S)]
OFF = {}
_o = 0
for _n, _w in CONSTS:
    OFF[_n] = (_o, _o + _w)
    _o += _w
NCONST = _o


def tables():
    p = np.arange(P)
    q = p % S
    a = {}
    a["ident"] = np.eye(P)
    a["headmask"] = (p[:, None] // DK == np.arange(8)[None])
    a["diag"] = ((p[:, None] % 64) // DK == np.arange(P)[None] // S)
    a["expand"] = (p[:, None] // S == np.arange(HG * DK)[None] // DK)
    a["rep"] = (q[:, None] == np.arange(S)[None])
    inv = np.float32(1.0) / np.float32(10000.0) ** (np.arange(0, DK, 2, dtype=np.float32) / np.float32(DK))
    ang = (q.astype(np.float32)[:, None] * inv[None]).astype(np.float32)
    a["cos"] = np.repeat(np.cos(ang), 2, axis=1)
    sign = np.where(np.arange(DK) % 2 == 0, -1.0, 1.0)
    a["sin"] = np.repeat(np.sin(ang), 2, axis=1) * sign
    a["causal"] = np.where(q[:, None] >= np.arange(S)[None], 0.0, NEG)
    a["batch_ones"] = (p[:, None] // S == p[None] // S)
    j = np.arange(BT * CAP)
    a["code"] = np.where(p[:, None] // S == j[None] // CAP, j[None] % CAP, -1)
    a["before"] = (np.arange(S)[None] < q[:, None])
    a["after"] = (np.arange(S)[None] > q[:, None])
    return np.concatenate([np.asarray(a[n], np.float32) for n, _ in CONSTS], axis=1)


class Sig:

    def __init__(self, sem, steps, base=0):
        self.sem, self.n, self.base = sem, len(steps), base
        self.at = {s: k + 1 for k, s in enumerate(steps)}

    def done(self, t, step):
        return t * self.n + (self.base + self.at[step])

    def whole(self, t):
        return t * self.n + self.base


def later(t):
    return not (isinstance(t, int) and t == 0)


def perceiver(nc, a, out):
    ctx = ExitStack()
    with ctx:
        def sb(name, shape, dt=F32):
            return ctx.enter_context(nc.sbuf_tensor(name, shape, dt))

        def bank(name):
            return ctx.enter_context(nc.psum_tensor(name, [P, 512], F32))

        def sem(name):
            return ctx.enter_context(nc.semaphore(name))

        def sig(name, steps, base=0):
            return Sig(sem(name), steps, base)

        cst = sb("cst", [P, NCONST])

        def k_(name):
            return cst[:, OFF[name][0]:OFF[name][1]]

        wq, wk, wv, wo = (sb(n, [P, C, D]) for n in ("wq", "wk", "wv", "wo"))
        wqkv = sb("wqkv", [P, C, 3 * D])
        wo2 = sb("wo2", [P, C, D])
        gate = sb("gate", [P, C, E])
        cols = sb("cols", [P, 3, C])
        bqs = sb("bqs", [P, C])
        bo_b = sb("bo_b", [P, 2, D])
        mask_i = sb("mask_i", [B, KEYS], I32)
        mask_f = sb("mask_f", [B, KEYS])
        mask_b = sb("mask_b", [B, KEYS], BF16)
        row0 = sb("row0", [P, P], BF16)
        mrow = sb("mrow", [P, KB], BF16)
        mhalf = sb("mhalf", [P, TILES])
        eps = sb("eps", [P, TILES])
        x_all = sb("x_all", [P, TILES, D])
        xn1 = sb("xn1", [P, 2, D])
        st1 = sb("st1", [P, TILES, 6])
        mv1 = sb("mv1", [P, TILES, 2])
        ve1 = sb("ve1", [P, TILES])
        rstd1 = sb("rstd1", [P, TILES])
        qT = sb("qT", [P, C, TILES * P])
        ctx_last = sb("ctx_last", [P, C, B])
        vlast = sb("vlast", [P, TILES, C, BT])
        wide = sb("wide", [P, 2 * C * KB])
        ctxT = wide[:, 0:C * KB].rearrange("p (c n) -> p c n", c=C)
        kT = wide[:, C * KB:].rearrange("p (c n) -> p c n", c=C)
        ys = wide[:, 0:TILES * 2 * D].rearrange("p (t g n) -> p t g n", t=TILES, g=2)
        blocks = sb("blocks", [P, 2, C * BT * 8 * S])
        qblk = blocks[:, 0, :].rearrange("p (c b n) -> p c b n", c=C, b=BT)
        kblk = blocks[:, 1, :].rearrange("p (c b n) -> p c b n", c=C, b=BT)
        xT1 = blocks[:, 1, :].rearrange("p (c n) -> p c n", c=C)
        hT = blocks[:].rearrange("p i (j n) -> p i j n", j=HC)
        v = sb("v", [P, BT, KT, D])
        nmax = sb("nmax", [P, H])
        probs = sb("probs", [P, 2, 2, KEYS])
        rsum = sb("rsum", [P, G, BT])
        rinv = sb("rinv", [P, G, BT])
        pT = sb("pT", [P, 2, 2, KT * P])
        masked = sb("masked", [P, 4 * P])
        att_u = sb("att_u", [P, 2, C, 2 * S])
        rep_r = sb("rep_r", [P, G, BT * S])
        rep_p = sb("rep_p", [P, G, BT * S])
        att = sb("att", [P, C, P])
        x1 = sb("x1", [P, D])
        x1b = sb("x1b", [P, D])
        st = sb("st", [P, 2, 6])
        mv = sb("mv", [P, 2, 2])
        ve = sb("ve", [P, 2])
        rstd = sb("rstd", [P, 2])
        x2 = sb("x2", [P, D])
        hold = sb("hold", [P, 1])
        xn = sb("xn", [P, D])
        xT2 = sb("xT2", [P, C, P])
        rot_a = sb("rot_a", [P, 2 * D])
        rot_b = sb("rot_b", [P, 2 * D])
        vz = sb("vz", [P, BT, D])
        qk2 = sb("qk2", [P, 2, C, P])
        sc = sb("sc", [P, H, S])
        mx2 = sb("mx2", [P, H])
        ex = sb("ex", [P, H, S])
        sm2 = sb("sm2", [P, H])
        ri2 = sb("ri2", [P, H])
        pn = sb("pn", [P, H * S])
        pT2 = sb("pT2", [P, H * S])
        masked2 = sb("masked2", [P, 2, 4 * P])
        att2 = sb("att2", [P, C, P])
        xn3 = sb("xn3", [P, D])
        xT3 = sb("xT3", [P, C, P])
        gmx = sb("gmx", [P, 1])
        gex = sb("gex", [P, E])
        gsm = sb("gsm", [P, 1])
        gri = sb("gri", [P, 1])
        gp = sb("gp", [P, E])
        dsp = sb("dsp", [P, E, S])
        cgt = sb("cgt", [P, E, S])
        cge = sb("cge", [P, E, S])
        rank = sb("rank", [P, E])
        sel = sb("sel", [P, E, BT * CAP])
        selw = sb("selw", [P, E, BT * CAP])
        xin = sb("xin", [P, C, E, TILES * BT * CAP])
        selT = sb("selT", [P, TILES, 2, P])
        w1s = [sb(f"w1s{i}", [P, C, HID]) for i in range(2)]
        w2s = [sb(f"w2s{i}", [P, HC, D]) for i in range(2)]
        fin = sb("fin", [P, 2, D])

        sbk = [bank(f"sbk{i}") for i in range(3)]
        ring = [bank(f"ring{i}") for i in range(2)]
        obk = bank("obk")
        mbk = [bank(f"mbk{i}") for i in range(2)]

        s_const, s_w, s_x, s_mask = (sem(n) for n in ("s_const", "s_w", "s_x", "s_mask"))
        s_ctx, s_mrow, s_mst = sem("s_ctx"), sem("s_mrow"), sem("s_mst")
        s_w1, s_w2 = ([sem(f"s_w{j}_{i}") for i in range(2)] for j in (1, 2))
        s_out = [sem(f"s_out{i}") for i in range(2)]
        N_W = 11

        pro = sig("pro", ["mask0", "mask", "mrow0", "row0", "row1", "half", "eps", "bqs", "vz0", "st", "mv"])
        pro_xn = sig("pro_xn", ["xn"])
        pro_xT = sig("pro_xT", ["xT"])
        pro_pool = sig("pro_pool", ["var", "rstd"])
        pro_t = sig("pro_t", ["t"])
        pro_q = sig("pro_q", ["q00", "q01", "q10", "q11"])
        pro_qe = sig("pro_qe", ["q00", "q01", "q10", "q11"])
        pro_vl = sem("pro_vl")
        pro_vle = sem("pro_vle")
        pro_xbo = sig("pro_xbo", ["x"])

        pe_k = sig("pe_k", [f"k{i}" for i in range(6)])
        pe_v = sig("pe_v", [f"v{b}" for b in range(BT)])
        act_k = sig("act_k", [f"k{i}" for i in range(6)])
        dve_v = sig("dve_v", [f"v{b}" for b in range(BT)])
        pool_q = sig("pool_q", [f"q{c}" for c in range(C)])
        pe_s = sig("pe_s", [f"s{i}" for i in range(H)])
        dve_max = sig("dve_max", [f"m{i}" for i in range(H)])
        act_exp = sig("act_exp", [f"e{i}" for i in range(H)])
        pool_last = sig("pool_last", [f"l{i}" for i in range(H)])
        pe_t = sig("pe_t", [f"t{p}" for p in range(8)])
        turned = [sig("dve_t", [f"t{p}" for p in range(0, 8, 2)]), sig("act_t", [f"t{p}" for p in range(1, 8, 2)])]
        pe_o = sig("pe_o", [f"o{p}" for p in range(8)])
        dve_o = sig("dve_o", ["mask0", "sum0", "mask1", "sum1"])
        dve_r = sig("dve_r", ["rinv"])
        pool_e = sig("pool_e", ["rep_r"])
        pe_e = sig("pe_e", ["expanded", "projected"])
        dve_a = sig("dve_a", ["last", "plus", "norm", "att", "x1"])
        dve_s = sig("dve_s", ["stats", "aggr", "xn", "xT", "cos", "sin0", "sin1", "rope", "scaled", "max", "sub",
                              "sum", "rinv", "probs", "turned", "mask0", "mask1", "sum0", "sum1", "x2", "kept"])
        pool_s = sig("pool_s", ["x1b", "var", "rstd", "kblk0", "kblk1"])
        act_s = sig("act_s", ["v0", "v1", "v2", "v3", "qk", "exp"])
        pe_x = sig("pe_x", ["xT", "qk", "v", "qkT", "scores", "pv", "projected"])
        dve_g = sig("dve_g", ["stats", "aggr", "xn", "xT", "max", "rinv", "p", "spread", "gt", "ge", "gt_m",
                              "ge_m", "both", "rank", "sel", "selw", "xin0", "xin1", "selT"])
        pool_g = sig("pool_g", ["var", "rstd"])
        act_g = sig("act_g", ["exp"])
        pe_g = sig("pe_g", ["xT", "logits", "others", "xin0", "xin1", "selT"])
        EQ = 4
        pe_h = sig("pe_h", [f"h{e}{j}" for e in range(EQ) for j in range(HC // 2)])
        act_h = sig("act_h", [f"h{e}{j}" for e in range(EQ) for j in range(HC // 2)])
        pe_y = sig("pe_y", [f"y{e}" for e in range(EQ)])
        dve_y = sig("dve_y", [f"y{e}{q}" for e in range(EQ) for q in range(BT)], base=1)
        pe_f = sig("pe_f", ["f"])
        dve_f = sig("dve_f", ["f"])

        uses = [(act_k, f"k{i}") for i in range(6)] + [(dve_v, "v0")]
        for p in range(9):
            if p % 2 == 0 and p // 2 + 1 < BT:
                uses.append((dve_v, f"v{p // 2 + 1}"))
            if p >= 1:
                uses.append((turned[(p - 1) % 2], f"t{p - 1}"))
        place = {(id(s), n): u for u, (s, n) in enumerate(uses)}

        def ring_bank(s, n):
            return ring[place[(id(s), n)] % 2]

        def ring_read(t, s, n):
            u = place[(id(s), n)]
            last, step = uses[u - 2]
            return (last.sem, last.done(t, step)) if u >= 2 else (last.sem, last.whole(t))

        def over(ap, n, at):
            shape = list(ap.shape)
            ap = ap.unsqueeze(at)
            return ap.broadcast_to(shape[:at] + [n] + shape[at:])

        block = ctx.enter_context(nc.Block())

        def tiles(eng, body):
            body(0, None, None)
            body(1, 0, None)
            with eng.Fori(2, TILES) as t:
                body(t, t - 1, t - 2)
            body(None, TILES - 1, TILES - 2)
            body(None, None, TILES - 1)

        @block.sync
        def _(sp):
            sp.dma_start(cst[:], a["consts"]).then_inc(s_const, 16)
            sp.dma_start(mask_i[:], a["mask"]).then_inc(s_mask, 16)
            sp.dma_start(x_all[:], a["x"].rearrange("(t p) d -> p t d", p=P)).then_inc(s_x, 16)
            for dst, n in ((wq, "wq"), (wk, "wk"), (wv, "wv"), (wo, "wo"), (wqkv, "wqkv"), (wo2, "wo2"), (gate, "gate")):
                sp.dma_start(dst[:], a[n].rearrange("(c p) n -> p c n", p=P)).then_inc(s_w, 16)
            sp.dma_start(ctx_last[:], a["ctx_last"].rearrange("(c p) n -> p c n", p=P)).then_inc(s_w, 16)
            sp.dma_start(cols[:], a["cols"].rearrange("p (j c) -> p j c", c=C)).then_inc(s_w, 16)
            for j in range(2):
                sp.dma_start(bo_b[:, j, :], a["bo"][j].partition_broadcast(P)).then_inc(s_w, 16)
            ctx_d = a["ctxT"].rearrange("t (c p) n -> t p c n", p=P)

            def load_tile(t):
                if later(t):
                    sp.wait_ge(pe_v.sem, pe_v.whole(t))
                src = ctx_d[t] if isinstance(t, int) else ctx_d[bass.ds(t, 1)].rearrange("t p c n -> (t p) c n")
                sp.dma_start(ctxT, src).then_inc(s_ctx, 16)
                if later(t):
                    sp.wait_ge(pe_s.sem, pe_s.whole(t))
                sp.dma_start(mrow[0:1, :], terms[bass.ds(t, 1), :]).then_inc(s_mrow, 16)

            def load_expert(e):
                w1_d, w2_d = (a[n].rearrange("e (c p) n -> e p c n", p=P) for n in ("w1", "w2"))
                if e >= 2:
                    sp.wait_ge(pe_h.sem, (e - 1) * HC // 2)
                sp.dma_start(w1s[e % 2][:], w1_d[e]).then_inc(s_w1[e % 2], 16)
                if e >= 2:
                    sp.wait_ge(pe_y.sem, e - 1)
                sp.dma_start(w2s[e % 2][:], w2_d[e]).then_inc(s_w2[e % 2], 16)

            terms = a["mask_terms"].rearrange("(t b) k -> t (b k)", b=BT)
            sp.wait_ge(pro.sem, pro.done(0, "mask"))
            sp.dma_start(a["mask_terms"], mask_b[:]).then_inc(s_mst, 16)
            sp.wait_ge(s_mst, 16)
            sp.wait_ge(pro.sem, pro.done(0, "mrow0"))
            load_tile(0)
            load_expert(0)
            load_expert(1)
            with sp.Fori(1, TILES) as t:
                load_tile(t)
            for e in range(2, E):
                load_expert(e)
            for t in range(TILES):
                sp.wait_ge(dve_f.sem, dve_f.done(t, "f"))
                sp.dma_start(out[t * P:(t + 1) * P, :], fin[:, t % 2, :]).then_inc(s_out[t % 2], 16)
            for i in range(2):
                sp.wait_ge(s_out[i], 16 * TILES // 2)

        @block.tensor
        def _(pe):
            mm = pe.matmul
            ident = k_("ident")
            pe.wait_ge(s_const, 16)
            pe.wait_ge(s_w, 16 * N_W)
            for c in range(C):
                for j in range(C):
                    m = mm(ring[0][:, c * B:(c + 1) * B], wv[:, j, c * P:(c + 1) * P], ctx_last[:, j, :],
                           start=(j == 0), stop=(j == C - 1))
            m.then_inc(pro_vl, 1)
            for t in range(TILES):
                pe.wait_ge(pro_xn.sem, pro_xn.done(t, "xn"))
                if t >= 2:
                    pe.wait_ge(pro_xT.sem, pro_xT.done(t - 2, "xT"))
                for c in range(C):
                    m = pe.transpose(mbk[t % 2][:, c * P:(c + 1) * P], xn1[:, t % 2, c * P:(c + 1) * P], ident)
                m.then_inc(pro_t.sem, 1)
                if t % 4 == 3:
                    n = t // 4
                    pe.wait_ge(pro_xT.sem, pro_xT.done(t, "xT"))
                    for c in range(C):
                        if n:
                            pe.wait_ge(pro_qe.sem, pro_qe.done(0, f"q{n - 1}{c}"))
                        for j in range(C):
                            m = mm(sbk[c][:], wq[:, j, c * P:(c + 1) * P], xT1[:, j, n * 512:(n + 1) * 512],
                                   start=(j == 0), stop=(j == C - 1))
                        m.then_inc(pro_q.sem, 1)
            pe.wait_ge(pro_vle, 1)
            pe.wait_ge(pro_qe.sem, pro_qe.done(0, "q11"))
            pe.wait_ge(pro_xT.sem, pro_xT.done(TILES - 1, "xT"))
            pe.wait_ge(pro.sem, pro.done(0, "row1"))

            def keys(t, i):
                if later(t) or i >= 2:
                    pe.wait_ge(*ring_read(t, act_k, f"k{i}"))
                c, (o, n) = i // 3, PIECES[i % 3]
                for j in range(C):
                    m = mm(ring_bank(act_k, f"k{i}")[:, 0:n], wk[:, j, c * P:(c + 1) * P], ctxT[:, j, o:o + n],
                           start=(j == 0), stop=(j == C - 1))
                m.then_inc(pe_k.sem, 1)

            def values(t, b):
                pe.wait_ge(*ring_read(t, dve_v, f"v{b}"))
                for kt in range(KT):
                    o = b * KEYS + kt * P
                    for j in range(C):
                        m = mm(ring_bank(dve_v, f"v{b}")[:, kt * D:(kt + 1) * D], ctxT[:, j, o:o + P], wv[:, j, :],
                               start=(j == 0), stop=(j == C - 1))
                m.then_inc(pe_v.sem, 1)

            def scores(t, i):
                b, g = i // G, i % G
                if i >= 3:
                    pe.wait_ge(act_exp.sem, act_exp.done(t, f"e{i - 3}"))
                else:
                    if later(t):
                        pe.wait_ge(act_exp.sem, act_exp.whole(t))
                o, c = sbk[i % 3][:, 0:KEYS], g // 2
                mm(o, row0[:], mrow[:, b * KEYS:(b + 1) * KEYS], start=True, stop=False)
                mm(o, qblk[:, c, b, (g % 2) * P:(g % 2 + 1) * P], kT[:, c, b * KEYS:(b + 1) * KEYS],
                   start=False, stop=True).then_inc(pe_s.sem, 1)

            def turn(t, p):
                name = f"t{p}"
                pe.wait_ge(*ring_read(t, turned[p % 2], name))
                pe.wait_ge(act_exp.sem, act_exp.done(t, f"e{2 * p + 1}"))
                for gg in range(2):
                    for kt in range(KT):
                        o = (gg * KT + kt) * P
                        m = pe.transpose(ring_bank(turned[p % 2], name)[:, o:o + P],
                                         probs[:, p % 2, gg, kt * P:(kt + 1) * P], ident)
                m.then_inc(pe_t.sem, 1)

            def attend(t, p):
                b, c = p // 2, p % 2
                if p == 0:
                    if later(t):
                        pe.wait_ge(dve_a.sem, dve_a.whole(t))
                if p == 4:
                    pe.wait_ge(dve_o.sem, dve_o.done(t, "mask0"))
                pe.wait_ge(turned[p % 2].sem, turned[p % 2].done(t, f"t{p}"))
                pe.wait_ge(dve_v.sem, dve_v.done(t, f"v{b}"))
                for gg in range(2):
                    g = 2 * c + gg
                    for kt in range(KT):
                        m = mm(obk[64 * gg:64 * gg + 64, c * 256 + (b % 2) * P:c * 256 + (b % 2 + 1) * P],
                               v[:, b, kt, g * 64:(g + 1) * 64], pT[:, p % 2, gg, kt * P:(kt + 1) * P],
                               start=(kt == 0), stop=(kt == KT - 1))
                m.then_inc(pe_o.sem, 1)

            def expand(t):
                pe.wait_ge(pool_e.sem, pool_e.done(t, "rep_r"))
                pe.wait_ge(pool_last.sem, pool_last.done(t, f"l{H - 1}"))
                pe.wait_ge(dve_o.sem, dve_o.done(t, "mask1"))
                for k, r in enumerate((rep_r, rep_p)):
                    for g in range(G):
                        o = k * 256 + (g // 2) * P
                        m = mm(obk[64 * (g % 2):64 * (g % 2) + 64, o:o + P], k_("expand"), r[:, g, :],
                               start=True, stop=True)
                m.then_inc(pe_e.sem, 1)

            def project(t):
                pe.wait_ge(dve_a.sem, dve_a.done(t, "att"))
                for j in range(C):
                    m = mm(obk[:, 0:D], att[:, j, :], wo[:, j, :], start=(j == 0), stop=(j == C - 1))
                m.then_inc(pe_e.sem, 1)

            def self_xT(u):
                pe.wait_ge(dve_s.sem, dve_s.done(u, "xn"))
                for c in range(C):
                    m = pe.transpose(mbk[1][:, c * P:(c + 1) * P], xn[:, c * P:(c + 1) * P], ident)
                m.then_inc(pe_x.sem, 1)

            def self_qkv(u):
                pe.wait_ge(dve_s.sem, dve_s.done(u, "xT"))
                for o, n, bk in ((0, 512, mbk[0]), (512, D, mbk[1])):
                    for j in range(C):
                        m = mm(bk[:, 0:n], xT2[:, j, :], wqkv[:, j, o:o + n], start=(j == 0), stop=(j == C - 1))
                    m.then_inc(pe_x.sem, 1)

            def self_qkT(u):
                pe.wait_ge(dve_s.sem, dve_s.done(u, "rope"))
                for j in range(4):
                    m = pe.transpose(mbk[0][:, j * P:(j + 1) * P], rot_a[:, j * P:(j + 1) * P], ident)
                m.then_inc(pe_x.sem, 1)

            def self_scores(u):
                pe.wait_ge(act_s.sem, act_s.done(u, "qk"))
                pe.wait_ge(pool_s.sem, pool_s.done(u, "kblk1"))
                for b in range(BT):
                    for c in range(C):
                        m = mm(mbk[0][S * b:S * b + S, c * 256:(c + 1) * 256], qk2[:, 0, c, S * b:S * b + S],
                               kblk[:, c, b, :], start=True, stop=True)
                m.then_inc(pe_x.sem, 1)

            def self_attend(u):
                pe.wait_ge(dve_s.sem, dve_s.done(u, "turned"))
                pe.wait_ge(act_s.sem, act_s.done(u, "v3"))
                for g in range(G):
                    for b in range(BT):
                        m = mm(mbk[g // 2][64 * (g % 2):64 * (g % 2) + 64, b * P:(b + 1) * P],
                               vz[:, b, g * 64:(g + 1) * 64], pT2[:, g * P:(g + 1) * P], start=True, stop=True)
                m.then_inc(pe_x.sem, 1)

            def self_project(u):
                pe.wait_ge(dve_s.sem, dve_s.done(u, "sum1"))
                for j in range(C):
                    m = mm(mbk[0][:, 0:D], att2[:, j, :], wo2[:, j, :], start=(j == 0), stop=(j == C - 1))
                m.then_inc(pe_x.sem, 1)

            def route_xT(w):
                pe.wait_ge(dve_g.sem, dve_g.done(w, "xn"))
                for c in range(C):
                    m = pe.transpose(mbk[0][:, c * P:(c + 1) * P], xn3[:, c * P:(c + 1) * P], ident)
                m.then_inc(pe_g.sem, 1)

            def route_logits(u, w):
                if u is not None:
                    pe.wait_ge(act_s.sem, act_s.done(u, "v3"))
                pe.wait_ge(dve_g.sem, dve_g.done(w, "xT"))
                for j in range(C):
                    m = mm(mbk[1][:, 0:E], xT3[:, j, :], gate[:, j, :], start=(j == 0), stop=(j == C - 1))
                m.then_inc(pe_g.sem, 1)

            def route_others(w):
                pe.wait_ge(dve_g.sem, dve_g.done(w, "spread"))
                mm(mbk[1][:, 0:E * S], k_("batch_ones"), dsp[:].rearrange("p e s -> p (e s)"),
                   start=True, stop=True).then_inc(pe_g.sem, 1)

            def route_gather(u, w):
                pe.wait_ge(dve_g.sem, dve_g.done(w, "selw"))
                for c in range(C):
                    mm(mbk[1][:, c * 256:(c + 1) * 256], xn3[:, c * P:(c + 1) * P],
                       sel[:].rearrange("p e s -> p (e s)"), start=True, stop=True).then_inc(pe_g.sem, 1)
                if u is not None:
                    pe.wait_ge(dve_s.sem, dve_s.done(u, "scaled"))
                flat = selw[:].rearrange("p e s -> p (e s)")
                for k in range(2):
                    m = pe.transpose(mbk[0][:, k * P:(k + 1) * P], flat[:, k * P:(k + 1) * P], ident)
                m.then_inc(pe_g.sem, 1)

            def body(t, u, w):
                if t is not None:
                    pe.wait_ge(s_ctx, (t + 1) * 16)
                    keys(t, 0)
                if u is not None:
                    attend(u, 7)
                if t is not None:
                    keys(t, 1)
                if w is not None:
                    route_xT(w)
                if t is not None:
                    keys(t, 2)
                if u is not None:
                    expand(u)
                if t is not None:
                    keys(t, 3)
                    keys(t, 4)
                if u is not None:
                    project(u)
                if t is not None:
                    keys(t, 5)
                    values(t, 0)
                    pe.wait_ge(s_mrow, (t + 1) * 16)
                    pe.wait_ge(pool_q.sem, pool_q.done(t, f"q{C - 1}"))
                    pe.wait_ge(act_k.sem, act_k.done(t, "k5"))
                for p in range(9):
                    if t is not None:
                        if p < 8:
                            scores(t, 2 * p)
                            scores(t, 2 * p + 1)
                            if p % 2 == 0 and p // 2 + 1 < BT:
                                values(t, p // 2 + 1)
                        if p >= 1:
                            turn(t, p - 1)
                        if p >= 2:
                            attend(t, p - 2)
                    if u is not None and p == 0:
                        self_xT(u)
                    if u is not None and p == 1:
                        if w is not None:
                            pe.wait_ge(dve_g.sem, dve_g.done(w, "xT"))
                        self_qkv(u)
                    if w is not None and p == 2:
                        route_logits(u, w)
                    if u is not None and p == 3:
                        self_qkT(u)
                    if w is not None and p == 4:
                        route_others(w)
                    if u is not None and p == 4:
                        self_scores(u)
                    if w is not None and p == 5:
                        route_gather(u, w)
                    if u is not None and p == 7:
                        if w is not None:
                            pe.wait_ge(dve_g.sem, dve_g.done(w, "selT"))
                        self_attend(u)
                    if u is not None and p == 8:
                        self_project(u)

            tiles(pe, body)

            hbk = [sbk[0], sbk[1], sbk[2], ring[0]]
            pe.wait_ge(dve_g.sem, dve_g.done(TILES - 1, "selT"))

            def hidden(r, k, e):
                for j in range(HC // 2):
                    if k:
                        pe.wait_ge(act_h.sem, act_h.done(r, f"h{k - 1}{j}"))
                    for jj in range(2):
                        for c in range(C):
                            o = (2 * j + jj) * P
                            m = mm(hbk[j][:, jj * 256:(jj + 1) * 256], w1s[k % 2][:, c, o:o + P],
                                   xin[:, c, e, :] if isinstance(e, int) else
                                   xin[:, c, bass.ds(e, 1), :].rearrange("p e n -> p (e n)"),
                                   start=(c == 0), stop=(c == C - 1))
                    m.then_inc(pe_h.sem, 1)

            def result(r, k):
                pe.wait_ge(s_w2[k % 2], r * 32 + 16 * (k // 2 + 1))
                pe.wait_ge(act_h.sem, act_h.done(r, f"h{k}{HC // 2 - 1}"))
                if k >= 2:
                    pe.wait_ge(dve_y.sem, dve_y.done(r, f"y{k - 2}{BT - 1}"))
                else:
                    if later(r):
                        pe.wait_ge(dve_y.sem, dve_y.whole(r))
                for half in range(2):
                    for j in range(HC):
                        m = mm(mbk[k % 2][:, half * D:(half + 1) * D], hT[:, k % 2, j, half * P:(half + 1) * P],
                               w2s[k % 2][:, j, :], start=(j == 0), stop=(j == HC - 1))
                m.then_inc(pe_y.sem, 1)

            def experts(r):
                for k in range(EQ):
                    pe.wait_ge(s_w1[k % 2], r * 32 + 16 * (k // 2 + 1))
                    hidden(r, k, r * EQ + k)
                    if k:
                        result(r, k - 1)
                result(r, EQ - 1)

            with pe.Fori(0, E // EQ) as r:
                experts(r)

            for t in range(TILES):
                pe.wait_ge(dve_y.sem, dve_y.done(1, f"y{EQ - 1}{BT - 1}"))
                if t >= 2:
                    pe.wait_ge(dve_f.sem, dve_f.done(t - 2, "f"))
                for r in range(2):
                    m = mm(mbk[t % 2][:, 0:D], selT[:, t, r, :], ys[:, t, r, :], start=(r == 0), stop=(r == 1))
                m.then_inc(pe_f.sem, 1)

        @block.scalar
        def _(act):
            A = act.activation
            act.wait_ge(s_w, 16 * N_W)
            act.wait_ge(pro.sem, pro.done(0, "bqs"))
            for n in range(2):
                for c in range(C):
                    act.wait_ge(pro_q.sem, pro_q.done(0, f"q{n}{c}"))
                    A(qT[:, c, n * 512:(n + 1) * 512], sbk[c][:], ACT.Identity, bias=bqs[:, c:c + 1],
                      scale=0.25).then_inc(pro_qe.sem, 1)

            def keys(t, i):
                act.wait_ge(pe_k.sem, pe_k.done(t, f"k{i}"))
                c, (o, n) = i // 3, PIECES[i % 3]
                A(kT[:, c, o:o + n], ring_bank(act_k, f"k{i}")[:, 0:n], ACT.Identity,
                  bias=cols[:, 1, c:c + 1]).then_inc(act_k.sem, 1)

            def exps(t, i):
                b, g, p = i // G, i % G, i // 2
                act.wait_ge(dve_max.sem, dve_max.done(t, f"m{i}"))
                if i % 2 == 0:
                    if p >= 2:
                        act.wait_ge(pe_t.sem, pe_t.done(t, f"t{p - 2}"))
                        act.wait_ge(pool_last.sem, pool_last.done(t, f"l{2 * p - 3}"))
                    else:
                        if later(t):
                            act.wait_ge(pe_t.sem, pe_t.whole(t))
                        if later(t):
                            act.wait_ge(pool_last.sem, pool_last.whole(t))
                if i == 0:
                    if later(t):
                        act.wait_ge(dve_r.sem, dve_r.whole(t))
                A(probs[:, p % 2, i % 2, :], sbk[i % 3][:, 0:KEYS], ACT.Exp, bias=nmax[:, i:i + 1],
                  accum_out=rsum[:, g, b:b + 1]).then_inc(act_exp.sem, 1)

            def turn(t, p):
                act.wait_ge(pe_t.sem, pe_t.done(t, f"t{p}"))
                if p >= 2:
                    act.wait_ge(pe_o.sem, pe_o.done(t, f"o{p - 2}"))
                else:
                    if later(t):
                        act.wait_ge(pe_o.sem, pe_o.whole(t))
                A(pT[:, p % 2].rearrange("p g n -> p (g n)"), ring_bank(turned[1], f"t{p}")[:], ACT.Copy
                  ).then_inc(turned[1].sem, 1)

            def self_v(u):
                act.wait_ge(pe_x.sem, pe_x.done(u, "v"))
                for b in range(BT):
                    A(vz[S * b:S * b + S, b, :], mbk[1][S * b:S * b + S, 0:D], ACT.Copy).then_inc(act_s.sem, 1)

            def self_qk(u):
                act.wait_ge(pe_x.sem, pe_x.done(u, "qkT"))
                A(qk2[:].rearrange("p k c n -> p (k c n)"), mbk[0][:], ACT.Copy).then_inc(act_s.sem, 1)

            def self_exp(u):
                act.wait_ge(dve_s.sem, dve_s.done(u, "sub"))
                A(ex[:], sc[:], ACT.Exp).then_inc(act_s.sem, 1)

            def body(t, u, w):
                if t is not None:
                    for i in range(6):
                        keys(t, i)
                for p in range(9):
                    if t is not None:
                        if p < 8:
                            exps(t, 2 * p)
                            exps(t, 2 * p + 1)
                        if p >= 1 and p % 2 == 0:
                            turn(t, p - 1)
                    if u is not None and p == 2:
                        self_v(u)
                    if w is not None and p == 3:
                        act.wait_ge(dve_g.sem, dve_g.done(w, "max"))
                        A(gex[:], mbk[1][:, 0:E], ACT.Exp, bias=gmx[:, 0:1],
                          accum_out=gsm[:, 0:1]).then_inc(act_g.sem, 1)
                    if u is not None and p == 4:
                        self_qk(u)
                    if u is not None and p == 6:
                        self_exp(u)

            tiles(act, body)

            hbk = [sbk[0], sbk[1], sbk[2], ring[0]]

            def experts(r):
                for k in range(EQ):
                    for j in range(HC // 2):
                        act.wait_ge(pe_h.sem, pe_h.done(r, f"h{k}{j}"))
                        A(hT[:, k % 2, 2 * j:2 * j + 2, :].rearrange("p j n -> p (j n)"), hbk[j][:], ACT.Gelu
                          ).then_inc(act_h.sem, 1)

            with act.Fori(0, E // EQ) as r:
                experts(r)

        @block.gpsimd
        def _(pool):
            pool.wait_ge(pro.sem, pro.done(0, "mv"))
            pool.wait_ge(pro.sem, pro.done(0, "half"))
            pool.tensor_tensor(ve1[:], mv1[:, :, 1], eps[:], ALU.add).then_inc(pro_pool.sem, 1)
            pool.wait_ge(pro_pool.sem, pro_pool.done(0, "var"))
            pool.tensor_tensor(rstd1[:], ve1[:], mhalf[:], ALU.pow).then_inc(pro_pool.sem, 1)
            pool.wait_ge(s_const, 16)
            pool.wait_ge(s_w, 16 * N_W)
            pool.wait_ge(pro_qe.sem, pro_qe.done(0, "q11"))

            def block_diagonal(dst, src, sig):
                pool.tensor_tensor(dst.rearrange("p b (h q) -> p b h q", h=8),
                                   over(src.rearrange("p (b q) -> p b q", b=BT), 8, 2),
                                   over(over(k_("headmask"), BT, 1), S, 3), ALU.mult).then_inc(sig.sem, 1)

            def queries(t):
                if later(t):
                    pool.wait_ge(pe_s.sem, pe_s.whole(t))
                for c in range(C):
                    src = qT[:, c, bass.ds(t * P, P)]
                    block_diagonal(qblk[:, c], src, pool_q)

            def last(t, i):
                b, g, p = i // G, i % G, i // 2
                pool.wait_ge(act_exp.sem, act_exp.done(t, f"e{i}"))
                if i == 0:
                    if later(t):
                        pool.wait_ge(pe_e.sem, pe_e.whole(t))
                pool.tensor_tensor(rep_p[:, g, b * S:(b + 1) * S], k_("rep"),
                                   probs[:, p % 2, i % 2, KEYS - 1:KEYS].broadcast_to([P, S]), ALU.mult
                                   ).then_inc(pool_last.sem, 1)

            def repeat(t):
                pool.wait_ge(dve_r.sem, dve_r.done(t, "rinv"))
                pool.tensor_tensor(rep_r[:].rearrange("p g (b q) -> p (g b) q", b=BT), over(k_("rep"), G * BT, 1),
                                   over(rinv[:].rearrange("p g b -> p (g b)"), S, 2), ALU.mult
                                   ).then_inc(pool_e.sem, 1)

            def body(t, u, w):
                if u is not None:
                    repeat(u)
                if w is not None:
                    pool.wait_ge(dve_g.sem, dve_g.done(w, "aggr"))
                    pool.tensor_tensor(ve[:, 1:2], mv[:, 1, 1:2], eps[:, 0:1], ALU.add).then_inc(pool_g.sem, 1)
                    pool.wait_ge(pool_g.sem, pool_g.done(w, "var"))
                    pool.tensor_tensor(rstd[:, 1:2], ve[:, 1:2], mhalf[:, 0:1], ALU.pow).then_inc(pool_g.sem, 1)
                if t is not None:
                    queries(t)
                if u is not None:
                    pool.wait_ge(dve_a.sem, dve_a.done(u, "x1"))
                    pool.tensor_tensor(x1b[:], x1[:], bo_b[:, 1, :], ALU.add).then_inc(pool_s.sem, 1)
                    pool.wait_ge(dve_s.sem, dve_s.done(u, "aggr"))
                    pool.tensor_tensor(ve[:, 0:1], mv[:, 0, 1:2], eps[:, 0:1], ALU.add).then_inc(pool_s.sem, 1)
                    pool.wait_ge(pool_s.sem, pool_s.done(u, "var"))
                    pool.tensor_tensor(rstd[:, 0:1], ve[:, 0:1], mhalf[:, 0:1], ALU.pow).then_inc(pool_s.sem, 1)
                for p in range(8):
                    if t is not None:
                        last(t, 2 * p)
                        last(t, 2 * p + 1)
                    if u is not None and p == 4:
                        pool.wait_ge(act_s.sem, act_s.done(u, "qk"))
                        for c in range(C):
                            block_diagonal(kblk[:, c], qk2[:, 1, c, :], pool_s)

            tiles(pool, body)

        @block.vector
        def _(dve):
            def step(ins, sig):
                ins.then_inc(sig.sem, 1)

            TT, TS, RED = dve.tensor_tensor, dve.tensor_scalar, dve.tensor_reduce
            dve.wait_ge(s_mask, 16)
            TS(mask_f[:], mask_i[:], 0.0, -3e38, ALU.is_equal, ALU.mult).then_inc(pro.sem, 1)
            dve.wait_ge(pro.sem, pro.done(0, "mask0"))
            TS(mask_b[:], mask_f[:], 4.0, None, ALU.mult).then_inc(pro.sem, 1)
            dve.memset(mrow[:], 0.0).then_inc(pro.sem, 1)
            dve.memset(row0[:], 0.0).then_inc(pro.sem, 1)
            dve.wait_ge(pro.sem, pro.done(0, "row0"))
            dve.memset(row0[0:1, :], 1.0).then_inc(pro.sem, 1)
            dve.memset(mhalf[:], -0.5).then_inc(pro.sem, 1)
            dve.memset(eps[:], EPS).then_inc(pro.sem, 1)
            dve.wait_ge(s_w, 16 * N_W)
            TS(bqs[:], cols[:, 0, :], 0.25, None, ALU.mult).then_inc(pro.sem, 1)
            dve.memset(vz[:], 0.0).then_inc(pro.sem, 1)
            dve.wait_ge(s_x, 16)
            for t in range(TILES):
                i = dve.bn_stats(st1[:, t, :], x_all[:, t, :])
            i.then_inc(pro.sem, 1)
            dve.wait_ge(pro.sem, pro.done(0, "st"))
            for t in range(TILES):
                i = dve.bn_aggr(mv1[:, t, :], st1[:, t, :])
            i.then_inc(pro.sem, 1)
            dve.wait_ge(pro.sem, pro.done(0, "mv"))
            dve.wait_ge(pro_pool.sem, pro_pool.done(0, "rstd"))
            dve.wait_ge(s_const, 16)

            def first_xT(t):
                dve.wait_ge(pro_t.sem, pro_t.done(t, "t"))
                dve.tensor_copy(xT1[:, :, t * P:(t + 1) * P],
                                mbk[t % 2][:, 0:D].rearrange("p (c n) -> p c n", c=C)).then_inc(pro_xT.sem, 1)

            for t in range(TILES):
                if t >= 2:
                    dve.wait_ge(pro_t.sem, pro_t.done(t - 2, "t"))
                TS(xn1[:, t % 2, :], x_all[:, t, :], mv1[:, t, 0:1], rstd1[:, t:t + 1], ALU.subtract, ALU.mult
                   ).then_inc(pro_xn.sem, 1)
                if t:
                    first_xT(t - 1)
            first_xT(TILES - 1)
            dve.wait_ge(pro_vl, 1)
            dve.tensor_copy(vlast[:].rearrange("p t c b -> p c t b"),
                            ring[0][:, 0:C * B].rearrange("p (c t b) -> p c t b", c=C, b=BT)).then_inc(pro_vle, 1)
            dve.wait_ge(pro_xn.sem, pro_xn.done(TILES - 1, "xn"))
            for t in range(TILES):
                TT(x_all[:, t, :], x_all[:, t, :], bo_b[:, 0, :], ALU.add).then_inc(pro_xbo.sem, 1)
            dve.wait_ge(pro_xbo.sem, pro_xbo.done(TILES - 1, "x"))
            dve.wait_ge(pro_vle, 1)
            diag = over(k_("diag"), 4, 1)

            def values(t, b):
                dve.wait_ge(pe_v.sem, pe_v.done(t, f"v{b}"))
                dve.tensor_copy(v[:, b].rearrange("p k n -> p (k n)"), ring_bank(dve_v, f"v{b}")[:]
                                ).then_inc(dve_v.sem, 1)

            def maxima(t, i):
                dve.wait_ge(pe_s.sem, pe_s.done(t, f"s{i}"))
                RED(nmax[:, i:i + 1], sbk[i % 3][:, 0:KEYS], X, ALU.max, negate=True).then_inc(dve_max.sem, 1)

            def turn(t, p):
                dve.wait_ge(pe_t.sem, pe_t.done(t, f"t{p}"))
                if p >= 2:
                    dve.wait_ge(pe_o.sem, pe_o.done(t, f"o{p - 2}"))
                else:
                    if later(t):
                        dve.wait_ge(pe_o.sem, pe_o.whole(t))
                dve.tensor_copy(pT[:, p % 2].rearrange("p g n -> p (g n)"), ring_bank(turned[0], f"t{p}")[:]
                                ).then_inc(turned[0].sem, 1)

            def heads(t, half):
                if half:
                    dve.wait_ge(dve_o.sem, dve_o.done(t, "sum0"))
                else:
                    if later(t):
                        dve.wait_ge(dve_a.sem, dve_a.whole(t))
                dve.wait_ge(pe_o.sem, pe_o.done(t, f"o{4 * half + 3}"))
                TT(masked[:].rearrange("p (m n) -> p m n", m=4), obk[:].rearrange("p (m n) -> p m n", m=4), diag,
                   ALU.mult).then_inc(dve_o.sem, 1)
                dve.wait_ge(dve_o.sem, dve_o.done(t, f"mask{half}"))
                RED(att_u[:, half].rearrange("p c (b q) -> p (c b) q", b=2),
                    masked[:].rearrange("p (m h q) -> p m q h", m=4, h=HG), X, ALU.add).then_inc(dve_o.sem, 1)

            def cross_att(t):
                n = 2 * P
                m8 = masked[:, 0:n].rearrange("p (cb q) -> p cb q", q=S)
                dve.wait_ge(dve_o.sem, dve_o.done(t, "sum1"))
                dve.wait_ge(pe_e.sem, pe_e.done(t, "expanded"))
                TT(m8, obk[:, n:2 * n].rearrange("p (cb q) -> p cb q", q=S),
                   over(vlast[:, t].rearrange("p c b -> p (c b)") if isinstance(t, int) else
                        vlast[:, bass.ds(t, 1)].rearrange("p t c b -> p (t c b)"), S, 2), ALU.mult).then_inc(dve_a.sem, 1)
                dve.wait_ge(dve_a.sem, dve_a.done(t, "last"))
                m4 = masked[:, 0:n].rearrange("p (c h n) -> p c h n", c=C, h=2)
                TT(m4, m4, att_u[:].rearrange("p h c n -> p c h n"), ALU.add).then_inc(dve_a.sem, 1)
                dve.wait_ge(dve_a.sem, dve_a.done(t, "plus"))
                TT(masked[:, 0:n], obk[:, 0:n], masked[:, 0:n], ALU.mult).then_inc(dve_a.sem, 1)
                dve.wait_ge(dve_a.sem, dve_a.done(t, "norm"))
                TT(att[:], masked[:, 0:n].rearrange("p (c n) -> p c n", c=C), over(cols[:, 2, :], P, 2), ALU.add
                   ).then_inc(dve_a.sem, 1)

            def cross_x1(t):
                dve.wait_ge(pe_e.sem, pe_e.done(t, "projected"))
                TT(x1[:], obk[:, 0:D], x_all[:, t, :] if isinstance(t, int) else
                   x_all[:, bass.ds(t, 1), :].rearrange("p t n -> p (t n)"), ALU.add).then_inc(dve_a.sem, 1)

            def norm(sig, t, src, made, at, dst, k, pool_sig):
                dve.wait_ge(made, at)
                dve.bn_stats(st[:, k, :], src).then_inc(sig.sem, 1)
                dve.wait_ge(sig.sem, sig.done(t, "stats"))
                dve.memset(hold[:], 0.0)
                dve.bn_aggr(mv[:, k, :], st[:, k, :]).then_inc(sig.sem, 1)
                dve.wait_ge(pool_sig.sem, pool_sig.done(t, "rstd"))
                dve.wait_ge(sig.sem, sig.done(t, "aggr"))
                TS(dst, src, mv[:, k, 0:1], rstd[:, k:k + 1], ALU.subtract, ALU.mult).then_inc(sig.sem, 1)

            def self_xT(u):
                dve.wait_ge(pe_x.sem, pe_x.done(u, "xT"))
                dve.tensor_copy(xT2[:].rearrange("p c n -> p (c n)"), mbk[1][:, 0:D]).then_inc(dve_s.sem, 1)

            def self_rope(u):
                dve.wait_ge(pe_x.sem, pe_x.done(u, "qk"))
                heads2 = 2 * H
                m = mbk[0][:].rearrange("p (n d) -> p n d", d=DK)
                TT(rot_a[:].rearrange("p (n d) -> p n d", d=DK), m, over(k_("cos"), heads2, 1), ALU.mult
                   ).then_inc(dve_s.sem, 1)
                m2, r2 = (y[:].rearrange("p (n d two) -> p two n d", two=2, d=DK // 2) for y in (mbk[0], rot_b))
                sin2 = k_("sin").rearrange("p (d two) -> p two d", two=2)
                for z in range(2):
                    TT(r2[:, z], m2[:, 1 - z], over(sin2[:, z], heads2, 1), ALU.mult).then_inc(dve_s.sem, 1)
                dve.wait_ge(dve_s.sem, dve_s.done(u, "sin1"))
                TT(rot_a[:], rot_a[:], rot_b[:], ALU.add).then_inc(dve_s.sem, 1)

            def self_softmax_a(u):
                dve.wait_ge(pe_x.sem, pe_x.done(u, "scores"))
                dve.scalar_tensor_tensor(sc[:], mbk[0][:].rearrange("p (h k) -> p h k", h=H), 1.0 / DK,
                                         over(k_("causal"), H, 1), ALU.mult, ALU.add).then_inc(dve_s.sem, 1)
                dve.wait_ge(dve_s.sem, dve_s.done(u, "scaled"))
                RED(mx2[:], sc[:], X, ALU.max).then_inc(dve_s.sem, 1)
                dve.wait_ge(dve_s.sem, dve_s.done(u, "max"))
                TT(sc[:], sc[:], over(mx2[:], S, 2), ALU.subtract).then_inc(dve_s.sem, 1)

            def self_softmax_b(u):
                dve.wait_ge(act_s.sem, act_s.done(u, "exp"))
                RED(sm2[:], ex[:], X, ALU.add).then_inc(dve_s.sem, 1)
                dve.wait_ge(dve_s.sem, dve_s.done(u, "sum"))
                dve.reciprocal(ri2[:], sm2[:]).then_inc(dve_s.sem, 1)
                dve.wait_ge(dve_s.sem, dve_s.done(u, "rinv"))
                TT(pn[:].rearrange("p (h k) -> p h k", h=H), ex[:], over(ri2[:], S, 2), ALU.mult
                   ).then_inc(dve_s.sem, 1)
                dve.wait_ge(dve_s.sem, dve_s.done(u, "probs"))
                dve.transpose(pT2[:], pn[:]).then_inc(dve_s.sem, 1)

            def self_heads(u):
                dve.wait_ge(pe_x.sem, pe_x.done(u, "pv"))
                for c in range(C):
                    TT(masked2[:, c].rearrange("p (b n) -> p b n", b=BT), mbk[c][:].rearrange("p (b n) -> p b n", b=BT),
                       diag, ALU.mult).then_inc(dve_s.sem, 1)
                for c in range(C):
                    dve.wait_ge(dve_s.sem, dve_s.done(u, f"mask{c}"))
                    RED(att2[:, c].rearrange("p (b q) -> p b q", b=BT),
                        masked2[:, c].rearrange("p (b h q) -> p b q h", b=BT, h=HG), X, ALU.add).then_inc(dve_s.sem, 1)

            def self_end(u):
                dve.wait_ge(pe_x.sem, pe_x.done(u, "projected"))
                dve.wait_ge(pool_s.sem, pool_s.done(u, "x1b"))
                TT(x2[:], mbk[0][:, 0:D], x1b[:], ALU.add).then_inc(dve_s.sem, 1)
                dve.wait_ge(dve_s.sem, dve_s.done(u, "x2"))
                TS(x_all[:, bass.ds(u, 1), :].rearrange("p t n -> p (t n)"), x2[:], 1.0, None, ALU.mult).then_inc(dve_s.sem, 1)

            def route_max(w):
                dve.wait_ge(pe_g.sem, pe_g.done(w, "logits"))
                RED(gmx[:], mbk[1][:, 0:E], X, ALU.max, negate=True).then_inc(dve_g.sem, 1)

            def route_p(w):
                dve.wait_ge(act_g.sem, act_g.done(w, "exp"))
                dve.reciprocal(gri[:], gsm[:]).then_inc(dve_g.sem, 1)
                dve.wait_ge(dve_g.sem, dve_g.done(w, "rinv"))
                TS(gp[:], gex[:], gri[:, 0:1], None, ALU.mult).then_inc(dve_g.sem, 1)
                dve.wait_ge(dve_g.sem, dve_g.done(w, "p"))
                TT(dsp[:], over(gp[:], S, 2), over(k_("rep"), E, 1), ALU.mult).then_inc(dve_g.sem, 1)

            def route_rank(w):
                dve.wait_ge(pe_g.sem, pe_g.done(w, "others"))
                m = mbk[1][:, 0:E * S].rearrange("p (e s) -> p e s", e=E)
                TT(cgt[:], m, over(gp[:], S, 2), ALU.is_gt).then_inc(dve_g.sem, 1)
                TT(cge[:], m, over(gp[:], S, 2), ALU.is_ge).then_inc(dve_g.sem, 1)
                dve.wait_ge(dve_g.sem, dve_g.done(w, "gt"))
                TT(cgt[:], cgt[:], over(k_("after"), E, 1), ALU.mult).then_inc(dve_g.sem, 1)
                dve.wait_ge(dve_g.sem, dve_g.done(w, "ge"))
                TT(cge[:], cge[:], over(k_("before"), E, 1), ALU.mult).then_inc(dve_g.sem, 1)
                dve.wait_ge(dve_g.sem, dve_g.done(w, "ge_m"))
                TT(cgt[:], cgt[:], cge[:], ALU.add).then_inc(dve_g.sem, 1)
                dve.wait_ge(dve_g.sem, dve_g.done(w, "both"))
                RED(rank[:], cgt[:], X, ALU.add).then_inc(dve_g.sem, 1)
                dve.wait_ge(dve_g.sem, dve_g.done(w, "rank"))
                TT(sel[:], over(rank[:], BT * CAP, 2), over(k_("code"), E, 1), ALU.is_equal).then_inc(dve_g.sem, 1)
                dve.wait_ge(dve_g.sem, dve_g.done(w, "sel"))
                TT(selw[:], sel[:], over(gp[:], BT * CAP, 2), ALU.mult).then_inc(dve_g.sem, 1)

            def route_keep(w):
                n = BT * CAP
                for c in range(C):
                    dve.wait_ge(pe_g.sem, pe_g.done(w, f"xin{C - 1}"))
                    dve.tensor_copy(xin[:, c, :, bass.ds(w * n, n)],
                                    mbk[1][:, c * 256:(c + 1) * 256].rearrange("p (e s) -> p e s", e=E)
                                    ).then_inc(dve_g.sem, 1)
                dve.wait_ge(pe_g.sem, pe_g.done(w, "selT"))
                dve.tensor_copy(selT[:, bass.ds(w, 1)].rearrange("p t k n -> p (t k n)"), mbk[0][:, 0:2 * P]
                                ).then_inc(dve_g.sem, 1)

            def body(t, u, w):
                if u is not None:
                    heads(u, 1)
                if w is not None:
                    norm(dve_g, w, x2[:], dve_s.sem, dve_s.done(w, "x2"), xn3[:], 1, pool_g)
                if u is not None:
                    cross_att(u)
                if w is not None:
                    dve.wait_ge(pe_g.sem, pe_g.done(w, "xT"))
                    dve.tensor_copy(xT3[:].rearrange("p c n -> p (c n)"), mbk[0][:, 0:D]).then_inc(dve_g.sem, 1)
                if u is not None:
                    cross_x1(u)
                    norm(dve_s, u, x1[:], dve_a.sem, dve_a.done(u, "x1"), xn[:], 0, pool_s)
                if t is not None:
                    values(t, 0)
                for p in range(9):
                    if t is not None:
                        if p < 8:
                            maxima(t, 2 * p)
                            maxima(t, 2 * p + 1)
                            if p % 2 == 0 and p // 2 + 1 < BT:
                                values(t, p // 2 + 1)
                        if p >= 1 and p % 2 == 1:
                            turn(t, p - 1)
                        if p == 6:
                            heads(t, 0)
                        if p == 8:
                            dve.wait_ge(act_exp.sem, act_exp.done(t, f"e{H - 1}"))
                            dve.reciprocal(rinv[:], rsum[:]).then_inc(dve_r.sem, 1)
                    if u is not None and p == 0:
                        self_xT(u)
                    if u is not None and p == 2:
                        self_rope(u)
                    if w is not None and p == 2:
                        route_max(w)
                    if w is not None and p == 3:
                        route_p(w)
                    if w is not None and p == 4:
                        route_rank(w)
                    if u is not None and p == 5:
                        self_softmax_a(u)
                    if w is not None and p == 6:
                        route_keep(w)
                    if u is not None and p == 6:
                        self_softmax_b(u)
                    if u is not None and p == 8:
                        self_heads(u)
                        self_end(u)

            tiles(dve, body)

            dve.memset(hold[:], 0.0).then_inc(dve_y.sem, dve_y.base)

            def experts(r):
                for k in range(EQ):
                    dve.wait_ge(pe_y.sem, pe_y.done(r, f"y{k}"))
                    for q in range(BT):
                        src = mbk[k % 2][S * q:S * q + S, :].rearrange("p (h n) -> p h n", h=2)
                        dst = ys[S * k:S * k + S, q::BT, bass.ds(r, 1), :].rearrange("p h r n -> p h (r n)")
                        dve.tensor_copy(dst, src).then_inc(dve_y.sem, 1)

            with dve.Fori(0, E // EQ) as r:
                experts(r)
            for t in range(TILES):
                dve.wait_ge(pe_f.sem, pe_f.done(t, "f"))
                if t >= 2:
                    dve.wait_ge(s_out[t % 2], 16 * (t // 2))
                TT(fin[:, t % 2, :], mbk[t % 2][:, 0:D], x_all[:, t, :], ALU.add).then_inc(dve_f.sem, 1)


def kernel(**inputs):
    import concourse.bacc as bacc
    from concourse.bass_utils import run_bass_kernel_spmd as run

    i = {k: np.asarray(v) for k, v in inputs.items()}
    ctx = i["ctx_1024"]
    T = lambda n: np.ascontiguousarray(i[n].T)
    ctx_t = ctx.reshape(TILES, BT * KEYS, D)
    arrays = {
        "consts": tables(),
        "mask": np.ascontiguousarray(i["mask_Bx1x1xS2_if1"].reshape(B, KEYS)),
        "x": np.ascontiguousarray(i["x"].reshape(B * S, D)),
        "wq": T("L0_xattn_Wq"), "wk": T("L0_xattn_Wk"), "wv": T("L0_xattn_Wv"), "wo": T("L0_xattn_Wo"),
        "wqkv": np.ascontiguousarray(np.concatenate([i["L0_attn_Wq"], i["L0_attn_Wk"], i["L0_attn_Wv"]], axis=0).T),
        "wo2": T("L0_attn_Wo"),
        "gate": np.ascontiguousarray(i["L0_ffn_gate_w"]),
        "ctx_last": np.ascontiguousarray(ctx[:, KEYS - 1, :].T),
        "cols": np.ascontiguousarray(np.concatenate(
            [i[n].reshape(C, P).T for n in ("L0_xattn_bq", "L0_xattn_bk", "L0_xattn_bv")], axis=1)),
        "bo": np.ascontiguousarray(np.stack([i["L0_xattn_bo"], i["L0_attn_bo"]])),
        "ctxT": np.ascontiguousarray(ctx_t.transpose(0, 2, 1)),
        "w1": np.ascontiguousarray(i["L0_ffn_w1"]),
        "w2": np.ascontiguousarray(i["L0_ffn_w2"]),
    }
    nc = bacc.Bacc("TRN2", target_bir_lowering=False, num_devices=1)
    a = {n: nc.dram_tensor(f"in_{n}", v.shape, mybir.dt.from_np(v.dtype), kind="ExternalInput").ap()
         for n, v in arrays.items()}
    a["mask_terms"] = nc.dram_tensor("mask_terms", [B, KEYS], BF16, kind="Internal").ap()
    out = nc.dram_tensor("out", [B * S, D], F32, kind="ExternalOutput").ap()
    perceiver(nc, a, out)
    r = run(nc, [{f"in_{n}": v for n, v in arrays.items()}], core_ids=[0])
    return r.results[0]["out"].reshape(B, S, D)
```

```python
from contextlib import ExitStack

import concourse.bass as bass
from concourse import mybir
import numpy as np

ALU = mybir.AluOpType
ACT = mybir.ActivationFunctionType
F32 = mybir.dt.float32
F32R = mybir.dt.float32r
BF16 = mybir.dt.bfloat16
I32 = mybir.dt.int32
X = mybir.AxisListType.X

B, S, D = 32, 32, 256
KEYS = 257
H, DK = 16, 16
E, CAP, HID = 8, 8, 1024
EPS = 1e-5
P = 128
BT = P // S
TILES = B // BT
C = D // P
G = 4
HG = H // G
KB = BT * KEYS
KT = (KEYS - 1) // P
KW = KB + 8 // C
SW = KEYS + 1
PIECES = [(0, 344), (344, 342), (686, 342)]
HC = HID // P
NEG = -10000.0

CONSTS = [("ident", P), ("headmask", 8), ("diag", P), ("expand", HG * DK), ("rep", S), ("cos", DK), ("sin", DK),
          ("causal", S), ("batch_ones", P), ("code", BT * CAP), ("before", S), ("after", S)]
OFF = {}
_o = 0
for _n, _w in CONSTS:
    OFF[_n] = (_o, _o + _w)
    _o += _w
NCONST = _o


def tables():
    p = np.arange(P)
    q = p % S
    a = {}
    a["ident"] = np.eye(P)
    a["headmask"] = (p[:, None] // DK == np.arange(8)[None])
    a["diag"] = ((p[:, None] % 64) // DK == np.arange(P)[None] // S)
    a["expand"] = (p[:, None] // S == np.arange(HG * DK)[None] // DK)
    a["rep"] = (q[:, None] == np.arange(S)[None])
    inv = np.float32(1.0) / np.float32(10000.0) ** (np.arange(0, DK, 2, dtype=np.float32) / np.float32(DK))
    ang = (q.astype(np.float32)[:, None] * inv[None]).astype(np.float32)
    a["cos"] = np.repeat(np.cos(ang), 2, axis=1)
    sign = np.where(np.arange(DK) % 2 == 0, -1.0, 1.0)
    a["sin"] = np.repeat(np.sin(ang), 2, axis=1) * sign
    a["causal"] = np.where(q[:, None] >= np.arange(S)[None], 0.0, NEG)
    a["batch_ones"] = (p[:, None] // S == p[None] // S)
    j = np.arange(BT * CAP)
    a["code"] = np.where(p[:, None] // S == j[None] // CAP, j[None] % CAP, -1)
    a["before"] = (np.arange(S)[None] < q[:, None])
    a["after"] = (np.arange(S)[None] > q[:, None])
    return np.concatenate([np.asarray(a[n], np.float32) for n, _ in CONSTS], axis=1)


class Sig:

    def __init__(self, sem, steps, base=0):
        self.sem, self.n, self.base = sem, len(steps), base
        self.at = {s: k + 1 for k, s in enumerate(steps)}

    def done(self, t, step):
        return t * self.n + (self.base + self.at[step])

    def whole(self, t):
        return t * self.n + self.base


HI, LO = 0, 1
PASSES = ((LO, HI), (HI, LO), (HI, HI))


def later(t):
    return not (isinstance(t, int) and t == 0)


def perceiver(nc, a, out):
    ctx = ExitStack()
    with ctx:
        def sb(name, shape, dt=F32):
            return ctx.enter_context(nc.sbuf_tensor(name, shape, dt))

        def bank(name):
            return ctx.enter_context(nc.psum_tensor(name, [P, 512], F32))

        def sem(name):
            return ctx.enter_context(nc.semaphore(name))

        def sig(name, steps, base=0):
            return Sig(sem(name), steps, base)

        cst = sb("cst", [P, NCONST])

        def k_(name):
            return cst[:, OFF[name][0]:OFF[name][1]]

        gate = sb("gate", [P, C, E])
        cols = sb("cols", [P, 3, C])
        bqs = sb("bqs", [P, C])
        bo_b = sb("bo_b", [P, 2, D])
        mask_b = sb("mask_b", [B, KEYS], BF16)
        row0 = sb("row0", [P, P], BF16)
        mrow = sb("mrow", [P, KW], BF16)
        mhalf = sb("mhalf", [P, TILES])
        eps = sb("eps", [P, TILES])
        x_all = sb("x_all", [P, TILES, D])
        st1 = sb("st1", [P, TILES, 6])
        mv1 = sb("mv1", [P, TILES, 2])
        ve1 = sb("ve1", [P, TILES])
        rstd1 = sb("rstd1", [P, TILES])
        ctx_last = sb("ctx_last", [P, C, B])
        vlast = sb("vlast", [P, TILES, C, BT])
        def room(name, n):
            start = (nc.sbuf_base + 31) // 32 * 32
            sb(name, [P, n])

            def laid(part, k, shape, dt=F32):
                flat = nc.alloc_sbuf_tensor_at(part, [P, int(np.prod(shape))], dt, offset=start + 4 * k)
                names = "abcd"[:len(shape)]
                return flat[:].rearrange(f"p ({' '.join(names)}) -> p {' '.join(names)}", **dict(zip(names, shape)))
            return laid

        NQ = C * BT * 8 * S
        laid = room("tile_room", C * KB + C * KW)
        ctxT = laid("ctxT", 0, [C, KB])
        ctxL = laid("ctxL", 0, [C, KB], F32R)
        kTH = laid("kTH", C * KB, [C, KW], F32R)
        ys = laid("ys", 0, [TILES, 2, D])
        laid = room("block_room", 2 * NQ)
        qblkH = laid("qblkH", 0, [C, BT, 8 * S], F32R)
        kblk = laid("kblk", NQ, [C, BT, 8 * S])
        xT1 = laid("xT1", NQ, [C, TILES * P])
        hH = laid("hH", 0, [2, HC, 2 * P], F32R)
        laid = room("split_room", C * KB + C * KW + NQ)
        ctxH = laid("ctxH", 0, [C, KB], F32R)
        kTL = laid("kTL", C * KB, [C, KW], F32R)
        qblkL = laid("qblkL", C * KB + C * KW, [C, BT, 8 * S], F32R)
        w1s = [laid(f"w1s{i}", i * C * HID, [C, HID]) for i in range(2)]
        w1L = [laid(f"w1L{i}", i * C * HID, [C, HID], F32R) for i in range(2)]
        w2s, w2L = [laid("w2s0", 2 * C * HID, [HC, D])], [laid("w2L0", 2 * C * HID, [HC, D], F32R)]
        laid = room("query_room", C * TILES * P)
        qT = laid("qT", 0, [C, TILES * P])
        w2s.append(laid("w2s1", 0, [HC, D]))
        w2L.append(laid("w2L1", 0, [HC, D], F32R))
        qtH = sb("qtH", [P, C, P], F32R)[:]
        qtL = sb("qtL", [P, C, P])[:]
        laid = room("projection_room", 6 * C * D)
        wq, wo, wo2 = (laid(n, k * C * D, [C, D]) for k, n in enumerate(("wq", "wo", "wo2")))
        wqkv = laid("wqkv", 3 * C * D, [C, 3 * D])
        hf = laid("hf", 0, [HC, 2 * P])
        fin = laid("fin", HC * 2 * P, [2, D])
        laid = room("weight_room", 4 * C * D + BT * KT * D)
        wk, wv = (laid(n, k * C * D, [C, D]) for k, n in enumerate(("wk", "wv")))
        wkL, wvL, wkH, wvH = (laid(n, k * C * D, [C, D], F32R) for k, n in enumerate(("wkL", "wvL", "wkH", "wvH")))
        v = laid("v", 4 * C * D, [BT, KT, D])
        wH0 = [laid("w1H0", 0, [C, HID], F32R), laid("w2H0", C * HID, [HC, D], F32R)]

        def f32(ap):
            return ap.bitcast(F32)

        ctx2, wk2, wv2, kT2, qblk2 = (ctxH, ctxL), (wkH, wkL), (wvH, wvL), (kTH, kTL), (qblkH, qblkL)
        nmax = sb("nmax", [P, H])
        rsum = sb("rsum", [P, G, BT])
        rinv = sb("rinv", [P, G, BT])
        laid = room("cross_room", 10 * 512)
        mask_i = laid("mask_i", 0, [KEYS], I32)[0:B]
        mask_f = laid("mask_f", 512, [KEYS])[0:B]
        probs = laid("probs", 0, [2, 2, KEYS])
        pT, k = laid("pT", 1032, [2, 2, KT * P]), 1032 + 4 * KT * P
        masked, k = laid("masked", k, [4 * P]), k + 4 * P
        att_u, k = laid("att_u", k, [2, C, 2 * S]), k + 2 * C * 2 * S
        rep_r, k = laid("rep_r", k, [G, BT * S]), k + G * BT * S
        rep_p, k = laid("rep_p", k, [G, BT * S]), k + G * BT * S
        att = laid("att", k, [C, P])
        wH1 = [laid("w1H1", 0, [C, HID], F32R), laid("w2H1", C * HID, [HC, D], F32R)]
        w1H, w2H = zip(wH0, wH1)
        x1 = sb("x1", [P, D])
        x1b = sb("x1b", [P, D])
        st = sb("st", [P, 2, 6])
        mv = sb("mv", [P, 2, 2])
        ve = sb("ve", [P, 2])
        rstd = sb("rstd", [P, 2])
        x2 = sb("x2", [P, D])
        hold = sb("hold", [P, 1])
        xn = sb("xn", [P, D])
        xT2 = sb("xT2", [P, C, P])
        laid = room("self_room", 4 * D + BT * D + 2 * 4 * P + 4 * H * S)
        rot_a = laid("rot_a", 0, [2 * D])
        rot_b = laid("rot_b", 2 * D, [2 * D])
        vz = laid("vz", 4 * D, [BT, D])
        masked2 = laid("masked2", 4 * D + BT * D, [2, 4 * P])
        sc, ex = (laid(n, (6 + k) * 512, [H, S]) for k, n in enumerate(("sc", "ex")))
        pn, pT2 = (laid(n, (8 + k) * 512, [H * S]) for k, n in enumerate(("pn", "pT2")))
        xn1 = laid("xn1", 4 * D + BT * D, [2, D])
        hL = [laid(f"hL{k}", (1 + 4 * k) * 512, [HC, 2 * P], F32R) for k in range(2)]
        qk2 = sb("qk2", [P, 2, C, P])
        mx2 = sb("mx2", [P, H])
        sm2 = sb("sm2", [P, H])
        ri2 = sb("ri2", [P, H])
        att2 = sb("att2", [P, C, P])
        xn3 = sb("xn3", [P, D])
        xT3 = sb("xT3", [P, C, P])
        gmx = sb("gmx", [P, 1])
        gex = sb("gex", [P, E])
        gsm = sb("gsm", [P, 1])
        gri = sb("gri", [P, 1])
        gp = sb("gp", [P, E])
        dsp = sb("dsp", [P, E, S])
        cgt = sb("cgt", [P, E, S])
        cge = sb("cge", [P, E, S])
        rank = sb("rank", [P, E])
        sel = sb("sel", [P, E, BT * CAP])
        selw = sb("selw", [P, E, BT * CAP])
        xin2 = [sb(n, [P, C, E, TILES * BT * CAP], F32R) for n in ("xinH", "xinL")]
        selT = sb("selT", [P, TILES, 2, P])

        sbk = [bank(f"sbk{i}") for i in range(3)]
        ring = [bank(f"ring{i}") for i in range(2)]
        obk = bank("obk")
        mbk = [bank(f"mbk{i}") for i in range(2)]

        s_const, s_w, s_x, s_mask = (sem(n) for n in ("s_const", "s_w", "s_x", "s_mask"))
        s_ctx, s_mrow, s_mst = sem("s_ctx"), sem("s_mrow"), sem("s_mst")
        s_w1, s_w2 = ([sem(f"s_w{j}_{i}") for i in range(2)] for j in (1, 2))
        s_out = [sem(f"s_out{i}") for i in range(2)]
        N_W = 11

        pro = sig("pro", ["mask0", "mask", "mrow0", "row0", "row1", "half", "eps", "pad0", "pad1", "bqs", "vz0", "st",
                          "mv"])
        pro_xn = sig("pro_xn", ["xn"])
        pro_xT = sig("pro_xT", ["xT"])
        pro_pool = sig("pro_pool", ["var", "rstd"])
        pro_t = sig("pro_t", ["t"])
        pro_q = sig("pro_q", ["q00", "q01", "q10", "q11"])
        pro_qe = sig("pro_qe", ["q00", "q01", "q10", "q11"])
        pro_w = sig("pro_w", ["hk", "hv", "lk", "lv"])
        act_c = sig("act_c", ["hi0", "hi1"])
        pool_c = sig("pool_c", ["lo0", "lo1"])
        pro_vl = sem("pro_vl")
        pro_vle = sem("pro_vle")
        pro_xbo = sig("pro_xbo", ["x"])

        pe_k = sig("pe_k", [f"k{i}" for i in range(6)])
        pe_v = sig("pe_v", [f"v{b}" for b in range(BT)])
        act_k = sig("act_k", [f"k{i}" for i in range(6)])
        dve_k = sig("dve_k", [f"k{i}" for i in range(6)])
        act_v = sig("act_v", [f"v{b}" for b in range(BT)])
        act_q = sig("act_q", ["hi"])
        pool_q = sig("pool_q", [f"q{HI}{c}" for c in range(C)] + ["lo"] + [f"q{LO}{c}" for c in range(C)])
        pe_s = sig("pe_s", [f"s{i}" for i in range(H)])
        dve_max = sig("dve_max", [f"m{i}" for i in range(H)])
        act_exp = sig("act_exp", [f"e{i}" for i in range(H)])
        pool_last = sig("pool_last", [f"l{i}" for i in range(H)])
        pe_t = sig("pe_t", [f"t{p}" for p in range(8)])
        act_t = sig("act_t", [f"t{p}" for p in range(8)])
        pe_o = sig("pe_o", [f"o{p}" for p in range(8)])
        dve_o = sig("dve_o", ["mask0", "sum0", "mask1", "sum1"])
        dve_r = sig("dve_r", ["rinv"])
        pool_e = sig("pool_e", ["rep_r"])
        pe_e = sig("pe_e", ["expanded", "projected"])
        dve_a = sig("dve_a", ["last", "plus", "norm", "att", "x1"])
        dve_s = sig("dve_s", ["stats", "aggr", "xn", "xT", "cos", "sin0", "sin1", "rope", "scaled", "max", "sub",
                              "sum", "rinv", "probs", "turned", "mask0", "mask1", "sum0", "sum1", "x2", "kept"])
        pool_s = sig("pool_s", ["x1b", "var", "rstd", "kblk0", "kblk1"])
        act_s = sig("act_s", ["v0", "v1", "v2", "v3", "qk", "exp"])
        pe_x = sig("pe_x", ["xT", "qk", "v", "qkT", "scores", "pv", "projected"])
        dve_g = sig("dve_g", ["stats", "aggr", "xn", "xT", "max", "rinv", "p", "spread", "gt", "ge", "rank", "sel", "selw", "xinH", "xinL", "selT"])
        pool_g = sig("pool_g", ["var", "rstd", "gt_m", "ge_m", "both"])
        act_g = sig("act_g", ["exp"])
        pe_g = sig("pe_g", ["xT", "logits", "others", "xin0", "xin1", "selT"])
        EQ = 4
        pe_h = sig("pe_h", [f"h{e}{j}" for e in range(EQ) for j in range(HC // 2)])
        act_h = sig("act_h", [f"{z}{e}{j}" for e in range(EQ) for j in range(HC // 2) for z in "fh"])
        dve_h = sig("dve_h", [f"h{e}{j}" for e in range(EQ) for j in range(HC // 2)])
        act_w = sig("act_w", ["w10", "w11", "w20", "w12", "w21", "w13", "w22", "w23"])
        dve_w = sig("dve_w", ["w11", "w20", "w12", "w21", "w13", "w22", "w23"])
        pool_w = sig("pool_w", ["w10", "w20", "w21", "w22", "w23"])
        pe_y = sig("pe_y", [f"y{e}" for e in range(EQ)])
        dve_y = sig("dve_y", [f"y{e}{q}" for e in range(EQ) for q in range(BT)], base=1)
        pe_f = sig("pe_f", ["f"])
        dve_f = sig("dve_f", ["f"])

        uses = [(dve_k, f"k{i}") for i in range(6)] + [(act_v, "v0")]
        for p in range(9):
            if p % 2 == 0 and p // 2 + 1 < BT:
                uses.append((act_v, f"v{p // 2 + 1}"))
            if p >= 1:
                uses.append((act_t, f"t{p - 1}"))
        place = {(id(s), n): u for u, (s, n) in enumerate(uses)}

        def ring_bank(s, n):
            return ring[place[(id(s), n)] % 2]

        def ring_read(t, s, n):
            u = place[(id(s), n)]
            last, step = uses[u - 2]
            return (last.sem, last.done(t if u >= 2 else t - 1, step))

        def over(ap, n, at):
            shape = list(ap.shape)
            ap = ap.unsqueeze(at)
            return ap.broadcast_to(shape[:at] + [n] + shape[at:])

        block = ctx.enter_context(nc.Block())

        def tiles(eng, body):
            body(0, None, None)
            body(1, 0, None)
            with eng.Fori(2, TILES - 1) as t:
                body(t, t - 1, t - 2)
            body(TILES - 1, TILES - 2, TILES - 3)
            body(None, TILES - 1, TILES - 2)
            body(None, None, TILES - 1)

        @block.sync
        def _(sp):
            sp.dma_start(cst[:], a["consts"]).then_inc(s_const, 16)
            sp.dma_start(mask_i[:], a["mask"]).then_inc(s_mask, 16)
            sp.dma_start(x_all[:], a["x"].rearrange("(t p) d -> p t d", p=P)).then_inc(s_x, 16)
            for dst, n in ((wq, "wq"), (wk, "wk"), (wv, "wv"), (wo, "wo"), (wqkv, "wqkv"), (wo2, "wo2"),
                           (gate[:], "gate")):
                sp.dma_start(dst, a[n].rearrange("(c p) n -> p c n", p=P)).then_inc(s_w, 16)
            sp.dma_start(ctx_last[:], a["ctx_last"].rearrange("(c p) n -> p c n", p=P)).then_inc(s_w, 16)
            sp.dma_start(cols[:], a["cols"].rearrange("p (j c) -> p j c", c=C)).then_inc(s_w, 16)
            for j in range(2):
                sp.dma_start(bo_b[:, j, :], a["bo"][j].partition_broadcast(P)).then_inc(s_w, 16)
            ctx_d = a["ctxT"].rearrange("t (c p) n -> t p c n", p=P)

            def load_tile(t):
                if later(t):
                    sp.wait_ge(pe_v.sem, pe_v.whole(t))
                src = ctx_d[t] if isinstance(t, int) else ctx_d[bass.ds(t, 1)].rearrange("t p c n -> (t p) c n")
                sp.dma_start(ctxT, src).then_inc(s_ctx, 16)
                if later(t):
                    sp.wait_ge(pe_s.sem, pe_s.whole(t))
                sp.dma_start(mrow[0:1, 0:KB], terms[bass.ds(t, 1), :]).then_inc(s_mrow, 16)

            def load_expert(e):
                w1_d, w2_d = (a[n].rearrange("e (c p) n -> e p c n", p=P) for n in ("w1", "w2"))
                if e >= 2:
                    sp.wait_ge(pe_h.sem, (e - 1) * HC // 2)
                sp.dma_start(w1s[e % 2], w1_d[e]).then_inc(s_w1[e % 2], 16)
                if e >= 2:
                    sp.wait_ge(pe_y.sem, e - 1)
                sp.dma_start(w2s[e % 2], w2_d[e]).then_inc(s_w2[e % 2], 16)

            terms = a["mask_terms"].rearrange("(t b) k -> t (b k)", b=BT)
            sp.wait_ge(pro.sem, pro.done(0, "mask"))
            sp.dma_start(a["mask_terms"], mask_b[:]).then_inc(s_mst, 16)
            sp.wait_ge(s_mst, 16)
            sp.wait_ge(pro.sem, pro.done(0, "mrow0"))
            load_tile(0)
            with sp.Fori(1, TILES) as t:
                load_tile(t)
            sp.wait_ge(pe_s.sem, pe_s.whole(TILES))
            sp.wait_ge(pe_v.sem, pe_v.whole(TILES))
            for e in range(E):
                load_expert(e)
            for t in range(TILES):
                sp.wait_ge(dve_f.sem, dve_f.done(t, "f"))
                sp.dma_start(out[t * P:(t + 1) * P, :], fin[:, t % 2, :]).then_inc(s_out[t % 2], 16)
            for i in range(2):
                sp.wait_ge(s_out[i], 16 * TILES // 2)

        @block.tensor
        def _(pe):
            mm = pe.matmul
            ident = k_("ident")
            pe.wait_ge(s_const, 16)
            pe.wait_ge(s_w, 16 * N_W)
            for c in range(C):
                for j in range(C):
                    m = mm(ring[0][:, c * B:(c + 1) * B], wv[:, j, c * P:(c + 1) * P], ctx_last[:, j, :],
                           start=(j == 0), stop=(j == C - 1))
            m.then_inc(pro_vl, 1)
            for t in range(TILES):
                pe.wait_ge(pro_xn.sem, pro_xn.done(t, "xn"))
                if t >= 2:
                    pe.wait_ge(pro_xT.sem, pro_xT.done(t - 2, "xT"))
                for c in range(C):
                    m = pe.transpose(mbk[t % 2][:, c * P:(c + 1) * P], xn1[:, t % 2, c * P:(c + 1) * P], ident)
                m.then_inc(pro_t.sem, 1)
                if t % 4 == 3:
                    n = t // 4
                    pe.wait_ge(pro_xT.sem, pro_xT.done(t, "xT"))
                    for c in range(C):
                        if n:
                            pe.wait_ge(pro_qe.sem, pro_qe.done(0, f"q{n - 1}{c}"))
                        for j in range(C):
                            m = mm(sbk[c][:], wq[:, j, c * P:(c + 1) * P], xT1[:, j, n * 512:(n + 1) * 512],
                                   start=(j == 0), stop=(j == C - 1))
                        m.then_inc(pro_q.sem, 1)
            pe.wait_ge(pro_vle, 1)
            pe.wait_ge(pro_qe.sem, pro_qe.done(0, "q11"))
            pe.wait_ge(pro_xT.sem, pro_xT.done(TILES - 1, "xT"))
            pe.wait_ge(pro.sem, pro.done(0, "row1"))

            def split_product(out, left, right):
                steps = [(l, r, j) for j in range(left[0].shape[1]) for l, r in PASSES]
                for n, (l, r, j) in enumerate(steps):
                    m = mm(out, left[l][:, j], right[r][:, j], start=(n == 0), stop=(n == len(steps) - 1))
                return m

            def keys(t, i):
                if later(t) or i >= 2:
                    pe.wait_ge(*ring_read(t, dve_k, f"k{i}"))
                c, (o, n) = i // 3, PIECES[i % 3]
                split_product(ring_bank(dve_k, f"k{i}")[:, 0:n], [z[:, :, c * P:(c + 1) * P] for z in wk2],
                              [z[:, :, o:o + n] for z in ctx2]).then_inc(pe_k.sem, 1)

            def values(t, b):
                pe.wait_ge(*ring_read(t, act_v, f"v{b}"))
                for kt in range(KT):
                    o = b * KEYS + kt * P
                    m = split_product(ring_bank(act_v, f"v{b}")[:, kt * D:(kt + 1) * D],
                                      [z[:, :, o:o + P] for z in ctx2], wv2)
                m.then_inc(pe_v.sem, 1)

            def scores(t, i):
                b, g = i // G, i % G
                if i >= 3:
                    pe.wait_ge(act_exp.sem, act_exp.done(t, f"e{i - 3}"))
                else:
                    if later(t):
                        pe.wait_ge(act_exp.sem, act_exp.whole(t))
                o, c = sbk[i % 3][:, 0:SW], g // 2
                mm(o, row0[:], mrow[:, b * KEYS:b * KEYS + SW], start=True, stop=False)
                for l, r in PASSES:
                    m = mm(o, qblk2[l][:, c, b, (g % 2) * P:(g % 2 + 1) * P], kT2[r][:, c, b * KEYS:b * KEYS + SW],
                           start=False, stop=((l, r) == PASSES[-1]))
                m.then_inc(pe_s.sem, 1)

            def turn(t, p):
                name = f"t{p}"
                pe.wait_ge(*ring_read(t, act_t, name))
                pe.wait_ge(act_exp.sem, act_exp.done(t, f"e{2 * p + 1}"))
                for gg in range(2):
                    for kt in range(KT):
                        o = (gg * KT + kt) * P
                        m = pe.transpose(ring_bank(act_t, name)[:, o:o + P],
                                         probs[:, p % 2, gg, kt * P:(kt + 1) * P], ident)
                m.then_inc(pe_t.sem, 1)

            def attend(t, p):
                b, c = p // 2, p % 2
                if p == 0:
                    if later(t):
                        pe.wait_ge(dve_a.sem, dve_a.whole(t))
                if p == 4:
                    pe.wait_ge(dve_o.sem, dve_o.done(t, "mask0"))
                pe.wait_ge(act_t.sem, act_t.done(t, f"t{p}"))
                pe.wait_ge(act_v.sem, act_v.done(t, f"v{b}"))
                for gg in range(2):
                    g = 2 * c + gg
                    for kt in range(KT):
                        m = mm(obk[64 * gg:64 * gg + 64, c * 256 + (b % 2) * P:c * 256 + (b % 2 + 1) * P],
                               v[:, b, kt, g * 64:(g + 1) * 64], pT[:, p % 2, gg, kt * P:(kt + 1) * P],
                               start=(kt == 0), stop=(kt == KT - 1))
                m.then_inc(pe_o.sem, 1)

            def expand(t):
                pe.wait_ge(pool_e.sem, pool_e.done(t, "rep_r"))
                pe.wait_ge(pool_last.sem, pool_last.done(t, f"l{H - 1}"))
                pe.wait_ge(dve_o.sem, dve_o.done(t, "mask1"))
                for k, r in enumerate((rep_r, rep_p)):
                    for g in range(G):
                        o = k * 256 + (g // 2) * P
                        m = mm(obk[64 * (g % 2):64 * (g % 2) + 64, o:o + P], k_("expand"), r[:, g, :],
                               start=True, stop=True)
                m.then_inc(pe_e.sem, 1)

            def project(t):
                pe.wait_ge(dve_a.sem, dve_a.done(t, "att"))
                for j in range(C):
                    m = mm(obk[:, 0:D], att[:, j, :], wo[:, j, :], start=(j == 0), stop=(j == C - 1))
                m.then_inc(pe_e.sem, 1)

            def self_xT(u):
                pe.wait_ge(dve_s.sem, dve_s.done(u, "xn"))
                for c in range(C):
                    m = pe.transpose(mbk[1][:, c * P:(c + 1) * P], xn[:, c * P:(c + 1) * P], ident)
                m.then_inc(pe_x.sem, 1)

            def self_qkv(u):
                pe.wait_ge(dve_s.sem, dve_s.done(u, "xT"))
                for o, n, bk in ((0, 512, mbk[0]), (512, D, mbk[1])):
                    for j in range(C):
                        m = mm(bk[:, 0:n], xT2[:, j, :], wqkv[:, j, o:o + n], start=(j == 0), stop=(j == C - 1))
                    m.then_inc(pe_x.sem, 1)

            def self_qkT(u):
                pe.wait_ge(dve_s.sem, dve_s.done(u, "rope"))
                for j in range(4):
                    m = pe.transpose(mbk[0][:, j * P:(j + 1) * P], rot_a[:, j * P:(j + 1) * P], ident)
                m.then_inc(pe_x.sem, 1)

            def self_scores(u):
                pe.wait_ge(act_s.sem, act_s.done(u, "qk"))
                pe.wait_ge(pool_s.sem, pool_s.done(u, "kblk1"))
                for b in range(BT):
                    for c in range(C):
                        m = mm(mbk[0][S * b:S * b + S, c * 256:(c + 1) * 256], qk2[:, 0, c, S * b:S * b + S],
                               kblk[:, c, b, :], start=True, stop=True)
                m.then_inc(pe_x.sem, 1)

            def self_attend(u):
                pe.wait_ge(dve_s.sem, dve_s.done(u, "turned"))
                pe.wait_ge(act_s.sem, act_s.done(u, "v3"))
                for g in range(G):
                    for b in range(BT):
                        m = mm(mbk[g // 2][64 * (g % 2):64 * (g % 2) + 64, b * P:(b + 1) * P],
                               vz[:, b, g * 64:(g + 1) * 64], pT2[:, g * P:(g + 1) * P], start=True, stop=True)
                m.then_inc(pe_x.sem, 1)

            def self_project(u):
                pe.wait_ge(dve_s.sem, dve_s.done(u, "sum1"))
                for j in range(C):
                    m = mm(mbk[0][:, 0:D], att2[:, j, :], wo2[:, j, :], start=(j == 0), stop=(j == C - 1))
                m.then_inc(pe_x.sem, 1)

            def route_xT(w):
                pe.wait_ge(dve_g.sem, dve_g.done(w, "xn"))
                for c in range(C):
                    m = pe.transpose(mbk[0][:, c * P:(c + 1) * P], xn3[:, c * P:(c + 1) * P], ident)
                m.then_inc(pe_g.sem, 1)

            def route_logits(u, w):
                if u is not None:
                    pe.wait_ge(act_s.sem, act_s.done(u, "v3"))
                pe.wait_ge(dve_g.sem, dve_g.done(w, "xT"))
                for j in range(C):
                    m = mm(mbk[1][:, 0:E], xT3[:, j, :], gate[:, j, :], start=(j == 0), stop=(j == C - 1))
                m.then_inc(pe_g.sem, 1)

            def route_others(w):
                pe.wait_ge(dve_g.sem, dve_g.done(w, "spread"))
                mm(mbk[1][:, 0:E * S], k_("batch_ones"), dsp[:].rearrange("p e s -> p (e s)"),
                   start=True, stop=True).then_inc(pe_g.sem, 1)

            def route_gather(u, w):
                pe.wait_ge(dve_g.sem, dve_g.done(w, "selw"))
                for c in range(C):
                    mm(mbk[1][:, c * 256:(c + 1) * 256], xn3[:, c * P:(c + 1) * P],
                       sel[:].rearrange("p e s -> p (e s)"), start=True, stop=True).then_inc(pe_g.sem, 1)
                if u is not None:
                    pe.wait_ge(dve_s.sem, dve_s.done(u, "scaled"))
                flat = selw[:].rearrange("p e s -> p (e s)")
                for k in range(2):
                    m = pe.transpose(mbk[0][:, k * P:(k + 1) * P], flat[:, k * P:(k + 1) * P], ident)
                m.then_inc(pe_g.sem, 1)

            def body(t, u, w):
                if u is not None:
                    attend(u, 7)
                if t is not None:
                    pe.wait_ge(pool_c.sem, pool_c.done(t, "lo1"))
                    keys(t, 0)
                if w is not None:
                    self_attend(w)
                if t is not None:
                    keys(t, 1)
                    keys(t, 2)
                if u is not None:
                    expand(u)
                if w is not None:
                    self_project(w)
                if t is not None:
                    keys(t, 3)
                    keys(t, 4)
                if u is not None:
                    project(u)
                if t is not None:
                    keys(t, 5)
                    values(t, 0)
                if w is not None:
                    route_xT(w)
                if t is not None:
                    pe.wait_ge(s_mrow, (t + 1) * 16)
                    pe.wait_ge(pool_q.sem, pool_q.done(t, f"q{LO}{C - 1}"))
                    pe.wait_ge(dve_k.sem, dve_k.done(t, "k5"))
                for p in range(9):
                    if t is not None:
                        if p < 8:
                            scores(t, 2 * p)
                            scores(t, 2 * p + 1)
                            if p % 2 == 0 and p // 2 + 1 < BT:
                                values(t, p // 2 + 1)
                    if u is not None and p == 5:
                        self_scores(u)
                    if w is not None and p == 7:
                        route_gather(u, w)
                    if t is not None:
                        if p >= 1:
                            turn(t, p - 1)
                        if p >= 2:
                            attend(t, p - 2)
                    if u is not None and p == 0:
                        self_xT(u)
                    if u is not None and p == 1:
                        if w is not None:
                            pe.wait_ge(dve_g.sem, dve_g.done(w, "xT"))
                        self_qkv(u)
                    if w is not None and p == 2:
                        route_logits(u, w)
                    if u is not None and p == 3:
                        self_qkT(u)
                    if w is not None and p == 4:
                        route_others(w)
                    if w is not None and p == 8:
                        pe.wait_ge(dve_g.sem, dve_g.done(w, "selT"))

            tiles(pe, body)

            hbk = [sbk[0], sbk[1], sbk[2], ring[0]]
            pe.wait_ge(dve_g.sem, dve_g.done(TILES - 1, "selT"))

            def hidden(r, k, e):
                for j in range(HC // 2):
                    if k:
                        pe.wait_ge(act_h.sem, act_h.done(r, f"h{k - 1}{j}"))
                    for jj in range(2):
                        o = (2 * j + jj) * P
                        m = split_product(hbk[j][:, jj * 256:(jj + 1) * 256], [w[k % 2][:, :, o:o + P] for w in (w1H, w1L)],
                                          [x[:, :, bass.ds(e, 1), :].rearrange("p c e n -> p c (e n)") for x in xin2])
                    m.then_inc(pe_h.sem, 1)

            def result(r, k):
                pe.wait_ge(pool_w.sem, pool_w.done(r, f"w2{k}"))
                pe.wait_ge(dve_w.sem, dve_w.done(r, f"w2{k}"))
                pe.wait_ge(dve_h.sem, dve_h.done(r, f"h{k}{HC // 2 - 1}"))
                if k >= 2:
                    pe.wait_ge(dve_y.sem, dve_y.done(r, f"y{k - 2}{BT - 1}"))
                else:
                    if later(r):
                        pe.wait_ge(dve_y.sem, dve_y.whole(r))
                for half in range(2):
                    m = split_product(mbk[k % 2][:, half * D:(half + 1) * D],
                                      [h[:, :, half * P:(half + 1) * P] for h in (hH[:, k % 2], hL[k % 2])],
                                      [w[k % 2] for w in (w2H, w2L)])
                m.then_inc(pe_y.sem, 1)

            def experts(r):
                for k in range(EQ):
                    if k:
                        pe.wait_ge(dve_w.sem, dve_w.done(r, f"w1{k}"))
                    else:
                        pe.wait_ge(pool_w.sem, pool_w.done(r, "w10"))
                    hidden(r, k, r * EQ + k)
                    if k:
                        result(r, k - 1)
                result(r, EQ - 1)

            with pe.Fori(0, E // EQ) as r:
                experts(r)

            for t in range(TILES):
                pe.wait_ge(dve_y.sem, dve_y.done(1, f"y{EQ - 1}{BT - 1}"))
                if t >= 2:
                    pe.wait_ge(dve_f.sem, dve_f.done(t - 2, "f"))
                for r in range(2):
                    m = mm(mbk[t % 2][:, 0:D], selT[:, t, r, :], ys[:, t, r, :], start=(r == 0), stop=(r == 1))
                m.then_inc(pe_f.sem, 1)

        @block.scalar
        def _(act):
            A = act.activation
            def keys(t, i):
                act.wait_ge(pe_k.sem, pe_k.done(t, f"k{i}"))
                c, (o, n) = i // 3, PIECES[i % 3]
                if i == 0 and later(t):
                    act.wait_ge(pe_s.sem, pe_s.whole(t))
                A(kT2[HI][:, c, o:o + n], ring_bank(dve_k, f"k{i}")[:, 0:n], ACT.Identity,
                  bias=cols[:, 1, c:c + 1]).then_inc(act_k.sem, 1)

            def values(t, b):
                act.wait_ge(pe_v.sem, pe_v.done(t, f"v{b}"))
                if b == 0 and later(t):
                    act.wait_ge(pe_o.sem, pe_o.whole(t))
                A(v[:, b].rearrange("p k n -> p (k n)"), ring_bank(act_v, f"v{b}")[:], ACT.Copy).then_inc(act_v.sem, 1)

            def context(t):
                act.wait_ge(s_ctx, (t + 1) * 16)
                if later(t):
                    act.wait_ge(pe_v.sem, pe_v.whole(t))
                for c in range(C):
                    A(ctx2[HI][:, c], ctxT[:, c], ACT.Copy).then_inc(act_c.sem, 1)

            def queries(t):
                if later(t):
                    act.wait_ge(pool_q.sem, pool_q.whole(t))
                A(qtH, qT[:, :, bass.ds(t * P, P)], ACT.Copy).then_inc(act_q.sem, 1)

            def exps(t, i):
                b, g, p = i // G, i % G, i // 2
                act.wait_ge(dve_max.sem, dve_max.done(t, f"m{i}"))
                if i % 2 == 0:
                    if p >= 2:
                        act.wait_ge(pe_t.sem, pe_t.done(t, f"t{p - 2}"))
                        act.wait_ge(pool_last.sem, pool_last.done(t, f"l{2 * p - 3}"))
                    else:
                        if later(t):
                            act.wait_ge(pe_t.sem, pe_t.whole(t))
                        if later(t):
                            act.wait_ge(pool_last.sem, pool_last.whole(t))
                if i == 0:
                    if later(t):
                        act.wait_ge(dve_r.sem, dve_r.whole(t))
                A(probs[:, p % 2, i % 2, :], sbk[i % 3][:, 0:KEYS], ACT.Exp, bias=nmax[:, i:i + 1],
                  accum_out=rsum[:, g, b:b + 1]).then_inc(act_exp.sem, 1)

            def turn(t, p):
                act.wait_ge(pe_t.sem, pe_t.done(t, f"t{p}"))
                if p >= 2:
                    act.wait_ge(pe_o.sem, pe_o.done(t, f"o{p - 2}"))
                else:
                    if later(t):
                        act.wait_ge(pe_o.sem, pe_o.whole(t))
                A(pT[:, p % 2].rearrange("p g n -> p (g n)"), ring_bank(act_t, f"t{p}")[:], ACT.Copy
                  ).then_inc(act_t.sem, 1)

            act.wait_ge(s_w, 16 * N_W)
            context(0)
            act.wait_ge(pro.sem, pro.done(0, "bqs"))
            for n in range(2):
                for c in range(C):
                    act.wait_ge(pro_q.sem, pro_q.done(0, f"q{n}{c}"))
                    A(qT[:, c, n * 512:(n + 1) * 512], sbk[c][:], ACT.Identity, bias=bqs[:, c:c + 1],
                      scale=0.25).then_inc(pro_qe.sem, 1)

            def self_v(u):
                act.wait_ge(pe_x.sem, pe_x.done(u, "v"))
                for b in range(BT):
                    A(vz[S * b:S * b + S, b, :], mbk[1][S * b:S * b + S, 0:D], ACT.Copy).then_inc(act_s.sem, 1)

            def self_qk(u):
                act.wait_ge(pe_x.sem, pe_x.done(u, "qkT"))
                A(qk2[:].rearrange("p k c n -> p (k c n)"), mbk[0][:], ACT.Copy).then_inc(act_s.sem, 1)

            def self_exp(u):
                act.wait_ge(dve_s.sem, dve_s.done(u, "sub"))
                A(ex[:], sc[:], ACT.Exp).then_inc(act_s.sem, 1)

            def body(t, u, w):
                if t is not None:
                    queries(t)
                    for i in range(6):
                        keys(t, i)
                    values(t, 0)
                for p in range(9):
                    if t is not None:
                        if p < 8:
                            exps(t, 2 * p)
                            exps(t, 2 * p + 1)
                            if p % 2 == 0 and p // 2 + 1 < BT:
                                values(t, p // 2 + 1)
                        if p >= 1:
                            turn(t, p - 1)
                        if p == 5 and (not isinstance(t, int) or t < TILES - 1):
                            context(t + 1)
                    if u is not None and p == 1:
                        self_v(u)
                    if u is not None and p == 3:
                        self_qk(u)
                    if w is not None and p == 3:
                        act.wait_ge(dve_g.sem, dve_g.done(w, "max"))
                        A(gex[:], mbk[1][:, 0:E], ACT.Exp, bias=gmx[:, 0:1],
                          accum_out=gsm[:, 0:1]).then_inc(act_g.sem, 1)
                    if u is not None and p == 6:
                        self_exp(u)

            tiles(act, body)

            hbk = [sbk[0], sbk[1], sbk[2], ring[0]]

            def weights(r, k, loaded, wh, w):
                act.wait_ge(loaded[k % 2], r * 32 + 16 * (k // 2 + 1))
                A(wh[k % 2], w[k % 2], ACT.Copy).then_inc(act_w.sem, 1)

            def experts(r):
                weights(r, 0, s_w1, w1H, w1s)
                weights(r, 1, s_w1, w1H, w1s)
                for k in range(EQ):
                    for j in range(HC // 2):
                        act.wait_ge(pe_h.sem, pe_h.done(r, f"h{k}{j}"))
                        if k:
                            act.wait_ge(dve_h.sem, dve_h.done(r, f"h{k - 1}{j}"))
                        for h, at in ((hf, 2 * j), (hH[:, k % 2], 2 * j)):
                            A(h[:, at:at + 2, :].rearrange("p j n -> p (j n)"), hbk[j][:], ACT.Gelu
                              ).then_inc(act_h.sem, 1)
                    if 2 <= k + 1 < EQ:
                        weights(r, k + 1, s_w1, w1H, w1s)
                    weights(r, k, s_w2, w2H, w2s)

            with act.Fori(0, E // EQ) as r:
                experts(r)

        @block.gpsimd
        def _(pool):
            pool.wait_ge(pro.sem, pro.done(0, "mv"))
            pool.wait_ge(pro.sem, pro.done(0, "half"))
            pool.tensor_tensor(ve1[:], mv1[:, :, 1], eps[:], ALU.add).then_inc(pro_pool.sem, 1)
            pool.wait_ge(pro_pool.sem, pro_pool.done(0, "var"))
            pool.tensor_tensor(rstd1[:], ve1[:], mhalf[:], ALU.pow).then_inc(pro_pool.sem, 1)
            pool.wait_ge(s_const, 16)
            pool.wait_ge(s_w, 16 * N_W)
            for w2, w in ((wk2, wk), (wv2, wv)):
                pool.tensor_copy(w2[HI], w).then_inc(pro_w.sem, 1)
            pool.wait_ge(pro_vl, 1)
            pool.wait_ge(pro_w.sem, pro_w.done(0, "hv"))
            for w2, w in ((wk2, wk), (wv2, wv)):
                pool.tensor_tensor(w2[LO], w, f32(w2[HI]), ALU.subtract).then_inc(pro_w.sem, 1)

            def context(t, c):
                pool.wait_ge(act_c.sem, act_c.done(t, f"hi{c}"))
                pool.tensor_tensor(ctx2[LO][:, c], ctxT[:, c], f32(ctxH[:, c]), ALU.subtract).then_inc(pool_c.sem, 1)

            for c in range(C):
                context(0, c)

            def block_diagonal(dst, src, sig):
                pool.tensor_tensor(dst.rearrange("p b (h q) -> p b h q", h=8),
                                   over(src.rearrange("p (b q) -> p b q", b=BT), 8, 2),
                                   over(over(k_("headmask"), BT, 1), S, 3), ALU.mult).then_inc(sig.sem, 1)

            def queries(t):
                if later(t):
                    pool.wait_ge(pe_s.sem, pe_s.whole(t))
                pool.wait_ge(act_q.sem, act_q.done(t, "hi"))
                for c in range(C):
                    block_diagonal(qblkH[:, c], f32(qtH[:, c]), pool_q)
                pool.tensor_tensor(qtL, qT[:, :, bass.ds(t * P, P)], f32(qtH), ALU.subtract).then_inc(pool_q.sem, 1)
                for c in range(C):
                    pool.wait_ge(pool_q.sem, pool_q.done(t, "lo"))
                    block_diagonal(qblkL[:, c], qtL[:, c], pool_q)

            def last(t, i):
                b, g, p = i // G, i % G, i // 2
                pool.wait_ge(act_exp.sem, act_exp.done(t, f"e{i}"))
                if i == 0:
                    if later(t):
                        pool.wait_ge(pe_e.sem, pe_e.whole(t))
                pool.tensor_tensor(rep_p[:, g, b * S:(b + 1) * S], k_("rep"),
                                   probs[:, p % 2, i % 2, KEYS - 1:KEYS].broadcast_to([P, S]), ALU.mult
                                   ).then_inc(pool_last.sem, 1)

            def before(w):
                pool.wait_ge(dve_g.sem, dve_g.done(w, "gt"))
                pool.tensor_tensor(cgt[:], cgt[:], over(k_("after"), E, 1), ALU.mult).then_inc(pool_g.sem, 1)
                pool.wait_ge(dve_g.sem, dve_g.done(w, "ge"))
                pool.tensor_tensor(cge[:], cge[:], over(k_("before"), E, 1), ALU.mult).then_inc(pool_g.sem, 1)
                pool.wait_ge(pool_g.sem, pool_g.done(w, "ge_m"))
                pool.tensor_tensor(cgt[:], cgt[:], cge[:], ALU.add).then_inc(pool_g.sem, 1)

            def repeat(t):
                pool.wait_ge(dve_r.sem, dve_r.done(t, "rinv"))
                pool.tensor_tensor(rep_r[:].rearrange("p g (b q) -> p (g b) q", b=BT), over(k_("rep"), G * BT, 1),
                                   over(rinv[:].rearrange("p g b -> p (g b)"), S, 2), ALU.mult
                                   ).then_inc(pool_e.sem, 1)

            def body(t, u, w):
                if u is not None:
                    repeat(u)
                if t is not None:
                    queries(t)
                if w is not None:
                    pool.wait_ge(dve_g.sem, dve_g.done(w, "aggr"))
                    pool.tensor_tensor(ve[:, 1:2], mv[:, 1, 1:2], eps[:, 0:1], ALU.add).then_inc(pool_g.sem, 1)
                    pool.wait_ge(pool_g.sem, pool_g.done(w, "var"))
                    pool.tensor_tensor(rstd[:, 1:2], ve[:, 1:2], mhalf[:, 0:1], ALU.pow).then_inc(pool_g.sem, 1)
                if u is not None:
                    pool.wait_ge(dve_a.sem, dve_a.done(u, "x1"))
                    pool.tensor_tensor(x1b[:], x1[:], bo_b[:, 1, :], ALU.add).then_inc(pool_s.sem, 1)
                    pool.wait_ge(dve_s.sem, dve_s.done(u, "aggr"))
                    pool.tensor_tensor(ve[:, 0:1], mv[:, 0, 1:2], eps[:, 0:1], ALU.add).then_inc(pool_s.sem, 1)
                    pool.wait_ge(pool_s.sem, pool_s.done(u, "var"))
                    pool.tensor_tensor(rstd[:, 0:1], ve[:, 0:1], mhalf[:, 0:1], ALU.pow).then_inc(pool_s.sem, 1)
                for p in range(8):
                    if t is not None:
                        last(t, 2 * p)
                        last(t, 2 * p + 1)
                        if not isinstance(t, int) or t < TILES - 1:
                            if p in (5, 6):
                                context(t + 1, p - 5)
                    if w is not None and p == 4:
                        before(w)
                    if u is not None and p == 3:
                        pool.wait_ge(act_s.sem, act_s.done(u, "qk"))
                        for c in range(C):
                            block_diagonal(kblk[:, c], qk2[:, 1, c, :], pool_s)

            tiles(pool, body)

            with pool.Fori(0, E // EQ) as r:
                pool.wait_ge(act_w.sem, act_w.done(r, "w10"))
                pool.tensor_tensor(w1L[0], w1s[0], f32(w1H[0]), ALU.subtract).then_inc(pool_w.sem, 1)
                hi = slice(HC // 2, HC)
                for k in range(EQ):
                    pool.wait_ge(act_w.sem, act_w.done(r, f"w2{k}"))
                    pool.tensor_tensor(w2L[k % 2][:, hi], w2s[k % 2][:, hi], f32(w2H[k % 2][:, hi]), ALU.subtract
                                       ).then_inc(pool_w.sem, 1)

        @block.vector
        def _(dve):
            TT, TS, RED = dve.tensor_tensor, dve.tensor_scalar, dve.tensor_reduce
            dve.wait_ge(s_mask, 16)
            TS(mask_f[:], mask_i[:], 0.0, -3e38, ALU.is_equal, ALU.mult).then_inc(pro.sem, 1)
            dve.wait_ge(pro.sem, pro.done(0, "mask0"))
            TS(mask_b[:], mask_f[:], 4.0, None, ALU.mult).then_inc(pro.sem, 1)
            dve.memset(mrow[:], 0.0).then_inc(pro.sem, 1)
            dve.memset(row0[:], 0.0).then_inc(pro.sem, 1)
            dve.wait_ge(pro.sem, pro.done(0, "row0"))
            dve.memset(row0[0:1, :], 1.0).then_inc(pro.sem, 1)
            dve.memset(mhalf[:], -0.5).then_inc(pro.sem, 1)
            dve.memset(eps[:], EPS).then_inc(pro.sem, 1)
            dve.wait_ge(s_const, 16)
            for pad in (kTH[:, :, KB:], kTL[:, :, KB:]):
                TS(pad, k_("headmask").rearrange("p (c n) -> p c n", c=C), 0.0, None, ALU.mult).then_inc(pro.sem, 1)
            dve.wait_ge(s_w, 16 * N_W)
            TS(bqs[:], cols[:, 0, :], 0.25, None, ALU.mult).then_inc(pro.sem, 1)
            dve.memset(vz[:], 0.0).then_inc(pro.sem, 1)
            dve.wait_ge(s_x, 16)
            for t in range(TILES):
                i = dve.bn_stats(st1[:, t, :], x_all[:, t, :])
            i.then_inc(pro.sem, 1)
            dve.wait_ge(pro.sem, pro.done(0, "st"))
            for t in range(TILES):
                i = dve.bn_aggr(mv1[:, t, :], st1[:, t, :])
            i.then_inc(pro.sem, 1)
            dve.wait_ge(pro.sem, pro.done(0, "mv"))
            dve.wait_ge(pro_pool.sem, pro_pool.done(0, "rstd"))
            dve.wait_ge(s_const, 16)

            def first_xT(t):
                dve.wait_ge(pro_t.sem, pro_t.done(t, "t"))
                dve.tensor_copy(xT1[:, :, t * P:(t + 1) * P],
                                mbk[t % 2][:, 0:D].rearrange("p (c n) -> p c n", c=C)).then_inc(pro_xT.sem, 1)

            for t in range(TILES):
                if t >= 2:
                    dve.wait_ge(pro_t.sem, pro_t.done(t - 2, "t"))
                TS(xn1[:, t % 2, :], x_all[:, t, :], mv1[:, t, 0:1], rstd1[:, t:t + 1], ALU.subtract, ALU.mult
                   ).then_inc(pro_xn.sem, 1)
                if t:
                    first_xT(t - 1)
            first_xT(TILES - 1)
            dve.wait_ge(pro_vl, 1)
            dve.tensor_copy(vlast[:].rearrange("p t c b -> p c t b"),
                            ring[0][:, 0:C * B].rearrange("p (c t b) -> p c t b", c=C, b=BT)).then_inc(pro_vle, 1)
            dve.wait_ge(pro_xn.sem, pro_xn.done(TILES - 1, "xn"))
            for t in range(TILES):
                TT(x_all[:, t, :], x_all[:, t, :], bo_b[:, 0, :], ALU.add).then_inc(pro_xbo.sem, 1)
            dve.wait_ge(pro_xbo.sem, pro_xbo.done(TILES - 1, "x"))
            dve.wait_ge(pro_vle, 1)
            diag = over(k_("diag"), 4, 1)

            def keys(t, i):
                dve.wait_ge(act_k.sem, act_k.done(t, f"k{i}"))
                if i == 0 and later(t):
                    dve.wait_ge(pe_s.sem, pe_s.whole(t))
                c, (o, n) = i // 3, PIECES[i % 3]
                dve.scalar_tensor_tensor(kT2[LO][:, c, o:o + n], ring_bank(dve_k, f"k{i}")[:, 0:n],
                                         cols[:, 1, c:c + 1], f32(kTH[:, c, o:o + n]), ALU.add, ALU.subtract
                                         ).then_inc(dve_k.sem, 1)

            def maxima(t, i):
                dve.wait_ge(pe_s.sem, pe_s.done(t, f"s{i}"))
                RED(nmax[:, i:i + 1], sbk[i % 3][:, 0:KEYS], X, ALU.max, negate=True).then_inc(dve_max.sem, 1)

            def heads(t, half):
                if half:
                    dve.wait_ge(dve_o.sem, dve_o.done(t, "sum0"))
                else:
                    if later(t):
                        dve.wait_ge(dve_a.sem, dve_a.whole(t))
                dve.wait_ge(pe_o.sem, pe_o.done(t, f"o{4 * half + 3}"))
                TT(masked[:].rearrange("p (m n) -> p m n", m=4), obk[:].rearrange("p (m n) -> p m n", m=4), diag,
                   ALU.mult).then_inc(dve_o.sem, 1)

            def heads_sum(t, half):
                dve.wait_ge(dve_o.sem, dve_o.done(t, f"mask{half}"))
                RED(att_u[:, half].rearrange("p c (b q) -> p (c b) q", b=2),
                    masked[:].rearrange("p (m h q) -> p m q h", m=4, h=HG), X, ALU.add).then_inc(dve_o.sem, 1)

            def cross_att(t):
                n = 2 * P
                m8 = masked[:, 0:n].rearrange("p (cb q) -> p cb q", q=S)
                dve.wait_ge(dve_o.sem, dve_o.done(t, "sum1"))
                dve.wait_ge(pe_e.sem, pe_e.done(t, "expanded"))
                TT(m8, obk[:, n:2 * n].rearrange("p (cb q) -> p cb q", q=S),
                   over(vlast[:, t].rearrange("p c b -> p (c b)") if isinstance(t, int) else
                        vlast[:, bass.ds(t, 1)].rearrange("p t c b -> p (t c b)"), S, 2), ALU.mult).then_inc(dve_a.sem, 1)
                dve.wait_ge(dve_a.sem, dve_a.done(t, "last"))
                m4 = masked[:, 0:n].rearrange("p (c h n) -> p c h n", c=C, h=2)
                TT(m4, m4, att_u[:].rearrange("p h c n -> p c h n"), ALU.add).then_inc(dve_a.sem, 1)
                dve.wait_ge(dve_a.sem, dve_a.done(t, "plus"))
                TT(masked[:, 0:n], obk[:, 0:n], masked[:, 0:n], ALU.mult).then_inc(dve_a.sem, 1)
                dve.wait_ge(dve_a.sem, dve_a.done(t, "norm"))
                TT(att[:], masked[:, 0:n].rearrange("p (c n) -> p c n", c=C), over(cols[:, 2, :], P, 2), ALU.add
                   ).then_inc(dve_a.sem, 1)

            def cross_x1(t):
                dve.wait_ge(pe_e.sem, pe_e.done(t, "projected"))
                TT(x1[:], obk[:, 0:D], x_all[:, t, :] if isinstance(t, int) else
                   x_all[:, bass.ds(t, 1), :].rearrange("p t n -> p (t n)"), ALU.add).then_inc(dve_a.sem, 1)

            def norm(sig, t, src, made, at, dst, k, pool_sig):
                dve.wait_ge(made, at)
                dve.bn_stats(st[:, k, :], src).then_inc(sig.sem, 1)
                dve.wait_ge(sig.sem, sig.done(t, "stats"))
                dve.memset(hold[:], 0.0)
                dve.bn_aggr(mv[:, k, :], st[:, k, :]).then_inc(sig.sem, 1)
                dve.wait_ge(pool_sig.sem, pool_sig.done(t, "rstd"))
                dve.wait_ge(sig.sem, sig.done(t, "aggr"))
                TS(dst, src, mv[:, k, 0:1], rstd[:, k:k + 1], ALU.subtract, ALU.mult).then_inc(sig.sem, 1)

            def self_xT(u):
                dve.wait_ge(pe_x.sem, pe_x.done(u, "xT"))
                dve.tensor_copy(xT2[:].rearrange("p c n -> p (c n)"), mbk[1][:, 0:D]).then_inc(dve_s.sem, 1)

            def self_rope(u):
                dve.wait_ge(pe_x.sem, pe_x.done(u, "qk"))
                heads2 = 2 * H
                m = mbk[0][:].rearrange("p (n d) -> p n d", d=DK)
                TT(rot_a[:].rearrange("p (n d) -> p n d", d=DK), m, over(k_("cos"), heads2, 1), ALU.mult
                   ).then_inc(dve_s.sem, 1)
                m2, r2 = (y[:].rearrange("p (n d two) -> p two n d", two=2, d=DK // 2) for y in (mbk[0], rot_b))
                sin2 = k_("sin").rearrange("p (d two) -> p two d", two=2)
                for z in range(2):
                    TT(r2[:, z], m2[:, 1 - z], over(sin2[:, z], heads2, 1), ALU.mult).then_inc(dve_s.sem, 1)
                dve.wait_ge(dve_s.sem, dve_s.done(u, "sin1"))
                TT(rot_a[:], rot_a[:], rot_b[:], ALU.add).then_inc(dve_s.sem, 1)

            def self_softmax_a(u):
                dve.wait_ge(pe_x.sem, pe_x.done(u, "scores"))
                dve.scalar_tensor_tensor(sc[:], mbk[0][:].rearrange("p (h k) -> p h k", h=H), 1.0 / DK,
                                         over(k_("causal"), H, 1), ALU.mult, ALU.add).then_inc(dve_s.sem, 1)
                dve.wait_ge(dve_s.sem, dve_s.done(u, "scaled"))
                RED(mx2[:], sc[:], X, ALU.max).then_inc(dve_s.sem, 1)

            def self_less_max(u):
                dve.wait_ge(dve_s.sem, dve_s.done(u, "max"))
                TT(sc[:], sc[:], over(mx2[:], S, 2), ALU.subtract).then_inc(dve_s.sem, 1)

            def self_softmax_b(u):
                dve.wait_ge(act_s.sem, act_s.done(u, "exp"))
                RED(sm2[:], ex[:], X, ALU.add).then_inc(dve_s.sem, 1)
                dve.wait_ge(dve_s.sem, dve_s.done(u, "sum"))
                dve.reciprocal(ri2[:], sm2[:]).then_inc(dve_s.sem, 1)
                dve.wait_ge(dve_s.sem, dve_s.done(u, "rinv"))
                TT(pn[:].rearrange("p (h k) -> p h k", h=H), ex[:], over(ri2[:], S, 2), ALU.mult
                   ).then_inc(dve_s.sem, 1)
                dve.wait_ge(dve_s.sem, dve_s.done(u, "probs"))
                dve.transpose(pT2[:], pn[:]).then_inc(dve_s.sem, 1)

            def self_heads(u):
                dve.wait_ge(pe_x.sem, pe_x.done(u, "pv"))
                for c in range(C):
                    TT(masked2[:, c].rearrange("p (b n) -> p b n", b=BT), mbk[c][:].rearrange("p (b n) -> p b n", b=BT),
                       diag, ALU.mult).then_inc(dve_s.sem, 1)

            def self_heads_sum(u):
                for c in range(C):
                    dve.wait_ge(dve_s.sem, dve_s.done(u, f"mask{c}"))
                    RED(att2[:, c].rearrange("p (b q) -> p b q", b=BT),
                        masked2[:, c].rearrange("p (b h q) -> p b q h", b=BT, h=HG), X, ALU.add).then_inc(dve_s.sem, 1)

            def self_end(u):
                dve.wait_ge(pe_x.sem, pe_x.done(u, "projected"))
                dve.wait_ge(pool_s.sem, pool_s.done(u, "x1b"))
                TT(x2[:], mbk[0][:, 0:D], x1b[:], ALU.add).then_inc(dve_s.sem, 1)
                dve.wait_ge(dve_s.sem, dve_s.done(u, "x2"))
                TS(x_all[:, bass.ds(u, 1), :].rearrange("p t n -> p (t n)"), x2[:], 1.0, None, ALU.mult).then_inc(dve_s.sem, 1)

            def route_max(w):
                dve.wait_ge(pe_g.sem, pe_g.done(w, "logits"))
                RED(gmx[:], mbk[1][:, 0:E], X, ALU.max, negate=True).then_inc(dve_g.sem, 1)

            def route_p(w):
                dve.wait_ge(act_g.sem, act_g.done(w, "exp"))
                dve.reciprocal(gri[:], gsm[:]).then_inc(dve_g.sem, 1)
                dve.wait_ge(dve_g.sem, dve_g.done(w, "rinv"))
                TS(gp[:], gex[:], gri[:, 0:1], None, ALU.mult).then_inc(dve_g.sem, 1)
                dve.wait_ge(dve_g.sem, dve_g.done(w, "p"))
                TT(dsp[:], over(gp[:], S, 2), over(k_("rep"), E, 1), ALU.mult).then_inc(dve_g.sem, 1)

            def route_rank(w):
                dve.wait_ge(pe_g.sem, pe_g.done(w, "others"))
                m = mbk[1][:, 0:E * S].rearrange("p (e s) -> p e s", e=E)
                TT(cgt[:], m, over(gp[:], S, 2), ALU.is_gt).then_inc(dve_g.sem, 1)
                TT(cge[:], m, over(gp[:], S, 2), ALU.is_ge).then_inc(dve_g.sem, 1)

            def route_sel(w):
                dve.wait_ge(pool_g.sem, pool_g.done(w, "both"))
                RED(rank[:], cgt[:], X, ALU.add).then_inc(dve_g.sem, 1)
                dve.wait_ge(dve_g.sem, dve_g.done(w, "rank"))
                TT(sel[:], over(rank[:], BT * CAP, 2), over(k_("code"), E, 1), ALU.is_equal).then_inc(dve_g.sem, 1)
                dve.wait_ge(dve_g.sem, dve_g.done(w, "sel"))
                TT(selw[:], sel[:], over(gp[:], BT * CAP, 2), ALU.mult).then_inc(dve_g.sem, 1)

            def route_keep(w):
                n = BT * CAP
                xh, xl = (x[:, :, :, bass.ds(w * n, n)].rearrange("p c e n -> p (c e) n") for x in xin2)
                x = mbk[1][:].rearrange("p (ce s) -> p ce s", s=n)
                dve.wait_ge(pe_g.sem, pe_g.done(w, f"xin{C - 1}"))
                dve.tensor_copy(xh, x).then_inc(dve_g.sem, 1)
                dve.wait_ge(dve_g.sem, dve_g.done(w, "xinH"))
                TT(xl, x, f32(xh), ALU.subtract).then_inc(dve_g.sem, 1)
                dve.wait_ge(pe_g.sem, pe_g.done(w, "selT"))
                dve.tensor_copy(selT[:, bass.ds(w, 1)].rearrange("p t k n -> p (t k n)"), mbk[0][:, 0:2 * P]
                                ).then_inc(dve_g.sem, 1)

            def body(t, u, w):
                if u is not None:
                    heads(u, 1)
                if t is not None:
                    keys(t, 0)
                if u is not None:
                    heads_sum(u, 1)
                if w is not None:
                    self_heads(w)
                if t is not None:
                    keys(t, 1)
                if w is not None:
                    self_heads_sum(w)
                if t is not None:
                    keys(t, 2)
                if u is not None:
                    cross_att(u)
                if t is not None:
                    keys(t, 3)
                if w is not None:
                    self_end(w)
                if t is not None:
                    keys(t, 4)
                if w is not None:
                    norm(dve_g, w, x2[:], dve_s.sem, dve_s.done(w, "x2"), xn3[:], 1, pool_g)
                if t is not None:
                    keys(t, 5)
                if u is not None:
                    cross_x1(u)
                    norm(dve_s, u, x1[:], dve_a.sem, dve_a.done(u, "x1"), xn[:], 0, pool_s)
                for p in range(9):
                    if t is not None and p < 8:
                        maxima(t, 2 * p)
                        maxima(t, 2 * p + 1)
                    if w is not None and p == 0:
                        dve.wait_ge(pe_g.sem, pe_g.done(w, "xT"))
                        dve.tensor_copy(xT3[:].rearrange("p c n -> p (c n)"), mbk[0][:, 0:D]).then_inc(dve_g.sem, 1)
                    if u is not None and p == 0:
                        self_xT(u)
                    if u is not None and p == 2:
                        self_rope(u)
                    if w is not None and p == 2:
                        route_max(w)
                    if w is not None and p == 3:
                        route_p(w)
                    if w is not None and p == 4:
                        route_rank(w)
                    if u is not None and p == 5:
                        self_softmax_a(u)
                    if t is not None and p == 5:
                        heads(t, 0)
                    if u is not None and p == 6:
                        self_less_max(u)
                    if w is not None and p == 6:
                        route_sel(w)
                    if t is not None and p == 6:
                        heads_sum(t, 0)
                    if w is not None and p == 7:
                        route_keep(w)
                    if u is not None and p == 7:
                        self_softmax_b(u)
                    if t is not None and p == 8:
                        dve.wait_ge(act_exp.sem, act_exp.done(t, f"e{H - 1}"))
                        dve.reciprocal(rinv[:], rsum[:]).then_inc(dve_r.sem, 1)

            tiles(dve, body)

            dve.memset(hold[:], 0.0).then_inc(dve_y.sem, dve_y.base)

            def weights1(r, k):
                dve.wait_ge(act_w.sem, act_w.done(r, f"w1{k}"))
                TT(w1L[k % 2], w1s[k % 2], f32(w1H[k % 2]), ALU.subtract).then_inc(dve_w.sem, 1)

            def weights2(r, k):
                dve.wait_ge(act_w.sem, act_w.done(r, f"w2{k}"))
                lo = slice(0, HC // 2)
                TT(w2L[k % 2][:, lo], w2s[k % 2][:, lo], f32(w2H[k % 2][:, lo]), ALU.subtract).then_inc(dve_w.sem, 1)

            def results(r, k):
                dve.wait_ge(pe_y.sem, pe_y.done(r, f"y{k}"))
                for q in range(BT):
                    src = mbk[k % 2][S * q:S * q + S, :].rearrange("p (h n) -> p h n", h=2)
                    dst = ys[S * k:S * k + S, q::BT, bass.ds(r, 1), :].rearrange("p h r n -> p h (r n)")
                    dve.tensor_copy(dst, src).then_inc(dve_y.sem, 1)

            def experts(r):
                weights1(r, 1)
                for k in range(EQ):
                    for j in range(HC // 2):
                        dve.wait_ge(act_h.sem, act_h.done(r, f"h{k}{j}"))
                        at = slice(2 * j, 2 * j + 2)
                        TT(hL[k % 2][:, at], hf[:, at], f32(hH[:, k % 2, at]), ALU.subtract).then_inc(dve_h.sem, 1)
                    if 2 <= k + 1 < EQ:
                        weights1(r, k + 1)
                    weights2(r, k)
                    if k:
                        results(r, k - 1)
                results(r, EQ - 1)

            with dve.Fori(0, E // EQ) as r:
                experts(r)
            for t in range(TILES):
                dve.wait_ge(pe_f.sem, pe_f.done(t, "f"))
                if t >= 2:
                    dve.wait_ge(s_out[t % 2], 16 * (t // 2))
                TT(fin[:, t % 2, :], mbk[t % 2][:, 0:D], x_all[:, t, :], ALU.add).then_inc(dve_f.sem, 1)


def kernel(**inputs):
    import concourse.bacc as bacc
    from concourse.bass_utils import run_bass_kernel_spmd as run

    i = {k: np.asarray(v) for k, v in inputs.items()}
    ctx = i["ctx_1024"]
    T = lambda n: np.ascontiguousarray(i[n].T)
    ctx_t = ctx.reshape(TILES, BT * KEYS, D)
    arrays = {
        "consts": tables(),
        "mask": np.ascontiguousarray(i["mask_Bx1x1xS2_if1"].reshape(B, KEYS)),
        "x": np.ascontiguousarray(i["x"].reshape(B * S, D)),
        "wq": T("L0_xattn_Wq"), "wk": T("L0_xattn_Wk"), "wv": T("L0_xattn_Wv"), "wo": T("L0_xattn_Wo"),
        "wqkv": np.ascontiguousarray(np.concatenate([i["L0_attn_Wq"], i["L0_attn_Wk"], i["L0_attn_Wv"]], axis=0).T),
        "wo2": T("L0_attn_Wo"),
        "gate": np.ascontiguousarray(i["L0_ffn_gate_w"]),
        "ctx_last": np.ascontiguousarray(ctx[:, KEYS - 1, :].T),
        "cols": np.ascontiguousarray(np.concatenate(
            [i[n].reshape(C, P).T for n in ("L0_xattn_bq", "L0_xattn_bk", "L0_xattn_bv")], axis=1)),
        "bo": np.ascontiguousarray(np.stack([i["L0_xattn_bo"], i["L0_attn_bo"]])),
        "ctxT": np.ascontiguousarray(ctx_t.transpose(0, 2, 1)),
        "w1": np.ascontiguousarray(i["L0_ffn_w1"]),
        "w2": np.ascontiguousarray(i["L0_ffn_w2"]),
    }
    nc = bacc.Bacc("TRN2", target_bir_lowering=False, num_devices=1)
    a = {n: nc.dram_tensor(f"in_{n}", v.shape, mybir.dt.from_np(v.dtype), kind="ExternalInput").ap()
         for n, v in arrays.items()}
    a["mask_terms"] = nc.dram_tensor("mask_terms", [B, KEYS], BF16, kind="Internal").ap()
    out = nc.dram_tensor("out", [B * S, D], F32, kind="ExternalOutput").ap()
    perceiver(nc, a, out)
    r = run(nc, [{f"in_{n}": v for n, v in arrays.items()}], core_ids=[0])
    return r.results[0]["out"].reshape(B, S, D)
```

```python
from contextlib import ExitStack

import concourse.bass as bass
from concourse import mybir
import numpy as np

ALU = mybir.AluOpType
ACT = mybir.ActivationFunctionType
F32 = mybir.dt.float32
F32R = mybir.dt.float32r
BF16 = mybir.dt.bfloat16
I32 = mybir.dt.int32
X = mybir.AxisListType.X

B, S, D = 32, 32, 256
KEYS = 257
H, DK = 16, 16
E, CAP, HID = 8, 8, 1024
EPS = 1e-5
P = 128
BT = P // S
TILES = B // BT
C = D // P
G = 4
HG = H // G
KB = BT * KEYS
KT = (KEYS - 1) // P
KW = KB + 8 // C
SW = KEYS + 1
PIECES = [(0, 344), (344, 342), (686, 342)]
HC = HID // P
NEG = -10000.0

CONSTS = [("ident", P), ("headmask", 8), ("diag", P), ("expand", HG * DK), ("rep", S), ("cos", DK), ("sin", DK),
          ("causal", S), ("batch_ones", P), ("code", BT * CAP), ("before", S), ("after", S)]
OFF = {}
_o = 0
for _n, _w in CONSTS:
    OFF[_n] = (_o, _o + _w)
    _o += _w
NCONST = _o


def tables():
    p = np.arange(P)
    q = p % S
    a = {}
    a["ident"] = np.eye(P)
    a["headmask"] = (p[:, None] // DK == np.arange(8)[None])
    a["diag"] = ((p[:, None] % 64) // DK == np.arange(P)[None] // S)
    a["expand"] = (p[:, None] // S == np.arange(HG * DK)[None] // DK)
    a["rep"] = (q[:, None] == np.arange(S)[None])
    inv = np.float32(1.0) / np.float32(10000.0) ** (np.arange(0, DK, 2, dtype=np.float32) / np.float32(DK))
    ang = (q.astype(np.float32)[:, None] * inv[None]).astype(np.float32)
    a["cos"] = np.repeat(np.cos(ang), 2, axis=1)
    sign = np.where(np.arange(DK) % 2 == 0, -1.0, 1.0)
    a["sin"] = np.repeat(np.sin(ang), 2, axis=1) * sign
    a["causal"] = np.where(q[:, None] >= np.arange(S)[None], 0.0, NEG)
    a["batch_ones"] = (p[:, None] // S == p[None] // S)
    j = np.arange(BT * CAP)
    a["code"] = np.where(p[:, None] // S == j[None] // CAP, j[None] % CAP, -1)
    a["before"] = (np.arange(S)[None] < q[:, None])
    a["after"] = (np.arange(S)[None] > q[:, None])
    return np.concatenate([np.asarray(a[n], np.float32) for n, _ in CONSTS], axis=1)


class Sig:

    def __init__(self, sem, steps, base=0):
        self.sem, self.n, self.base = sem, len(steps), base
        self.at = {s: k + 1 for k, s in enumerate(steps)}

    def done(self, t, step):
        return t * self.n + (self.base + self.at[step])

    def whole(self, t):
        return t * self.n + self.base


HI, LO = 0, 1
LAST_ORDER = [q + BT * h for q in range(BT) for h in range(2)]
PASSES = ((LO, HI), (HI, LO), (HI, HI))


def later(t):
    return not (isinstance(t, int) and t == 0)


def perceiver(nc, a, out):
    ctx = ExitStack()
    with ctx:
        def sb(name, shape, dt=F32):
            return ctx.enter_context(nc.sbuf_tensor(name, shape, dt))

        def bank(name):
            return ctx.enter_context(nc.psum_tensor(name, [P, 512], F32))

        def sem(name):
            return ctx.enter_context(nc.semaphore(name))

        def sig(name, steps, base=0):
            return Sig(sem(name), steps, base)

        cst = sb("cst", [P, NCONST])

        def k_(name):
            return cst[:, OFF[name][0]:OFF[name][1]]

        gate = sb("gate", [P, C, E])
        cols = sb("cols", [P, 3, C])
        bqs = sb("bqs", [P, C])
        bo_b = sb("bo_b", [P, 2, D])
        mask_b = sb("mask_b", [B, KEYS], BF16)
        row0 = sb("row0", [P, P], BF16)
        mrow = sb("mrow", [P, KW], BF16)
        mhalf = sb("mhalf", [P, TILES])
        eps = sb("eps", [P, TILES])
        x_all = sb("x_all", [P, TILES, D])
        st1 = sb("st1", [P, TILES, 6])
        mv1 = sb("mv1", [P, TILES, 2])
        ve1 = sb("ve1", [P, TILES])
        rstd1 = sb("rstd1", [P, TILES])
        ctx_last = sb("ctx_last", [P, C, B])
        vlast = sb("vlast", [P, TILES, C, BT])
        def room(name, n):
            start = (nc.sbuf_base + 31) // 32 * 32
            sb(name, [P, n])

            def laid(part, k, shape, dt=F32):
                flat = nc.alloc_sbuf_tensor_at(part, [P, int(np.prod(shape))], dt, offset=start + 4 * k)
                names = "abcd"[:len(shape)]
                return flat[:].rearrange(f"p ({' '.join(names)}) -> p {' '.join(names)}", **dict(zip(names, shape)))
            return laid

        NQ = C * BT * 8 * S
        laid = room("tile_room", C * KB + C * KW)
        ctxT = laid("ctxT", 0, [C, KB])
        ctxL = laid("ctxL", 0, [C, KB], F32R)
        kTH = laid("kTH", C * KB, [C, KW], F32R)
        ys = laid("ys", 0, [TILES, 2, D])
        laid = room("block_room", 2 * NQ)
        qblkH = laid("qblkH", 0, [C, BT, 8 * S], F32R)
        kblk = laid("kblk", NQ, [C, BT, 8 * S])
        xT1 = laid("xT1", NQ, [C, TILES * P])
        hH = laid("hH", 0, [2, HC, 2 * P], F32R)
        laid = room("split_room", C * KB + C * KW + NQ)
        ctxH = laid("ctxH", 0, [C, KB], F32R)
        kTL = laid("kTL", C * KB, [C, KW], F32R)
        qblkL = laid("qblkL", C * KB + C * KW, [C, BT, 8 * S], F32R)
        w1s = [laid(f"w1s{i}", i * C * HID, [C, HID]) for i in range(2)]
        w1L = [laid(f"w1L{i}", i * C * HID, [C, HID], F32R) for i in range(2)]
        w2s, w2L = [laid("w2s0", 2 * C * HID, [HC, D])], [laid("w2L0", 2 * C * HID, [HC, D], F32R)]
        laid = room("query_room", C * TILES * P)
        qT = laid("qT", 0, [C, TILES * P])
        w2s.append(laid("w2s1", 0, [HC, D]))
        w2L.append(laid("w2L1", 0, [HC, D], F32R))
        qtH = sb("qtH", [P, C, P], F32R)[:]
        qtL = sb("qtL", [P, C, P])[:]
        laid = room("projection_room", 6 * C * D)
        wq, wo, wo2 = (laid(n, k * C * D, [C, D]) for k, n in enumerate(("wq", "wo", "wo2")))
        wqkv = laid("wqkv", 3 * C * D, [C, 3 * D])
        hf = laid("hf", 0, [HC, 2 * P])
        fin = laid("fin", 0, [TILES, D])
        laid = room("weight_room", 4 * C * D + BT * KT * D)
        wk, wv = (laid(n, k * C * D, [C, D]) for k, n in enumerate(("wk", "wv")))
        wkL, wvL, wkH, wvH = (laid(n, k * C * D, [C, D], F32R) for k, n in enumerate(("wkL", "wvL", "wkH", "wvH")))
        v = laid("v", 4 * C * D, [BT, KT, D])
        wH0 = [laid("w1H0", 0, [C, HID], F32R), laid("w2H0", C * HID, [HC, D], F32R)]

        def f32(ap):
            return ap.bitcast(F32)

        ctx2, wk2, wv2, kT2, qblk2 = (ctxH, ctxL), (wkH, wkL), (wvH, wvL), (kTH, kTL), (qblkH, qblkL)
        nmax = sb("nmax", [P, H])
        rsum = sb("rsum", [P, G, BT])
        rinv = sb("rinv", [P, G, BT])
        laid = room("cross_room", 10 * 512)
        mask_i = laid("mask_i", 0, [KEYS], I32)[0:B]
        mask_f = laid("mask_f", 512, [KEYS])[0:B]
        probs = laid("probs", 0, [2, 2, KEYS])
        pT, k = laid("pT", 1032, [2, 2, KT * P]), 1032 + 4 * KT * P
        masked, k = laid("masked", k, [4 * P]), k + 4 * P
        att_u, k = laid("att_u", k, [2, C, 2 * S]), k + 2 * C * 2 * S
        rep_r, k = laid("rep_r", k, [G, BT * S]), k + G * BT * S
        rep_p, k = laid("rep_p", k, [G, BT * S]), k + G * BT * S
        att = laid("att", k, [C, P])
        wH1 = [laid("w1H1", 0, [C, HID], F32R), laid("w2H1", C * HID, [HC, D], F32R)]
        w1H, w2H = zip(wH0, wH1)
        x1 = sb("x1", [P, D])
        x1b = sb("x1b", [P, D])
        st = sb("st", [P, 2, 6])
        mv = sb("mv", [P, 2, 2])
        ve = sb("ve", [P, 2])
        rstd = sb("rstd", [P, 2])
        x2 = sb("x2", [P, D])
        hold = sb("hold", [P, 1])
        xn = sb("xn", [P, D])
        xT2 = sb("xT2", [P, C, P])
        laid = room("self_room", 4 * D + BT * D + 2 * 4 * P + 4 * H * S)
        rot_a = laid("rot_a", 0, [2 * D])
        rot_b = laid("rot_b", 2 * D, [2 * D])
        vz = laid("vz", 4 * D, [BT, D])
        masked2 = laid("masked2", 4 * D + BT * D, [2, 4 * P])
        sc, ex = (laid(n, (6 + k) * 512, [H, S]) for k, n in enumerate(("sc", "ex")))
        pn, pT2 = (laid(n, (8 + k) * 512, [H * S]) for k, n in enumerate(("pn", "pT2")))
        xn1 = laid("xn1", 4 * D + BT * D, [2, D])
        hL = [laid(f"hL{k}", (1 + 4 * k) * 512, [HC, 2 * P], F32R) for k in range(2)]
        qk2 = sb("qk2", [P, 2, C, P])
        mx2 = sb("mx2", [P, H])
        sm2 = sb("sm2", [P, H])
        ri2 = sb("ri2", [P, H])
        att2 = sb("att2", [P, C, P])
        xn3 = sb("xn3", [P, D])
        xT3 = sb("xT3", [P, C, P])
        gmx = sb("gmx", [P, 1])
        gex = sb("gex", [P, E])
        gsm = sb("gsm", [P, 1])
        gri = sb("gri", [P, 1])
        gp = sb("gp", [P, E])
        dsp = sb("dsp", [P, E, S])
        cgt = sb("cgt", [P, E, S])
        cge = sb("cge", [P, E, S])
        rank = sb("rank", [P, E])
        sel = sb("sel", [P, E, BT * CAP])
        selw = sb("selw", [P, E, BT * CAP])
        xin2 = [sb(n, [P, C, E, TILES * BT * CAP], F32R) for n in ("xinH", "xinL")]
        selT = sb("selT", [P, TILES, 2, P])

        sbk = [bank(f"sbk{i}") for i in range(3)]
        ring = [bank(f"ring{i}") for i in range(2)]
        obk = bank("obk")
        mbk = [bank(f"mbk{i}") for i in range(2)]

        s_const, s_w, s_mask = (sem(n) for n in ("s_const", "s_w", "s_mask"))
        s_x = [sem(f"s_x{n}") for n in range(2)]
        s_cols, s_wq, s_wk, s_wv = (sem(n) for n in ("s_cols", "s_wq", "s_wk", "s_wv"))
        s_ctx, s_mrow, s_mst = sem("s_ctx"), sem("s_mrow"), sem("s_mst")
        s_w1, s_w2 = ([sem(f"s_w{j}_{i}") for i in range(2)] for j in (1, 2))
        s_out = sem("s_out")
        N_W = 6

        pro = sig("pro", ["half", "eps", "mrow0", "row0", "row1", "vz0", "mask0", "mask", "pad0", "pad1", "bqs"])
        pro_ln = sig("pro_ln", ["st0", "mv0", "st1", "mv1"])
        pro_pool = sig("pro_pool", ["var0", "rstd0", "var1", "rstd1"])
        pro_xn = sig("pro_xn", ["xn"])
        pro_xT = sig("pro_xT", ["xT"])
        pro_t = sig("pro_t", ["t"])
        pro_q = sig("pro_q", ["q00", "q01", "q10", "q11"])
        pro_qe = sig("pro_qe", ["q00", "q01", "q10", "q11"])
        pro_wh = sig("pro_wh", ["k", "v"])
        pro_wl = sig("pro_wl", ["k", "v"])
        act_c = sig("act_c", ["hi0", "hi1"])
        pool_c = sig("pool_c", ["lo0", "lo1"])
        pro_vl = sem("pro_vl")
        pro_vle = sem("pro_vle")
        pro_xbo = sem("pro_xbo")

        pe_k = sig("pe_k", [f"k{i}" for i in range(6)])
        pe_v = sig("pe_v", [f"v{b}" for b in range(BT)])
        act_k = sig("act_k", [f"k{i}" for i in range(6)])
        dve_k = sig("dve_k", [f"k{i}" for i in range(6)])
        act_v = sig("act_v", [f"v{b}" for b in range(BT)])
        act_q = sig("act_q", ["hi"])
        pool_q = sig("pool_q", [f"q{HI}{c}" for c in range(C)] + ["lo"] + [f"q{LO}{c}" for c in range(C)])
        pe_s = sig("pe_s", [f"s{i}" for i in range(H)])
        dve_max = sig("dve_max", [f"m{i}" for i in range(H)])
        act_exp = sig("act_exp", [f"e{i}" for i in range(H)])
        pool_last = sig("pool_last", [f"l{i}" for i in range(H)])
        pe_t = sig("pe_t", [f"t{p}" for p in range(8)])
        act_t = sig("act_t", [f"t{p}" for p in range(8)])
        pe_o = sig("pe_o", [f"o{p}" for p in range(8)])
        dve_o = sig("dve_o", ["mask0", "sum0", "mask1", "sum1"])
        dve_r = sig("dve_r", ["rinv"])
        pool_e = sig("pool_e", ["rep_r"])
        pe_e = sig("pe_e", ["expanded", "projected"])
        dve_a = sig("dve_a", ["last", "plus", "norm", "att", "x1"])
        dve_s = sig("dve_s", ["stats", "aggr", "xn", "xT", "cos", "sin0", "sin1", "rope", "kblk1", "scaled", "max", "sub",
                              "sum", "rinv", "probs", "turned", "mask0", "mask1", "sum0", "sum1", "x2", "kept"])
        pool_s = sig("pool_s", ["x1b", "var", "rstd", "kblk0"])
        act_s = sig("act_s", ["v0", "v1", "v2", "v3", "qk", "exp"])
        pe_x = sig("pe_x", ["xT", "qk", "v", "qkT", "scores", "pv", "projected"])
        dve_g = sig("dve_g", ["stats", "aggr", "xn", "xT", "max", "rinv", "p", "spread", "gt", "ge", "rank", "sel", "selw", "xinH", "xinL", "selT"])
        pool_g = sig("pool_g", ["var", "rstd", "gt_m", "ge_m", "both"])
        act_g = sig("act_g", ["exp"])
        pe_g = sig("pe_g", ["xT", "logits", "others", "xin0", "xin1", "selT"])
        EQ = 4
        pe_h = sig("pe_h", [f"h{e}{j}" for e in range(EQ) for j in range(HC // 2)])
        act_h = sig("act_h", [f"{z}{e}{j}" for e in range(EQ) for j in range(HC // 2) for z in "fh"])
        dve_h = sig("dve_h", [f"h{e}{j}" for e in range(EQ) for j in range(HC // 2)])
        act_w = sig("act_w", ["w10", "w11", "w20", "w12", "w21", "w13", "w22", "w23"])
        dve_w = sig("dve_w", ["w11", "w20", "w12", "w21", "w13", "w22", "w23"])
        pool_w = sig("pool_w", ["w10", "w11", "w20", "w12", "w21", "w13", "w22", "w23"])
        pe_y = sig("pe_y", [f"y{e}" for e in range(EQ)])
        dve_y = sig("dve_y", [f"y{e}{q}" for e in range(EQ) for q in range(BT)], base=1)
        pe_f = sig("pe_f", ["f"])
        dve_f = sig("dve_f", ["f"])

        uses = [(dve_k, f"k{i}") for i in range(6)] + [(act_v, "v0")]
        for p in range(9):
            if p % 2 == 0 and p // 2 + 1 < BT:
                uses.append((act_v, f"v{p // 2 + 1}"))
            if p >= 1:
                uses.append((act_t, f"t{p - 1}"))
        place = {(id(s), n): u for u, (s, n) in enumerate(uses)}

        def ring_bank(s, n):
            return ring[place[(id(s), n)] % 2]

        def ring_read(t, s, n):
            u = place[(id(s), n)]
            last, step = uses[u - 2]
            return (last.sem, last.done(t if u >= 2 else t - 1, step))

        def over(ap, n, at):
            shape = list(ap.shape)
            ap = ap.unsqueeze(at)
            return ap.broadcast_to(shape[:at] + [n] + shape[at:])

        def output_banks(u):
            return sbk if u is None else [mbk[0], mbk[1], mbk[0]]

        hbk = [sbk[0], sbk[1], sbk[2], ring[0]]

        block = ctx.enter_context(nc.Block())

        def tiles(eng, body):
            body(0, None, None)
            body(1, 0, None)
            with eng.Fori(2, TILES - 1) as t:
                body(t, t - 1, t - 2)
            body(TILES - 1, TILES - 2, TILES - 3)
            body(None, TILES - 1, TILES - 2)
            body(None, None, TILES - 1)

        @block.sync
        def _(sp):
            def weight(dst, n, done):
                sp.dma_start(dst, a[n].rearrange("(c p) n -> p c n", p=P)).then_inc(done, 16)

            def load_x(n):
                half = slice(n * TILES // 2, (n + 1) * TILES // 2)
                sp.dma_start(x_all[:, half], a["x"].rearrange("(t p) d -> p t d", p=P)[:, half]).then_inc(s_x[n], 16)

            ctx_d = a["ctxT"].rearrange("t (c p) n -> t p c n", p=P)
            terms = a["mask_terms"].rearrange("(t b) k -> t (b k)", b=BT)

            def load_context(t):
                if later(t):
                    sp.wait_ge(pe_v.sem, pe_v.whole(t))
                src = ctx_d[t] if isinstance(t, int) else ctx_d[bass.ds(t, 1)].rearrange("t p c n -> (t p) c n")
                sp.dma_start(ctxT, src).then_inc(s_ctx, 16)

            def load_mask(t):
                if later(t):
                    sp.wait_ge(pe_s.sem, pe_s.whole(t))
                sp.dma_start(mrow[0:1, 0:KB], terms[bass.ds(t, 1), :]).then_inc(s_mrow, 16)

            sp.dma_start(mask_i[:], a["mask"]).then_inc(s_mask, 16)
            sp.dma_start(cols[:], a["cols"].rearrange("p (j c) -> p j c", c=C)).then_inc(s_cols, 16)
            load_x(0)
            sp.dma_start(cst[:], a["consts"]).then_inc(s_const, 16)
            load_x(1)
            weight(wq, "wq", s_wq)
            load_context(0)
            weight(wk, "wk", s_wk)
            weight(wv, "wv", s_wv)
            weight(ctx_last[:], "ctx_last", s_wv)
            for j in range(2):
                sp.dma_start(bo_b[:, j, :], a["bo"][j].partition_broadcast(P)).then_inc(s_w, 16)
            sp.wait_ge(pro.sem, pro.done(0, "mask"))
            sp.dma_start(a["mask_terms"], mask_b[:]).then_inc(s_mst, 16)
            sp.wait_ge(s_mst, 16)
            load_mask(0)
            for dst, n in ((wo, "wo"), (wqkv, "wqkv"), (wo2, "wo2"), (gate[:], "gate")):
                weight(dst, n, s_w)

            w1_d, w2_d = (a[n].rearrange("e (c p) n -> e p c n", p=P) for n in ("w1", "w2"))

            def load_w1(e):
                if e >= 2:
                    sp.wait_ge(pe_h.sem, (e - 1) * HC // 2)
                sp.dma_start(w1s[e % 2], w1_d[e]).then_inc(s_w1[e % 2], 16)

            def load_w2(e):
                if e >= 2:
                    sp.wait_ge(pe_y.sem, e - 1)
                sp.dma_start(w2s[e % 2], w2_d[e]).then_inc(s_w2[e % 2], 16)

            with sp.Fori(1, TILES) as t:
                load_context(t)
                load_mask(t)
            sp.wait_ge(pe_s.sem, pe_s.whole(TILES))
            sp.wait_ge(pe_v.sem, pe_v.whole(TILES))
            load_w1(0)
            for e in range(1, E):
                load_w1(e)
                load_w2(e - 1)
            load_w2(E - 1)
            for n, t in enumerate(LAST_ORDER):
                sp.wait_ge(dve_f.sem, dve_f.done(n, "f"))
                sp.dma_start(out[t * P:(t + 1) * P, :], fin[:, t, :]).then_inc(s_out, 16)
            sp.wait_ge(s_out, 16 * TILES)

        @block.tensor
        def _(pe):
            mm = pe.matmul
            ident = k_("ident")
            pe.wait_ge(s_const, 16)

            def turn_x(t):
                pe.wait_ge(pro_xn.sem, pro_xn.done(t, "xn"))
                if t >= 2:
                    pe.wait_ge(pro_xT.sem, pro_xT.done(t - 2, "xT"))
                for c in range(C):
                    m = pe.transpose(mbk[t % 2][:, c * P:(c + 1) * P], xn1[:, t % 2, c * P:(c + 1) * P], ident)
                m.then_inc(pro_t.sem, 1)

            def queries(n):
                pe.wait_ge(s_wq, 16)
                pe.wait_ge(pro_xT.sem, pro_xT.done((n + 1) * TILES // 2 - 1, "xT"))
                for c in range(C):
                    if n:
                        pe.wait_ge(pro_qe.sem, pro_qe.done(0, f"q{n - 1}{c}"))
                    for j in range(C):
                        m = mm(sbk[c][:], wq[:, j, c * P:(c + 1) * P], xT1[:, j, n * 512:(n + 1) * 512],
                               start=(j == 0), stop=(j == C - 1))
                    m.then_inc(pro_q.sem, 1)

            for t in range(TILES // 2):
                turn_x(t)
            queries(0)
            pe.wait_ge(s_wv, 2 * 16)
            for c in range(C):
                for j in range(C):
                    m = mm(obk[:, c * B:(c + 1) * B], wv[:, j, c * P:(c + 1) * P], ctx_last[:, j, :],
                           start=(j == 0), stop=(j == C - 1))
            m.then_inc(pro_vl, 1)
            pe.wait_ge(pro_wl.sem, pro_wl.done(0, "k"))

            def second_queries():
                queries(1)
                pe.wait_ge(pro_vle, 1)
                pe.wait_ge(pro_qe.sem, pro_qe.done(0, "q11"))
                pe.wait_ge(pro.sem, pro.done(0, "row1"))
                pe.wait_ge(pro_wl.sem, pro_wl.done(0, "v"))
                pe.wait_ge(s_w, 16 * N_W)

            def split_product(out, left, right):
                steps = [(l, r, j) for j in range(left[0].shape[1]) for l, r in PASSES]
                for n, (l, r, j) in enumerate(steps):
                    m = mm(out, left[l][:, j], right[r][:, j], start=(n == 0), stop=(n == len(steps) - 1))
                return m

            def keys(t, i):
                if later(t) or i >= 2:
                    pe.wait_ge(*ring_read(t, dve_k, f"k{i}"))
                c, (o, n) = i // 3, PIECES[i % 3]
                split_product(ring_bank(dve_k, f"k{i}")[:, 0:n], [z[:, :, c * P:(c + 1) * P] for z in wk2],
                              [z[:, :, o:o + n] for z in ctx2]).then_inc(pe_k.sem, 1)
                if not later(t) and 1 <= i <= TILES // 2:
                    turn_x(TILES // 2 + i - 1)

            def values(t, b):
                pe.wait_ge(*ring_read(t, act_v, f"v{b}"))
                for kt in range(KT):
                    o = b * KEYS + kt * P
                    m = split_product(ring_bank(act_v, f"v{b}")[:, kt * D:(kt + 1) * D],
                                      [z[:, :, o:o + P] for z in ctx2], wv2)
                m.then_inc(pe_v.sem, 1)

            def scores(t, i):
                b, g = i // G, i % G
                if i >= 3:
                    pe.wait_ge(act_exp.sem, act_exp.done(t, f"e{i - 3}"))
                else:
                    if later(t):
                        pe.wait_ge(act_exp.sem, act_exp.whole(t))
                o, c = sbk[i % 3][:, 0:SW], g // 2
                mm(o, row0[:], mrow[:, b * KEYS:b * KEYS + SW], start=True, stop=False)
                for l, r in PASSES:
                    m = mm(o, qblk2[l][:, c, b, (g % 2) * P:(g % 2 + 1) * P], kT2[r][:, c, b * KEYS:b * KEYS + SW],
                           start=False, stop=((l, r) == PASSES[-1]))
                m.then_inc(pe_s.sem, 1)

            def turn(t, p):
                name = f"t{p}"
                pe.wait_ge(*ring_read(t, act_t, name))
                pe.wait_ge(act_exp.sem, act_exp.done(t, f"e{2 * p + 1}"))
                for gg in range(2):
                    for kt in range(KT):
                        o = (gg * KT + kt) * P
                        m = pe.transpose(ring_bank(act_t, name)[:, o:o + P],
                                         probs[:, p % 2, gg, kt * P:(kt + 1) * P], ident)
                m.then_inc(pe_t.sem, 1)

            def attend(t, p):
                b, c = p // 2, p % 2
                if p == 0:
                    if later(t):
                        pe.wait_ge(dve_a.sem, dve_a.whole(t))
                if p == 4:
                    pe.wait_ge(dve_o.sem, dve_o.done(t, "mask0"))
                pe.wait_ge(act_t.sem, act_t.done(t, f"t{p}"))
                pe.wait_ge(act_v.sem, act_v.done(t, f"v{b}"))
                for gg in range(2):
                    g = 2 * c + gg
                    for kt in range(KT):
                        m = mm(obk[64 * gg:64 * gg + 64, c * 256 + (b % 2) * P:c * 256 + (b % 2 + 1) * P],
                               v[:, b, kt, g * 64:(g + 1) * 64], pT[:, p % 2, gg, kt * P:(kt + 1) * P],
                               start=(kt == 0), stop=(kt == KT - 1))
                m.then_inc(pe_o.sem, 1)

            def expand(t):
                pe.wait_ge(pool_e.sem, pool_e.done(t, "rep_r"))
                pe.wait_ge(pool_last.sem, pool_last.done(t, f"l{H - 1}"))
                pe.wait_ge(dve_o.sem, dve_o.done(t, "mask1"))
                for k, r in enumerate((rep_r, rep_p)):
                    for g in range(G):
                        o = k * 256 + (g // 2) * P
                        m = mm(obk[64 * (g % 2):64 * (g % 2) + 64, o:o + P], k_("expand"), r[:, g, :],
                               start=True, stop=True)
                m.then_inc(pe_e.sem, 1)

            def project(t):
                pe.wait_ge(dve_a.sem, dve_a.done(t, "att"))
                for j in range(C):
                    m = mm(obk[:, 0:D], att[:, j, :], wo[:, j, :], start=(j == 0), stop=(j == C - 1))
                m.then_inc(pe_e.sem, 1)

            def self_xT(u):
                pe.wait_ge(dve_s.sem, dve_s.done(u, "xn"))
                for c in range(C):
                    m = pe.transpose(mbk[1][:, c * P:(c + 1) * P], xn[:, c * P:(c + 1) * P], ident)
                m.then_inc(pe_x.sem, 1)

            def self_qkv(u):
                pe.wait_ge(dve_s.sem, dve_s.done(u, "xT"))
                for o, n, bk in ((0, 512, mbk[0]), (512, D, mbk[1])):
                    for j in range(C):
                        m = mm(bk[:, 0:n], xT2[:, j, :], wqkv[:, j, o:o + n], start=(j == 0), stop=(j == C - 1))
                    m.then_inc(pe_x.sem, 1)

            def self_qkT(u):
                pe.wait_ge(dve_s.sem, dve_s.done(u, "rope"))
                for j in range(4):
                    m = pe.transpose(mbk[0][:, j * P:(j + 1) * P], rot_a[:, j * P:(j + 1) * P], ident)
                m.then_inc(pe_x.sem, 1)

            def self_scores(u):
                pe.wait_ge(act_s.sem, act_s.done(u, "qk"))
                pe.wait_ge(pool_s.sem, pool_s.done(u, "kblk0"))
                pe.wait_ge(dve_s.sem, dve_s.done(u, "kblk1"))
                for b in range(BT):
                    for c in range(C):
                        m = mm(mbk[0][S * b:S * b + S, c * 256:(c + 1) * 256], qk2[:, 0, c, S * b:S * b + S],
                               kblk[:, c, b, :], start=True, stop=True)
                m.then_inc(pe_x.sem, 1)

            def self_attend(u, banks):
                pe.wait_ge(dve_s.sem, dve_s.done(u, "turned"))
                pe.wait_ge(act_s.sem, act_s.done(u, "v3"))
                for g in range(G):
                    for b in range(BT):
                        m = mm(banks[g // 2][64 * (g % 2):64 * (g % 2) + 64, b * P:(b + 1) * P],
                               vz[:, b, g * 64:(g + 1) * 64], pT2[:, g * P:(g + 1) * P], start=True, stop=True)
                m.then_inc(pe_x.sem, 1)

            def self_project(u, banks):
                pe.wait_ge(dve_s.sem, dve_s.done(u, "sum1"))
                for j in range(C):
                    m = mm(banks[2][:, 0:D], att2[:, j, :], wo2[:, j, :], start=(j == 0), stop=(j == C - 1))
                m.then_inc(pe_x.sem, 1)

            def route_xT(w):
                pe.wait_ge(dve_g.sem, dve_g.done(w, "xn"))
                for c in range(C):
                    m = pe.transpose(mbk[0][:, c * P:(c + 1) * P], xn3[:, c * P:(c + 1) * P], ident)
                m.then_inc(pe_g.sem, 1)

            def route_logits(u, w):
                if u is not None:
                    pe.wait_ge(act_s.sem, act_s.done(u, "v3"))
                pe.wait_ge(dve_g.sem, dve_g.done(w, "xT"))
                for j in range(C):
                    m = mm(mbk[1][:, 0:E], xT3[:, j, :], gate[:, j, :], start=(j == 0), stop=(j == C - 1))
                m.then_inc(pe_g.sem, 1)

            def route_others(w):
                pe.wait_ge(dve_g.sem, dve_g.done(w, "spread"))
                mm(mbk[1][:, 0:E * S], k_("batch_ones"), dsp[:].rearrange("p e s -> p (e s)"),
                   start=True, stop=True).then_inc(pe_g.sem, 1)

            def route_gather(u, w):
                pe.wait_ge(dve_g.sem, dve_g.done(w, "selw"))
                for c in range(C):
                    mm(mbk[1][:, c * 256:(c + 1) * 256], xn3[:, c * P:(c + 1) * P],
                       sel[:].rearrange("p e s -> p (e s)"), start=True, stop=True).then_inc(pe_g.sem, 1)
                if u is not None:
                    pe.wait_ge(dve_s.sem, dve_s.done(u, "scaled"))
                flat = selw[:].rearrange("p e s -> p (e s)")
                for k in range(2):
                    m = pe.transpose(mbk[0][:, k * P:(k + 1) * P], flat[:, k * P:(k + 1) * P], ident)
                m.then_inc(pe_g.sem, 1)

            def body(t, u, w):
                if u is not None:
                    attend(u, 7)
                if t is not None:
                    pe.wait_ge(pool_c.sem, pool_c.done(t, "lo1"))
                    keys(t, 0)
                if w is not None:
                    self_attend(w, output_banks(u))
                    if u is None:
                        route_gather(w, w - 1)
                if t is not None:
                    keys(t, 1)
                    keys(t, 2)
                if u is not None:
                    expand(u)
                if t is not None:
                    keys(t, 3)
                if w is not None:
                    self_project(w, output_banks(u))
                if t is not None:
                    keys(t, 4)
                if u is not None:
                    project(u)
                if t is not None:
                    keys(t, 5)
                    if not later(t):
                        second_queries()
                    values(t, 0)
                if w is not None:
                    if u is None:
                        pe.wait_ge(dve_g.sem, dve_g.done(w - 1, "selT"))
                    route_xT(w)
                if t is not None:
                    pe.wait_ge(s_mrow, (t + 1) * 16)
                    pe.wait_ge(pool_q.sem, pool_q.done(t, f"q{LO}{C - 1}"))
                    pe.wait_ge(dve_k.sem, dve_k.done(t, "k5"))
                for p in range(9):
                    if t is not None:
                        if p < 8:
                            scores(t, 2 * p)
                            scores(t, 2 * p + 1)
                            if p % 2 == 0 and p // 2 + 1 < BT:
                                values(t, p // 2 + 1)
                    if u is not None and p == 5:
                        self_scores(u)
                    if w is not None and p == 7 and (t is not None or u is None):
                        route_gather(u, w)
                    if t is not None:
                        if p >= 1:
                            turn(t, p - 1)
                        if p >= 2:
                            attend(t, p - 2)
                    if u is not None and p == 0:
                        self_xT(u)
                    if u is not None and p == 1:
                        if w is not None:
                            pe.wait_ge(dve_g.sem, dve_g.done(w, "xT"))
                        self_qkv(u)
                    if w is not None and p == 2 and t is not None:
                        route_logits(u, w)
                    if u is not None and p == 3:
                        self_qkT(u)
                    if w is not None and p == 3 and t is None:
                        route_logits(u, w)
                    if w is not None and p == 4:
                        route_others(w)
                    if w is not None and p == 8 and t is not None:
                        pe.wait_ge(dve_g.sem, dve_g.done(w, "selT"))

            tiles(pe, body)

            pe.wait_ge(dve_g.sem, dve_g.done(TILES - 1, "selT"))

            def hidden(r, k, e):
                for j in range(HC // 2):
                    if k:
                        pe.wait_ge(act_h.sem, act_h.done(r, f"h{k - 1}{j}"))
                    for jj in range(2):
                        o = (2 * j + jj) * P
                        m = split_product(hbk[j][:, jj * 256:(jj + 1) * 256], [w[k % 2][:, :, o:o + P] for w in (w1H, w1L)],
                                          [x[:, :, bass.ds(e, 1), :].rearrange("p c e n -> p c (e n)") for x in xin2])
                    m.then_inc(pe_h.sem, 1)

            def result(r, k):
                pe.wait_ge(pool_w.sem, pool_w.done(r, f"w2{k}"))
                pe.wait_ge(dve_w.sem, dve_w.done(r, f"w2{k}"))
                pe.wait_ge(dve_h.sem, dve_h.done(r, f"h{k}{HC // 2 - 1}"))
                if k >= 2:
                    pe.wait_ge(dve_y.sem, dve_y.done(r, f"y{k - 2}{BT - 1}"))
                else:
                    if later(r):
                        pe.wait_ge(dve_y.sem, dve_y.whole(r))
                for half in range(2):
                    m = split_product(mbk[k % 2][:, half * D:(half + 1) * D],
                                      [h[:, :, half * P:(half + 1) * P] for h in (hH[:, k % 2], hL[k % 2])],
                                      [w[k % 2] for w in (w2H, w2L)])
                m.then_inc(pe_y.sem, 1)

            def experts(r):
                for k in range(EQ):
                    pe.wait_ge(pool_w.sem, pool_w.done(r, f"w1{k}"))
                    if k:
                        pe.wait_ge(dve_w.sem, dve_w.done(r, f"w1{k}"))
                    hidden(r, k, r * EQ + k)
                    if k:
                        result(r, k - 1)
                result(r, EQ - 1)

            with pe.Fori(0, E // EQ) as r:
                experts(r)

            for n, t in enumerate(LAST_ORDER):
                pe.wait_ge(dve_y.sem, dve_y.done(E // EQ - 1, f"y{EQ - 1}{t % BT}"))
                if n >= 4:
                    pe.wait_ge(dve_f.sem, dve_f.done(n - 4, "f"))
                for r in range(2):
                    m = mm(hbk[n % 4][:, 0:D], selT[:, t, r, :], ys[:, t, r, :], start=(r == 0), stop=(r == 1))
                m.then_inc(pe_f.sem, 1)

        @block.scalar
        def _(act):
            A = act.activation
            def keys(t, i):
                act.wait_ge(pe_k.sem, pe_k.done(t, f"k{i}"))
                c, (o, n) = i // 3, PIECES[i % 3]
                if i == 0 and later(t):
                    act.wait_ge(pe_s.sem, pe_s.whole(t))
                A(kT2[HI][:, c, o:o + n], ring_bank(dve_k, f"k{i}")[:, 0:n], ACT.Identity,
                  bias=cols[:, 1, c:c + 1]).then_inc(act_k.sem, 1)

            def values(t, b):
                act.wait_ge(pe_v.sem, pe_v.done(t, f"v{b}"))
                if b == 0 and later(t):
                    act.wait_ge(pe_o.sem, pe_o.whole(t))
                A(v[:, b].rearrange("p k n -> p (k n)"), ring_bank(act_v, f"v{b}")[:], ACT.Copy).then_inc(act_v.sem, 1)

            def context(t):
                act.wait_ge(s_ctx, (t + 1) * 16)
                if later(t):
                    act.wait_ge(pe_v.sem, pe_v.whole(t))
                for c in range(C):
                    A(ctx2[HI][:, c], ctxT[:, c], ACT.Copy).then_inc(act_c.sem, 1)

            def queries(t):
                if later(t):
                    act.wait_ge(pool_q.sem, pool_q.whole(t))
                A(qtH, qT[:, :, bass.ds(t * P, P)], ACT.Copy).then_inc(act_q.sem, 1)

            def exps(t, i):
                b, g, p = i // G, i % G, i // 2
                act.wait_ge(dve_max.sem, dve_max.done(t, f"m{i}"))
                if i % 2 == 0:
                    if p >= 2:
                        act.wait_ge(pe_t.sem, pe_t.done(t, f"t{p - 2}"))
                        act.wait_ge(pool_last.sem, pool_last.done(t, f"l{2 * p - 3}"))
                    else:
                        if later(t):
                            act.wait_ge(pe_t.sem, pe_t.whole(t))
                        if later(t):
                            act.wait_ge(pool_last.sem, pool_last.whole(t))
                if i == 0:
                    if later(t):
                        act.wait_ge(dve_r.sem, dve_r.whole(t))
                A(probs[:, p % 2, i % 2, :], sbk[i % 3][:, 0:KEYS], ACT.Exp, bias=nmax[:, i:i + 1],
                  accum_out=rsum[:, g, b:b + 1]).then_inc(act_exp.sem, 1)

            def turn(t, p):
                act.wait_ge(pe_t.sem, pe_t.done(t, f"t{p}"))
                if p >= 2:
                    act.wait_ge(pe_o.sem, pe_o.done(t, f"o{p - 2}"))
                else:
                    if later(t):
                        act.wait_ge(pe_o.sem, pe_o.whole(t))
                A(pT[:, p % 2].rearrange("p g n -> p (g n)"), ring_bank(act_t, f"t{p}")[:], ACT.Copy
                  ).then_inc(act_t.sem, 1)

            def first_queries(n):
                for c in range(C):
                    act.wait_ge(pro_q.sem, pro_q.done(0, f"q{n}{c}"))
                    A(qT[:, c, n * 512:(n + 1) * 512], sbk[c][:], ACT.Identity, bias=bqs[:, c:c + 1],
                      scale=0.25).then_inc(pro_qe.sem, 1)

            context(0)
            act.wait_ge(s_wk, 16)
            A(wkH, wk, ACT.Copy).then_inc(pro_wh.sem, 1)
            act.wait_ge(s_wv, 2 * 16)
            A(wvH, wv, ACT.Copy).then_inc(pro_wh.sem, 1)
            act.wait_ge(s_cols, 16)
            act.wait_ge(pro.sem, pro.done(0, "bqs"))
            first_queries(0)
            act.wait_ge(pro_qe.sem, pro_qe.done(0, "q01"))

            def self_v(u):
                act.wait_ge(pe_x.sem, pe_x.done(u, "v"))
                for b in range(BT):
                    A(vz[S * b:S * b + S, b, :], mbk[1][S * b:S * b + S, 0:D], ACT.Copy).then_inc(act_s.sem, 1)

            def self_qk(u):
                act.wait_ge(pe_x.sem, pe_x.done(u, "qkT"))
                A(qk2[:].rearrange("p k c n -> p (k c n)"), mbk[0][:], ACT.Copy).then_inc(act_s.sem, 1)

            def self_exp(u):
                act.wait_ge(dve_s.sem, dve_s.done(u, "sub"))
                A(ex[:], sc[:], ACT.Exp).then_inc(act_s.sem, 1)

            def body(t, u, w):
                if t is not None:
                    queries(t)
                    for i in range(6):
                        keys(t, i)
                    if not later(t):
                        first_queries(1)
                    values(t, 0)
                for p in range(9):
                    if t is not None:
                        if p < 8:
                            exps(t, 2 * p)
                            exps(t, 2 * p + 1)
                            if p % 2 == 0 and p // 2 + 1 < BT:
                                values(t, p // 2 + 1)
                        if p >= 1:
                            turn(t, p - 1)
                        if p == 5 and (not isinstance(t, int) or t < TILES - 1):
                            context(t + 1)
                    if u is not None and p == 1:
                        self_v(u)
                    if u is not None and p == 3:
                        self_qk(u)
                    if w is not None and p == 3:
                        act.wait_ge(dve_g.sem, dve_g.done(w, "max"))
                        A(gex[:], mbk[1][:, 0:E], ACT.Exp, bias=gmx[:, 0:1],
                          accum_out=gsm[:, 0:1]).then_inc(act_g.sem, 1)
                    if u is not None and p == 6:
                        self_exp(u)

            tiles(act, body)

            def weights(r, k, loaded, wh, w):
                act.wait_ge(loaded[k % 2], r * 32 + 16 * (k // 2 + 1))
                A(wh[k % 2], w[k % 2], ACT.Copy).then_inc(act_w.sem, 1)

            def experts(r):
                weights(r, 0, s_w1, w1H, w1s)
                weights(r, 1, s_w1, w1H, w1s)
                for k in range(EQ):
                    for j in range(HC // 2):
                        act.wait_ge(pe_h.sem, pe_h.done(r, f"h{k}{j}"))
                        if k:
                            act.wait_ge(dve_h.sem, dve_h.done(r, f"h{k - 1}{j}"))
                        for h, at in ((hf, 2 * j), (hH[:, k % 2], 2 * j)):
                            A(h[:, at:at + 2, :].rearrange("p j n -> p (j n)"), hbk[j][:], ACT.Gelu
                              ).then_inc(act_h.sem, 1)
                    if 2 <= k + 1 < EQ:
                        weights(r, k + 1, s_w1, w1H, w1s)
                    weights(r, k, s_w2, w2H, w2s)

            with act.Fori(0, E // EQ) as r:
                experts(r)

        @block.gpsimd
        def _(pool):
            pool.wait_ge(pro.sem, pro.done(0, "eps"))
            for n in range(2):
                half = slice(n * TILES // 2, (n + 1) * TILES // 2)
                pool.wait_ge(pro_ln.sem, pro_ln.done(0, f"mv{n}"))
                pool.tensor_tensor(ve1[:, half], mv1[:, half, 1], eps[:, half], ALU.add).then_inc(pro_pool.sem, 1)
                pool.wait_ge(pro_pool.sem, pro_pool.done(0, f"var{n}"))
                pool.tensor_tensor(rstd1[:, half], ve1[:, half], mhalf[:, half], ALU.pow).then_inc(pro_pool.sem, 1)
            pool.wait_ge(s_const, 16)

            def context(t, c):
                pool.wait_ge(act_c.sem, act_c.done(t, f"hi{c}"))
                pool.tensor_tensor(ctx2[LO][:, c], ctxT[:, c], f32(ctxH[:, c]), ALU.subtract).then_inc(pool_c.sem, 1)

            for c in range(C):
                context(0, c)

            def block_diagonal(dst, src, sig):
                pool.tensor_tensor(dst.rearrange("p b (h q) -> p b h q", h=8),
                                   over(src.rearrange("p (b q) -> p b q", b=BT), 8, 2),
                                   over(over(k_("headmask"), BT, 1), S, 3), ALU.mult).then_inc(sig.sem, 1)

            def queries(t):
                if later(t):
                    pool.wait_ge(pe_s.sem, pe_s.whole(t))
                pool.wait_ge(act_q.sem, act_q.done(t, "hi"))
                for c in range(C):
                    block_diagonal(qblkH[:, c], f32(qtH[:, c]), pool_q)
                pool.tensor_tensor(qtL, qT[:, :, bass.ds(t * P, P)], f32(qtH), ALU.subtract).then_inc(pool_q.sem, 1)
                for c in range(C):
                    pool.wait_ge(pool_q.sem, pool_q.done(t, "lo"))
                    block_diagonal(qblkL[:, c], qtL[:, c], pool_q)

            def last(t, i):
                b, g, p = i // G, i % G, i // 2
                pool.wait_ge(act_exp.sem, act_exp.done(t, f"e{i}"))
                if i == 0:
                    if later(t):
                        pool.wait_ge(pe_e.sem, pe_e.whole(t))
                pool.tensor_tensor(rep_p[:, g, b * S:(b + 1) * S], k_("rep"),
                                   probs[:, p % 2, i % 2, KEYS - 1:KEYS].broadcast_to([P, S]), ALU.mult
                                   ).then_inc(pool_last.sem, 1)

            def before(w):
                pool.wait_ge(dve_g.sem, dve_g.done(w, "gt"))
                pool.tensor_tensor(cgt[:], cgt[:], over(k_("after"), E, 1), ALU.mult).then_inc(pool_g.sem, 1)
                pool.wait_ge(dve_g.sem, dve_g.done(w, "ge"))
                pool.tensor_tensor(cge[:], cge[:], over(k_("before"), E, 1), ALU.mult).then_inc(pool_g.sem, 1)
                pool.wait_ge(pool_g.sem, pool_g.done(w, "ge_m"))
                pool.tensor_tensor(cgt[:], cgt[:], cge[:], ALU.add).then_inc(pool_g.sem, 1)

            def repeat(t):
                pool.wait_ge(dve_r.sem, dve_r.done(t, "rinv"))
                pool.tensor_tensor(rep_r[:].rearrange("p g (b q) -> p (g b) q", b=BT), over(k_("rep"), G * BT, 1),
                                   over(rinv[:].rearrange("p g b -> p (g b)"), S, 2), ALU.mult
                                   ).then_inc(pool_e.sem, 1)

            def body(t, u, w):
                if u is not None:
                    repeat(u)
                if t is not None:
                    queries(t)
                if w is not None:
                    pool.wait_ge(dve_g.sem, dve_g.done(w, "aggr"))
                    pool.tensor_tensor(ve[:, 1:2], mv[:, 1, 1:2], eps[:, 0:1], ALU.add).then_inc(pool_g.sem, 1)
                    pool.wait_ge(pool_g.sem, pool_g.done(w, "var"))
                    pool.tensor_tensor(rstd[:, 1:2], ve[:, 1:2], mhalf[:, 0:1], ALU.pow).then_inc(pool_g.sem, 1)
                if u is not None:
                    pool.wait_ge(dve_a.sem, dve_a.done(u, "x1"))
                    pool.tensor_tensor(x1b[:], x1[:], bo_b[:, 1, :], ALU.add).then_inc(pool_s.sem, 1)
                    pool.wait_ge(dve_s.sem, dve_s.done(u, "aggr"))
                    pool.tensor_tensor(ve[:, 0:1], mv[:, 0, 1:2], eps[:, 0:1], ALU.add).then_inc(pool_s.sem, 1)
                    pool.wait_ge(pool_s.sem, pool_s.done(u, "var"))
                    pool.tensor_tensor(rstd[:, 0:1], ve[:, 0:1], mhalf[:, 0:1], ALU.pow).then_inc(pool_s.sem, 1)
                for p in range(8):
                    if t is not None:
                        last(t, 2 * p)
                        last(t, 2 * p + 1)
                        if not isinstance(t, int) or t < TILES - 1:
                            if p in (5, 6):
                                context(t + 1, p - 5)
                    if w is not None and p == 4:
                        before(w)
                    if u is not None and p == 3:
                        pool.wait_ge(act_s.sem, act_s.done(u, "qk"))
                        block_diagonal(kblk[:, 0], qk2[:, 1, 0, :], pool_s)

            tiles(pool, body)

            def weights(r, k, step, wl, w, wh, part):
                pool.wait_ge(act_w.sem, act_w.done(r, step))
                pool.tensor_tensor(wl[k % 2][:, part], w[k % 2][:, part], f32(wh[k % 2][:, part]), ALU.subtract
                                   ).then_inc(pool_w.sem, 1)

            with pool.Fori(0, E // EQ) as r:
                weights(r, 0, "w10", w1L, w1s, w1H, slice(0, C))
                weights(r, 1, "w11", w1L, w1s, w1H, slice(1, C))
                for k in range(EQ):
                    if 2 <= k + 1 < EQ:
                        weights(r, k + 1, f"w1{k + 1}", w1L, w1s, w1H, slice(1, C))
                    weights(r, k, f"w2{k}", w2L, w2s, w2H, slice(HC // 2, HC))

        @block.vector
        def _(dve):
            TT, TS, RED = dve.tensor_tensor, dve.tensor_scalar, dve.tensor_reduce
            dve.memset(mhalf[:], -0.5).then_inc(pro.sem, 1)
            dve.memset(eps[:], EPS).then_inc(pro.sem, 1)
            dve.memset(mrow[:], 0.0).then_inc(pro.sem, 1)
            dve.memset(row0[:], 0.0).then_inc(pro.sem, 1)
            dve.wait_ge(pro.sem, pro.done(0, "row0"))
            dve.memset(row0[0:1, :], 1.0).then_inc(pro.sem, 1)
            dve.memset(vz[:], 0.0).then_inc(pro.sem, 1)
            dve.wait_ge(s_mask, 16)
            TS(mask_f[:], mask_i[:], 0.0, -3e38, ALU.is_equal, ALU.mult).then_inc(pro.sem, 1)
            dve.wait_ge(pro.sem, pro.done(0, "mask0"))
            TS(mask_b[:], mask_f[:], 4.0, None, ALU.mult).then_inc(pro.sem, 1)

            def first_stats(n):
                half = range(n * TILES // 2, (n + 1) * TILES // 2)
                dve.wait_ge(s_x[n], 16)
                for t in half:
                    i = dve.bn_stats(st1[:, t, :], x_all[:, t, :])
                i.then_inc(pro_ln.sem, 1)
                dve.wait_ge(pro_ln.sem, pro_ln.done(0, f"st{n}"))
                for t in half:
                    i = dve.bn_aggr(mv1[:, t, :], st1[:, t, :])
                i.then_inc(pro_ln.sem, 1)

            def first_norm(t):
                if t >= 2:
                    dve.wait_ge(pro_t.sem, pro_t.done(t - 2, "t"))
                TS(xn1[:, t % 2, :], x_all[:, t, :], mv1[:, t, 0:1], rstd1[:, t:t + 1], ALU.subtract, ALU.mult
                   ).then_inc(pro_xn.sem, 1)

            def first_xT(t):
                dve.wait_ge(pro_t.sem, pro_t.done(t, "t"))
                dve.tensor_copy(xT1[:, :, t * P:(t + 1) * P],
                                mbk[t % 2][:, 0:D].rearrange("p (c n) -> p c n", c=C)).then_inc(pro_xT.sem, 1)

            first_stats(0)
            dve.wait_ge(s_const, 16)
            for pad in (kTH[:, :, KB:], kTL[:, :, KB:]):
                TS(pad, k_("headmask").rearrange("p (c n) -> p c n", c=C), 0.0, None, ALU.mult).then_inc(pro.sem, 1)
            dve.wait_ge(s_cols, 16)
            TS(bqs[:], cols[:, 0, :], 0.25, None, ALU.mult).then_inc(pro.sem, 1)
            dve.wait_ge(pro_ln.sem, pro_ln.done(0, "mv0"))
            dve.wait_ge(pro_pool.sem, pro_pool.done(0, "rstd0"))
            for t in range(TILES // 2):
                first_norm(t)
                if t:
                    first_xT(t - 1)
            first_xT(TILES // 2 - 1)
            first_stats(1)
            dve.wait_ge(pro_wh.sem, pro_wh.done(0, "k"))
            TT(wkL, wk, f32(wkH), ALU.subtract).then_inc(pro_wl.sem, 1)
            dve.wait_ge(pro_ln.sem, pro_ln.done(0, "mv1"))
            dve.wait_ge(pro_pool.sem, pro_pool.done(0, "rstd1"))
            for t in range(TILES // 2, TILES // 2 + 2):
                first_norm(t)

            def second_half():
                dve.wait_ge(pro_vl, 1)
                dve.tensor_copy(vlast[:].rearrange("p t c b -> p c t b"),
                                obk[:, 0:C * B].rearrange("p (c t b) -> p c t b", c=C, b=BT)).then_inc(pro_vle, 1)
                dve.wait_ge(pro_wh.sem, pro_wh.done(0, "v"))
                TT(wvL, wv, f32(wvH), ALU.subtract).then_inc(pro_wl.sem, 1)
                dve.wait_ge(pro_xn.sem, pro_xn.done(TILES - 1, "xn"))
                dve.wait_ge(s_w, 16 * N_W)
                TT(x_all[:], x_all[:], over(bo_b[:, 0, :], TILES, 1), ALU.add).then_inc(pro_xbo, 1)
                dve.wait_ge(pro_xbo, 1)
                dve.wait_ge(pro_vle, 1)

            diag = over(k_("diag"), 4, 1)

            def keys(t, i):
                dve.wait_ge(act_k.sem, act_k.done(t, f"k{i}"))
                if i == 0 and later(t):
                    dve.wait_ge(pe_s.sem, pe_s.whole(t))
                c, (o, n) = i // 3, PIECES[i % 3]
                dve.scalar_tensor_tensor(kT2[LO][:, c, o:o + n], ring_bank(dve_k, f"k{i}")[:, 0:n],
                                         cols[:, 1, c:c + 1], f32(kTH[:, c, o:o + n]), ALU.add, ALU.subtract
                                         ).then_inc(dve_k.sem, 1)
                if not later(t) and 1 <= i <= TILES // 2:
                    first_xT(TILES // 2 + i - 1)
                    if i + 1 < TILES // 2:
                        first_norm(TILES // 2 + i + 1)

            def maxima(t, i):
                dve.wait_ge(pe_s.sem, pe_s.done(t, f"s{i}"))
                RED(nmax[:, i:i + 1], sbk[i % 3][:, 0:KEYS], X, ALU.max, negate=True).then_inc(dve_max.sem, 1)

            def heads(t, half):
                if half:
                    dve.wait_ge(dve_o.sem, dve_o.done(t, "sum0"))
                else:
                    if later(t):
                        dve.wait_ge(dve_a.sem, dve_a.whole(t))
                dve.wait_ge(pe_o.sem, pe_o.done(t, f"o{4 * half + 3}"))
                TT(masked[:].rearrange("p (m n) -> p m n", m=4), obk[:].rearrange("p (m n) -> p m n", m=4), diag,
                   ALU.mult).then_inc(dve_o.sem, 1)

            def heads_sum(t, half):
                dve.wait_ge(dve_o.sem, dve_o.done(t, f"mask{half}"))
                RED(att_u[:, half].rearrange("p c (b q) -> p (c b) q", b=2),
                    masked[:].rearrange("p (m h q) -> p m q h", m=4, h=HG), X, ALU.add).then_inc(dve_o.sem, 1)

            def cross_att(t):
                n = 2 * P
                m8 = masked[:, 0:n].rearrange("p (cb q) -> p cb q", q=S)
                dve.wait_ge(dve_o.sem, dve_o.done(t, "sum1"))
                dve.wait_ge(pe_e.sem, pe_e.done(t, "expanded"))
                TT(m8, obk[:, n:2 * n].rearrange("p (cb q) -> p cb q", q=S),
                   over(vlast[:, t].rearrange("p c b -> p (c b)") if isinstance(t, int) else
                        vlast[:, bass.ds(t, 1)].rearrange("p t c b -> p (t c b)"), S, 2), ALU.mult).then_inc(dve_a.sem, 1)
                dve.wait_ge(dve_a.sem, dve_a.done(t, "last"))
                m4 = masked[:, 0:n].rearrange("p (c h n) -> p c h n", c=C, h=2)
                TT(m4, m4, att_u[:].rearrange("p h c n -> p c h n"), ALU.add).then_inc(dve_a.sem, 1)
                dve.wait_ge(dve_a.sem, dve_a.done(t, "plus"))
                TT(masked[:, 0:n], obk[:, 0:n], masked[:, 0:n], ALU.mult).then_inc(dve_a.sem, 1)
                dve.wait_ge(dve_a.sem, dve_a.done(t, "norm"))
                TT(att[:], masked[:, 0:n].rearrange("p (c n) -> p c n", c=C), over(cols[:, 2, :], P, 2), ALU.add
                   ).then_inc(dve_a.sem, 1)

            def cross_x1(t):
                dve.wait_ge(pe_e.sem, pe_e.done(t, "projected"))
                TT(x1[:], obk[:, 0:D], x_all[:, t, :] if isinstance(t, int) else
                   x_all[:, bass.ds(t, 1), :].rearrange("p t n -> p (t n)"), ALU.add).then_inc(dve_a.sem, 1)

            def norm(sig, t, src, made, at, dst, k, pool_sig):
                dve.wait_ge(made, at)
                dve.bn_stats(st[:, k, :], src).then_inc(sig.sem, 1)
                dve.wait_ge(sig.sem, sig.done(t, "stats"))
                dve.memset(hold[:], 0.0)
                dve.bn_aggr(mv[:, k, :], st[:, k, :]).then_inc(sig.sem, 1)
                dve.wait_ge(pool_sig.sem, pool_sig.done(t, "rstd"))
                dve.wait_ge(sig.sem, sig.done(t, "aggr"))
                TS(dst, src, mv[:, k, 0:1], rstd[:, k:k + 1], ALU.subtract, ALU.mult).then_inc(sig.sem, 1)

            def self_xT(u):
                dve.wait_ge(pe_x.sem, pe_x.done(u, "xT"))
                dve.tensor_copy(xT2[:].rearrange("p c n -> p (c n)"), mbk[1][:, 0:D]).then_inc(dve_s.sem, 1)

            def self_rope(u):
                dve.wait_ge(pe_x.sem, pe_x.done(u, "qk"))
                heads2 = 2 * H
                m = mbk[0][:].rearrange("p (n d) -> p n d", d=DK)
                TT(rot_a[:].rearrange("p (n d) -> p n d", d=DK), m, over(k_("cos"), heads2, 1), ALU.mult
                   ).then_inc(dve_s.sem, 1)
                m2, r2 = (y[:].rearrange("p (n d two) -> p two n d", two=2, d=DK // 2) for y in (mbk[0], rot_b))
                sin2 = k_("sin").rearrange("p (d two) -> p two d", two=2)
                for z in range(2):
                    TT(r2[:, z], m2[:, 1 - z], over(sin2[:, z], heads2, 1), ALU.mult).then_inc(dve_s.sem, 1)
                dve.wait_ge(dve_s.sem, dve_s.done(u, "sin1"))
                TT(rot_a[:], rot_a[:], rot_b[:], ALU.add).then_inc(dve_s.sem, 1)

            def self_keys(u):
                dve.wait_ge(act_s.sem, act_s.done(u, "qk"))
                TT(kblk[:, 1].rearrange("p b (h q) -> p b h q", h=8),
                   over(qk2[:, 1, 1, :].rearrange("p (b q) -> p b q", b=BT), 8, 2),
                   over(over(k_("headmask"), BT, 1), S, 3), ALU.mult).then_inc(dve_s.sem, 1)

            def self_softmax_a(u):
                dve.wait_ge(pe_x.sem, pe_x.done(u, "scores"))
                dve.scalar_tensor_tensor(sc[:], mbk[0][:].rearrange("p (h k) -> p h k", h=H), 1.0 / DK,
                                         over(k_("causal"), H, 1), ALU.mult, ALU.add).then_inc(dve_s.sem, 1)
                dve.wait_ge(dve_s.sem, dve_s.done(u, "scaled"))
                RED(mx2[:], sc[:], X, ALU.max).then_inc(dve_s.sem, 1)

            def self_less_max(u):
                dve.wait_ge(dve_s.sem, dve_s.done(u, "max"))
                TT(sc[:], sc[:], over(mx2[:], S, 2), ALU.subtract).then_inc(dve_s.sem, 1)

            def self_softmax_b(u):
                dve.wait_ge(act_s.sem, act_s.done(u, "exp"))
                RED(sm2[:], ex[:], X, ALU.add).then_inc(dve_s.sem, 1)
                dve.wait_ge(dve_s.sem, dve_s.done(u, "sum"))
                dve.reciprocal(ri2[:], sm2[:]).then_inc(dve_s.sem, 1)
                dve.wait_ge(dve_s.sem, dve_s.done(u, "rinv"))
                TT(pn[:].rearrange("p (h k) -> p h k", h=H), ex[:], over(ri2[:], S, 2), ALU.mult
                   ).then_inc(dve_s.sem, 1)
                dve.wait_ge(dve_s.sem, dve_s.done(u, "probs"))
                dve.transpose(pT2[:], pn[:]).then_inc(dve_s.sem, 1)

            def self_heads(u, banks):
                dve.wait_ge(pe_x.sem, pe_x.done(u, "pv"))
                for c in range(C):
                    TT(masked2[:, c].rearrange("p (b n) -> p b n", b=BT), banks[c][:].rearrange("p (b n) -> p b n", b=BT),
                       diag, ALU.mult).then_inc(dve_s.sem, 1)

            def self_heads_sum(u):
                for c in range(C):
                    dve.wait_ge(dve_s.sem, dve_s.done(u, f"mask{c}"))
                    RED(att2[:, c].rearrange("p (b q) -> p b q", b=BT),
                        masked2[:, c].rearrange("p (b h q) -> p b q h", b=BT, h=HG), X, ALU.add).then_inc(dve_s.sem, 1)

            def self_end(u, banks):
                dve.wait_ge(pe_x.sem, pe_x.done(u, "projected"))
                dve.wait_ge(pool_s.sem, pool_s.done(u, "x1b"))
                TT(x2[:], banks[2][:, 0:D], x1b[:], ALU.add).then_inc(dve_s.sem, 1)
                dve.wait_ge(dve_s.sem, dve_s.done(u, "x2"))
                TS(x_all[:, bass.ds(u, 1), :].rearrange("p t n -> p (t n)"), x2[:], 1.0, None, ALU.mult).then_inc(dve_s.sem, 1)

            def route_max(w):
                dve.wait_ge(pe_g.sem, pe_g.done(w, "logits"))
                RED(gmx[:], mbk[1][:, 0:E], X, ALU.max, negate=True).then_inc(dve_g.sem, 1)

            def route_p(w):
                dve.wait_ge(act_g.sem, act_g.done(w, "exp"))
                dve.reciprocal(gri[:], gsm[:]).then_inc(dve_g.sem, 1)
                dve.wait_ge(dve_g.sem, dve_g.done(w, "rinv"))
                TS(gp[:], gex[:], gri[:, 0:1], None, ALU.mult).then_inc(dve_g.sem, 1)
                dve.wait_ge(dve_g.sem, dve_g.done(w, "p"))
                TT(dsp[:], over(gp[:], S, 2), over(k_("rep"), E, 1), ALU.mult).then_inc(dve_g.sem, 1)

            def route_rank(w):
                dve.wait_ge(pe_g.sem, pe_g.done(w, "others"))
                m = mbk[1][:, 0:E * S].rearrange("p (e s) -> p e s", e=E)
                TT(cgt[:], m, over(gp[:], S, 2), ALU.is_gt).then_inc(dve_g.sem, 1)
                TT(cge[:], m, over(gp[:], S, 2), ALU.is_ge).then_inc(dve_g.sem, 1)

            def route_sel(w):
                dve.wait_ge(pool_g.sem, pool_g.done(w, "both"))
                RED(rank[:], cgt[:], X, ALU.add).then_inc(dve_g.sem, 1)
                dve.wait_ge(dve_g.sem, dve_g.done(w, "rank"))
                TT(sel[:], over(rank[:], BT * CAP, 2), over(k_("code"), E, 1), ALU.is_equal).then_inc(dve_g.sem, 1)
                dve.wait_ge(dve_g.sem, dve_g.done(w, "sel"))
                TT(selw[:], sel[:], over(gp[:], BT * CAP, 2), ALU.mult).then_inc(dve_g.sem, 1)

            def route_keep(w):
                n = BT * CAP
                xh, xl = (x[:, :, :, bass.ds(w * n, n)].rearrange("p c e n -> p (c e) n") for x in xin2)
                x = mbk[1][:].rearrange("p (ce s) -> p ce s", s=n)
                dve.wait_ge(pe_g.sem, pe_g.done(w, f"xin{C - 1}"))
                dve.tensor_copy(xh, x).then_inc(dve_g.sem, 1)
                dve.wait_ge(dve_g.sem, dve_g.done(w, "xinH"))
                TT(xl, x, f32(xh), ALU.subtract).then_inc(dve_g.sem, 1)
                dve.wait_ge(pe_g.sem, pe_g.done(w, "selT"))
                dve.tensor_copy(selT[:, bass.ds(w, 1)].rearrange("p t k n -> p (t k n)"), mbk[0][:, 0:2 * P]
                                ).then_inc(dve_g.sem, 1)

            def body(t, u, w):
                if u is not None:
                    heads(u, 1)
                if t is not None:
                    keys(t, 0)
                if u is not None:
                    heads_sum(u, 1)
                if w is not None:
                    self_heads(w, output_banks(u))
                if t is not None:
                    keys(t, 1)
                if w is not None:
                    self_heads_sum(w)
                    if u is None:
                        route_keep(w - 1)
                if t is not None:
                    keys(t, 2)
                if u is not None:
                    cross_att(u)
                if t is not None:
                    keys(t, 3)
                if w is not None:
                    self_end(w, output_banks(u))
                if t is not None:
                    keys(t, 4)
                if w is not None:
                    norm(dve_g, w, x2[:], dve_s.sem, dve_s.done(w, "x2"), xn3[:], 1, pool_g)
                if t is not None:
                    keys(t, 5)
                    if not later(t):
                        second_half()
                if u is not None:
                    cross_x1(u)
                    norm(dve_s, u, x1[:], dve_a.sem, dve_a.done(u, "x1"), xn[:], 0, pool_s)
                for p in range(9):
                    if t is not None and p < 8:
                        maxima(t, 2 * p)
                        maxima(t, 2 * p + 1)
                    if w is not None and p == 0:
                        dve.wait_ge(pe_g.sem, pe_g.done(w, "xT"))
                        dve.tensor_copy(xT3[:].rearrange("p c n -> p (c n)"), mbk[0][:, 0:D]).then_inc(dve_g.sem, 1)
                    if u is not None and p == 0:
                        self_xT(u)
                    if u is not None and p == 2:
                        self_rope(u)
                    if w is not None and p == 2:
                        route_max(w)
                    if w is not None and p == 3:
                        route_p(w)
                    if u is not None and p == 4:
                        self_keys(u)
                    if w is not None and p == 4:
                        route_rank(w)
                    if u is not None and p == 5:
                        self_softmax_a(u)
                    if t is not None and p == 5:
                        heads(t, 0)
                    if u is not None and p == 6:
                        self_less_max(u)
                    if w is not None and p == 6:
                        route_sel(w)
                    if t is not None and p == 6:
                        heads_sum(t, 0)
                    if w is not None and p == 7 and (t is not None or u is None):
                        route_keep(w)
                    if u is not None and p == 7:
                        self_softmax_b(u)
                    if t is not None and p == 8:
                        dve.wait_ge(act_exp.sem, act_exp.done(t, f"e{H - 1}"))
                        dve.reciprocal(rinv[:], rsum[:]).then_inc(dve_r.sem, 1)

            tiles(dve, body)

            dve.memset(hold[:], 0.0).then_inc(dve_y.sem, dve_y.base)

            def weights1(r, k):
                dve.wait_ge(act_w.sem, act_w.done(r, f"w1{k}"))
                TT(w1L[k % 2][:, 0], w1s[k % 2][:, 0], f32(w1H[k % 2][:, 0]), ALU.subtract).then_inc(dve_w.sem, 1)

            def weights2(r, k):
                dve.wait_ge(act_w.sem, act_w.done(r, f"w2{k}"))
                lo = slice(0, HC // 2)
                TT(w2L[k % 2][:, lo], w2s[k % 2][:, lo], f32(w2H[k % 2][:, lo]), ALU.subtract).then_inc(dve_w.sem, 1)

            def results(r, k):
                dve.wait_ge(pe_y.sem, pe_y.done(r, f"y{k}"))
                for q in range(BT):
                    src = mbk[k % 2][S * q:S * q + S, :].rearrange("p (h n) -> p h n", h=2)
                    dst = ys[S * k:S * k + S, q::BT, bass.ds(r, 1), :].rearrange("p h r n -> p h (r n)")
                    dve.tensor_copy(dst, src).then_inc(dve_y.sem, 1)

            def experts(r):
                weights1(r, 1)
                for k in range(EQ):
                    for j in range(HC // 2):
                        dve.wait_ge(act_h.sem, act_h.done(r, f"h{k}{j}"))
                        at = slice(2 * j, 2 * j + 2)
                        TT(hL[k % 2][:, at], hf[:, at], f32(hH[:, k % 2, at]), ALU.subtract).then_inc(dve_h.sem, 1)
                    if 2 <= k + 1 < EQ:
                        weights1(r, k + 1)
                    weights2(r, k)
                    if k:
                        results(r, k - 1)
                results(r, EQ - 1)

            with dve.Fori(0, E // EQ) as r:
                experts(r)
            for n, t in enumerate(LAST_ORDER):
                dve.wait_ge(pe_f.sem, pe_f.done(n, "f"))
                TT(fin[:, t, :], hbk[n % 4][:, 0:D], x_all[:, t, :], ALU.add).then_inc(dve_f.sem, 1)


def kernel(**inputs):
    import concourse.bacc as bacc
    from concourse.bass_utils import run_bass_kernel_spmd as run

    i = {k: np.asarray(v) for k, v in inputs.items()}
    ctx = i["ctx_1024"]
    T = lambda n: np.ascontiguousarray(i[n].T)
    ctx_t = ctx.reshape(TILES, BT * KEYS, D)
    arrays = {
        "consts": tables(),
        "mask": np.ascontiguousarray(i["mask_Bx1x1xS2_if1"].reshape(B, KEYS)),
        "x": np.ascontiguousarray(i["x"].reshape(B * S, D)),
        "wq": T("L0_xattn_Wq"), "wk": T("L0_xattn_Wk"), "wv": T("L0_xattn_Wv"), "wo": T("L0_xattn_Wo"),
        "wqkv": np.ascontiguousarray(np.concatenate([i["L0_attn_Wq"], i["L0_attn_Wk"], i["L0_attn_Wv"]], axis=0).T),
        "wo2": T("L0_attn_Wo"),
        "gate": np.ascontiguousarray(i["L0_ffn_gate_w"]),
        "ctx_last": np.ascontiguousarray(ctx[:, KEYS - 1, :].T),
        "cols": np.ascontiguousarray(np.concatenate(
            [i[n].reshape(C, P).T for n in ("L0_xattn_bq", "L0_xattn_bk", "L0_xattn_bv")], axis=1)),
        "bo": np.ascontiguousarray(np.stack([i["L0_xattn_bo"], i["L0_attn_bo"]])),
        "ctxT": np.ascontiguousarray(ctx_t.transpose(0, 2, 1)),
        "w1": np.ascontiguousarray(i["L0_ffn_w1"]),
        "w2": np.ascontiguousarray(i["L0_ffn_w2"]),
    }
    nc = bacc.Bacc("TRN2", target_bir_lowering=False, num_devices=1)
    a = {n: nc.dram_tensor(f"in_{n}", v.shape, mybir.dt.from_np(v.dtype), kind="ExternalInput").ap()
         for n, v in arrays.items()}
    a["mask_terms"] = nc.dram_tensor("mask_terms", [B, KEYS], BF16, kind="Internal").ap()
    out = nc.dram_tensor("out", [B * S, D], F32, kind="ExternalOutput").ap()
    perceiver(nc, a, out)
    r = run(nc, [{f"in_{n}": v for n, v in arrays.items()}], core_ids=[0])
    return r.results[0]["out"].reshape(B, S, D)
```
